# Optimizing a Trainium2 kernel written in Bass

```python
import numpy as np
import jax
import jax.numpy as jnp

def _softmax(x, axis=-1):
    return jax.nn.softmax(x, axis=axis)

def _gelu(x):
    return jax.nn.gelu(x, approximate=True)

def _silu(x):
    return jax.nn.silu(x)

def _sigmoid(x):
    return jax.nn.sigmoid(x)

def _layernorm(x, axis=-1, eps=1e-05):
    m = jnp.mean(x, axis=axis, keepdims=True)
    v = jnp.var(x, axis=axis, keepdims=True)
    return (x - m) / jnp.sqrt(v + eps)

def _scatter_add(tgt, idx, src, axis=0):
    return tgt.at[idx].add(src)

def _segment_sum(src, seg, n):
    return jax.ops.segment_sum(src, seg, n)
kernel_name = 'mk_xattn_ffn_d1_seqx_r2_2a6144'

def setup_inputs(seed: int=0):
    np.random.seed(seed)
    _w = jnp.asarray

    def _rec_inputs():
        import jax
        import jax.numpy as jnp
        _rk = jax.random.key(seed)
        x = 0.0002417 + 0.9998 * jax.random.normal(jax.random.fold_in(_rk, 1), (1, 4096, 512), jnp.float32)
        _lenS = 4096 - jax.random.randint(jax.random.fold_in(_rk, 7), (1,), 0, max(1, 4096 // 4) + 1, jnp.int32)
        _lenS2 = 3202 - jax.random.randint(jax.random.fold_in(_rk, 8), (1,), 0, max(1, 3202 // 4) + 1, jnp.int32)
        _ctx_1024P = jax.random.normal(jax.random.fold_in(_rk, 11), (1, 16, 512), jnp.float32)
        _ctx_1024c = jax.random.dirichlet(jax.random.fold_in(_rk, 511), 0.3 * jnp.ones((16,), jnp.float32), (1, 3202))
        _ctx_1024t = jnp.einsum('bsk,bkd->bsd', _ctx_1024c, _ctx_1024P)
        _ctx_1024t = _ctx_1024t * jax.lax.rsqrt(jnp.mean(jnp.square(_ctx_1024t)) + 1e-12) * 0.953939
        ctx_1024 = 7.22013e-05 + 1.00017 * (_ctx_1024t + 0.3 * jax.random.normal(jax.random.fold_in(_rk, 611), (1, 3202, 512), jnp.float32))
        return (x, ctx_1024)
    x, ctx_1024 = _rec_inputs()

    def _L0_xattn_setup():
        import jax, jax.numpy as jnp
        import numpy as np
        D_MODEL = 512
        B, S = (4, 1024)
        key = jax.random.key(seed)
        ks = jax.random.split(key, 10)
        s = 1.0 / np.sqrt(D_MODEL)
        return {'k': jax.random.normal(ks[0], (B, S, D_MODEL), jnp.float32), 'v': jax.random.normal(ks[1], (B, S, D_MODEL), jnp.float32), 'q': jax.random.normal(ks[2], (B, S, D_MODEL), jnp.float32), 'Wk': jax.random.normal(ks[3], (D_MODEL, D_MODEL), jnp.float32) * s, 'Wv': jax.random.normal(ks[4], (D_MODEL, D_MODEL), jnp.float32) * s, 'bv': jnp.zeros((D_MODEL,), jnp.float32), 'Wq': jax.random.normal(ks[5], (D_MODEL, D_MODEL), jnp.float32) * s, 'bq': jnp.zeros((D_MODEL,), jnp.float32), 'Wo': jax.random.normal(ks[6], (D_MODEL, D_MODEL), jnp.float32) * s, 'bo': jnp.zeros((D_MODEL,), jnp.float32)}
    _L0_xattn_all = _L0_xattn_setup()
    _L0_xattn_in = {k: v for k, v in _L0_xattn_all.items() if k in ('Wk', 'Wv', 'bv', 'Wq', 'bq', 'Wo', 'bo')}
    del _L0_xattn_all

    def _L0_ffn_setup():
        import jax, jax.numpy as jnp
        import numpy as np
        E = 16
        K = 2
        LOAD = 1.0

        def _dispatch(xb, pb, cap):
            T, C = xb.shape
            top_k_probs, ei = jax.lax.top_k(pb, K)
            flat = ei.swapaxes(0, 1).ravel()
            one_hot = jax.nn.one_hot(flat, E, dtype=jnp.int32)
            pos = jnp.cumsum(one_hot, axis=0) * one_hot
            pos = pos.reshape(K, T, E).swapaxes(0, 1)
            pos = jnp.max(pos, axis=-1) - 1
            ei2 = flat.reshape(K, T).swapaxes(0, 1)
            xr = jnp.repeat(xb, K, axis=0)
            buf = jnp.zeros((E, cap, C), xb.dtype)
            buf = buf.at[ei2.ravel(), pos.ravel()].set(xr, mode='drop')
            return (top_k_probs, pos, ei2, buf)

        def _collect(eo_b, ei_b, pos_b, tk_b):
            out = eo_b[ei_b, pos_b]
            return jnp.sum(tk_b[..., None] * out, axis=1)
        key = jax.random.key(seed)
        k1, k2, k3, k4, k5 = jax.random.split(key, 5)
        B, T, C, H = (8, 2048, 512, 256)
        n_layer = 12
        x = jax.random.normal(k1, (B, T, C), dtype=jnp.float32)
        w_router = jax.random.normal(k2, (C, E), dtype=jnp.float32) * 0.02
        w_fc = jax.random.normal(k3, (E, C, H), dtype=jnp.float32) * 0.02
        w_gate = jax.random.normal(k4, (E, C, H), dtype=jnp.float32) * 0.02
        w_proj = jax.random.normal(k5, (E, H, C), dtype=jnp.float32) * (0.02 * (2 * n_layer) ** (-0.5))
        return {'x': x, 'w_router': w_router, 'w_fc': w_fc, 'w_gate': w_gate, 'w_proj': w_proj}
    _L0_ffn_all = _L0_ffn_setup()
    _L0_ffn_in = {k: v for k, v in _L0_ffn_all.items() if k in ('w_router', 'w_fc', 'w_gate', 'w_proj')}
    del _L0_ffn_all
    return {'x': x, 'ctx_1024': ctx_1024, 'L0_xattn_Wk': _L0_xattn_in['Wk'], 'L0_xattn_Wv': _L0_xattn_in['Wv'], 'L0_xattn_bv': _L0_xattn_in['bv'], 'L0_xattn_Wq': _L0_xattn_in['Wq'], 'L0_xattn_bq': _L0_xattn_in['bq'], 'L0_xattn_Wo': _L0_xattn_in['Wo'], 'L0_xattn_bo': _L0_xattn_in['bo'], 'L0_ffn_w_router': _L0_ffn_in['w_router'], 'L0_ffn_w_fc': _L0_ffn_in['w_fc'], 'L0_ffn_w_gate': _L0_ffn_in['w_gate'], 'L0_ffn_w_proj': _L0_ffn_in['w_proj']}

def reference(x, ctx_1024, L0_xattn_Wk, L0_xattn_Wv, L0_xattn_bv, L0_xattn_Wq, L0_xattn_bq, L0_xattn_Wo, L0_xattn_bo, L0_ffn_w_router, L0_ffn_w_fc, L0_ffn_w_gate, L0_ffn_w_proj):
    import jax
    import jax.numpy as jnp

    def _L0_xattn_ref(k, v, q, Wk, Wv, bv, Wq, bq, Wo, bo):
        import jax, jax.numpy as jnp
        import numpy as np
        D_MODEL = 512
        B, S = (4, 1024)
        kp = jnp.einsum('bsd,ed->bse', k, Wk)
        vp = jnp.einsum('bsd,ed->bse', v, Wv) + bv
        qp = jnp.einsum('bsd,ed->bse', q, Wq) + bq
        scale = 1.0 / jnp.sqrt(jnp.float32(kp.shape[-1]))
        scores = jnp.einsum('bqd,bkd->bqk', qp, kp) * scale
        probs = jax.nn.softmax(scores, axis=-1)
        ctx = jnp.einsum('bqk,bkd->bqd', probs, vp)
        return jnp.einsum('bqd,ed->bqe', ctx, Wo) + bo

    def _L0_ffn_ref(x, w_router, w_fc, w_gate, w_proj):
        import jax, jax.numpy as jnp
        import numpy as np
        E = 16
        K = 2
        LOAD = 1.0

        def _dispatch(xb, pb, cap):
            T, C = xb.shape
            top_k_probs, ei = jax.lax.top_k(pb, K)
            flat = ei.swapaxes(0, 1).ravel()
            one_hot = jax.nn.one_hot(flat, E, dtype=jnp.int32)
            pos = jnp.cumsum(one_hot, axis=0) * one_hot
            pos = pos.reshape(K, T, E).swapaxes(0, 1)
            pos = jnp.max(pos, axis=-1) - 1
            ei2 = flat.reshape(K, T).swapaxes(0, 1)
            xr = jnp.repeat(xb, K, axis=0)
            buf = jnp.zeros((E, cap, C), xb.dtype)
            buf = buf.at[ei2.ravel(), pos.ravel()].set(xr, mode='drop')
            return (top_k_probs, pos, ei2, buf)

        def _collect(eo_b, ei_b, pos_b, tk_b):
            out = eo_b[ei_b, pos_b]
            return jnp.sum(tk_b[..., None] * out, axis=1)
        B, T, C = x.shape
        cap = int(LOAD * K * max(1, T / E))
        g = jnp.einsum('btc,ce->bte', x, w_router)
        gate_probs = jax.nn.softmax(g, axis=-1)
        top_k_probs, positions, indices, expert_inputs = jax.vmap(lambda xb, pb: _dispatch(xb, pb, cap))(x, gate_probs)
        expert_inputs = jnp.swapaxes(expert_inputs, 0, 1).reshape(E, B * cap, C)
        gg = jnp.einsum('enc,ech->enh', expert_inputs, w_gate)
        h = jnp.einsum('enc,ech->enh', expert_inputs, w_fc)
        h = jax.nn.silu(gg) * h
        o = jnp.einsum('enh,ehc->enc', h, w_proj)
        expert_outputs = jnp.swapaxes(o.reshape(E, B, cap, C), 0, 1)
        y = jax.vmap(_collect)(expert_outputs, indices, positions, top_k_probs)
        return y
    x = x + _L0_xattn_ref(ctx_1024, ctx_1024, _layernorm(x, axis=-1), L0_xattn_Wk, L0_xattn_Wv, L0_xattn_bv, L0_xattn_Wq, L0_xattn_bq, L0_xattn_Wo, L0_xattn_bo)
    x = x + _L0_ffn_ref(_layernorm(x, axis=-1), L0_ffn_w_router, L0_ffn_w_fc, L0_ffn_w_gate, L0_ffn_w_proj)
    return x

_drawn_inputs = setup_inputs


def setup_inputs(seed=0):
    import zlib

    import numpy as np

    out = dict(_drawn_inputs(seed))
    spreads = {'L0_xattn_bv': (0.0, 0.1), 'L0_xattn_bq': (0.0, 0.362), 'L0_xattn_bo': (0.0, 0.1)}
    factors = {'L0_ffn_w_router': 8.0, 'L0_ffn_w_fc': 8.0, 'L0_ffn_w_gate': 8.0, 'L0_ffn_w_proj': 8.0}
    for name, (base, spread) in spreads.items():
        noise = np.random.default_rng([zlib.crc32(name.encode()), seed]).standard_normal(out[name].shape)
        drawn = base * np.exp(spread * noise) if base else spread * noise
        out[name] = jnp.asarray(drawn.astype(out[name].dtype))
    for name, factor in factors.items():
        out[name] = (out[name] * factor).astype(out[name].dtype)
    return out
```

```python
from contextlib import ExitStack

import concourse.bass as bass
from concourse import mybir

ALU = mybir.AluOpType
ACT = mybir.ActivationFunctionType
AX_X = mybir.AxisListType.X
F32, F16, BF16, I32 = mybir.dt.float32, mybir.dt.float16, mybir.dt.bfloat16, mybir.dt.int32

P = 128
EPS = 1e-5

XN_S = 2.0 ** 10
W_S = 2.0 ** 10
CTX_S = 2.0 ** 7
Q_S = 2.0 ** 7
PR_LN = 15
H_S = 2.0 ** 4
LN2 = 0.6931471805599453


def three_passes(pe, out, stationary, moving, first, last):
    s_hi, s_lo = stationary
    m_hi, m_lo = moving
    pe.matmul(out, s_hi, m_hi, start=first, stop=False)
    pe.matmul(out, s_hi, m_lo, start=False, stop=False)
    return pe.matmul(out, s_lo, m_hi, start=False, stop=last)


def build(nc, x, ctx_in, Wk, Wv, bv, Wq, bq, Wo, bo, w_router, w_fc, w_gate, w_proj, out):
    _, T, D = x.shape
    S = ctx_in.shape[1]
    E, _, H = w_fc.shape
    KT = D // P
    NT = T // P
    G4 = 4
    NG = NT // G4
    NK = S // P
    TAIL = S - NK * P
    CAP = 2 * T // E
    SM = float(D) ** -0.5
    assert D == 512 and 0 < TAIL <= 42 and CAP == 512 and NK == 3 * NG + 1 and H == 2 * P

    x_t = x.rearrange("a (n p) d -> (a n) p d", p=P)
    ctx2 = ctx_in.rearrange("a s d -> (a s) d")
    out_t = out.rearrange("a (n p) d -> (a n) p d", p=P)

    q_dram = nc.dram_tensor("q_dram", [NT, KT, P, 2 * P], F16, kind="Internal").ap()
    x1_dram = nc.dram_tensor("x1_dram", [NT, P, D], F32, kind="Internal").ap()
    rows_dram = nc.dram_tensor("rows_dram", [T, 2 * D], F16, kind="Internal").ap()
    TW = 16
    tbl_dram = nc.dram_tensor("tbl_dram", [2 * E * CAP, TW], F32, kind="Internal").ap()
    eo_dram = nc.dram_tensor("eo_dram", [E * CAP, D], F32, kind="Internal").ap()

    with ExitStack() as whole:
        def sem(name):
            return whole.enter_context(nc.semaphore(name))

        def sb(name, shape, dt, ctx=whole):
            return ctx.enter_context(nc.sbuf_tensor(name, shape, dt))

        ident = sb("ident", [P, P], F32)
        ident16 = sb("ident16", [P, P], F16)
        nhalf = sb("nhalf", [P, 1], F32)
        eps_c = sb("eps_c", [P, 1], F32)
        bo_row = sb("bo_row", [P, D], F32)
        R12 = sb("R12", [P, NT, 2], F32)
        PP = sb("PP", [P, NT, 2], F32)
        M12 = sb("M12", [P, NT, 2], F32)
        SE = sb("SE", [P, NT], F32)
        OH2 = sb("OH2", [P, NT, E], BF16)
        tot1 = sb("tot1", [P, E], F32)
        s_const = sem("s_const")

        with ExitStack() as attn:
            kT = sb("kT", [P, KT, 2, S], F16, attn)
            vv = sb("vv", [P, NK, 2, D], F16, attn)
            v_tail = sb("v_tail", [3 * TAIL, D], F16, attn)
            g_w = sb("g_w", [P, KT, 2, D], F16, attn)
            setup(nc, locals())
            attend(nc, locals())
        experts(nc, locals())
    return nc


def setup(nc, v):
    sb, sem = v["sb"], v["sem"]
    x_t, ctx2, q_dram, tbl_dram, TW = (v[n] for n in ("x_t", "ctx2", "q_dram", "tbl_dram", "TW"))
    Wk, Wv, bv, Wq, bq, Wo, bo = (v[n] for n in ("Wk", "Wv", "bv", "Wq", "bq", "Wo", "bo"))
    D, S, KT, NT, G4, NG, NK, TAIL, E, CAP = (v[n] for n in ("D", "S", "KT", "NT", "G4", "NG", "NK", "TAIL", "E", "CAP"))
    ident, ident16, nhalf, eps_c, bo_row, s_const = (v[n] for n in ("ident", "ident16", "nhalf", "eps_c", "bo_row", "s_const"))
    kT, vv, v_tail, g_w = v["kT"], v["vv"], v["v_tail"], v["g_w"]
    with ExitStack() as c:
        x_raw = sb("x_raw", [P, G4, D], F32, c)
        xs = sb("xs", [P, G4, D], F32, c)
        c_raw = sb("c_raw", [P, 3, D], F32, c)
        xnT = sb("xnT", [P, 2, KT, 2, G4 * P], F16, c)
        q_f = sb("q_f", [P, 2, G4 * P], F32, c)
        q_st = sb("q_st", [P, 2, G4, 2, P], F16, c)
        m_w = sb("m_w", [P, KT, 2, D], F16, c)
        w_a = sb("w_a", [P, KT, D], F32, c)
        w_b = sb("w_b", [P, KT, D], F32, c)
        woT = sb("woT", [P, KT, D], F32, c)
        bq_c = sb("bq_c", [P, KT], F32, c)
        bv_c = sb("bv_c", [P, KT], F32, c)
        bo_1 = sb("bo_1", [1, D], F32, c)
        ones = sb("ones", [P, P], F32, c)
        bv_b = sb("bv_b", [P, KT, P], F32, c)
        qb = sb("qb", [P, KT], F32, c)
        st6 = sb("st6", [P, 6], F32, c)
        mv = sb("mv", [P, 2], F32, c)
        var_e = sb("var_e", [P, 1], F32, c)
        rstd = sb("rstd", [P, 1], F32, c)
        zrow = sb("zrow", [P, E * CAP * TW // P], F32, c)
        tail_f = sb("tail_f", [3 * TAIL, D], F32, c)
        tail_hi = sb("tail_hi", [3 * TAIL, D], F16, c)
        tail_lo = sb("tail_lo", [3 * TAIL, D], F16, c)
        bank = [c.enter_context(nc.psum_tensor(f"bank{i}", [P, 512], F32)) for i in range(8)]

        s_w = [sem(f"s_w{i}") for i in range(4)]
        s_b = sem("s_b")
        s_x = [sem(f"s_x{i}") for i in range(G4)]
        s_c = [sem(f"s_c{i}") for i in range(3)]
        s_tail = sem("s_tail")
        s_zero = sem("s_zero")
        s_zr = sem("s_zr")
        mv_ready = sem("mv_ready")
        ve_ready = sem("ve_ready")
        rstd_ready = sem("rstd_ready")
        xs_ready = sem("xs_ready")
        xT_pe = sem("xT_pe")
        xT_hi = sem("xT_hi")
        xT_lo = sem("xT_lo")
        c_pe = sem("c_pe")
        c_hi = sem("c_hi")
        c_lo = sem("c_lo")
        mm_pe = sem("mm_pe")
        mm_hi = sem("mm_hi")
        mm_free = sem("mm_free")
        qb_pe = sem("qb_pe")
        qb_ready = sem("qb_ready")
        q_f_ready = sem("q_f_ready")
        q_hi = sem("q_hi")
        q_lo = sem("q_lo")
        q_out = [sem(f"q_out{i}") for i in range(2)]
        wo_pe = sem("wo_pe")
        wo_sb = sem("wo_sb")
        bvb = sem("bvb")
        bo_pe = sem("bo_pe")
        bo_done = sem("bo_done")
        tail_step = sem("tail_step")
        kt_pe = sem("kt_pe")
        kt_hi = sem("kt_hi")
        s_vt = sem("s_vt")
        w_free = sem("w_free")

        with nc.Block() as block:
            @block.sync
            def _(sp):
                def load_x(n, k):
                    sp.dma_start(x_raw[:, k, :], x_t[n, :, :]).then_inc(s_x[k], 16)

                def load_c(n, j):
                    sp.dma_start(c_raw[:, j, :], ctx2[bass.ds(n * P, P), :]).then_inc(s_c[j], 16)

                sp.dma_start(w_a[:], Wq.rearrange("(k p) d -> p k d", p=P)).then_inc(s_w[0], 16)
                sp.dma_start(w_b[:], Wk.rearrange("(k p) d -> p k d", p=P)).then_inc(s_w[1], 16)
                for k in range(G4):
                    load_x(k, k)
                for j in range(3):
                    load_c(j, j)

                def store_q(g, k):
                    sp.wait_ge(q_hi, G4 * g + k + 1)
                    sp.wait_ge(q_lo, G4 * g + k + 1)
                    sp.dma_start(q_dram[bass.ds(g * G4, G4), k].rearrange("j p c -> p j c"),
                                 q_st[:, k % 2].rearrange("p j h c -> p j (h c)")).then_inc(q_out[k % 2], 16)

                for n in range(G4, 3 * G4):
                    sp.wait_ge(xs_ready, n - G4 + 1)
                    load_x(n, n % G4)
                def step(g, more_x, more_c):
                    for k in range(G4):
                        if more_c and k < 3:
                            sp.wait_ge(c_lo, 3 * g + k + 1)
                            load_c(3 * (g + 1) + k, k)
                        store_q(g, k)
                        if more_x:
                            sp.wait_ge(xs_ready, G4 * (g + 2) + k + 1)
                            load_x(G4 * (g + 3) + k, k)

                sp.wait_ge(qb_pe, 1)
                sp.dma_start(w_a[:], Wv.rearrange("(k p) d -> p k d", p=P)).then_inc(s_w[2], 16)
                sp.dma_start(w_b[:], Wo.rearrange("(k p) d -> p k d", p=P)).then_inc(s_w[3], 16)

                with sp.Fori(0, NG - 3) as g:
                    step(g, True, True)
                step(NG - 3, False, True)
                step(NG - 2, False, True)
                sp.wait_ge(c_lo, 3 * (NG - 1) + 1)
                load_c(NK - 1, 0)
                step(NG - 1, False, False)
                for i in range(2):
                    sp.wait_ge(q_out[i], 16 * NG * 2)

            @block.gpsimd
            def _(pool):
                pool.memset(ident[:], 0.0).then_inc(s_const, 1)
                pool.memset(nhalf[:], -0.5).then_inc(s_const, 1)
                pool.memset(eps_c[:], EPS).then_inc(s_const, 1)
                pool.memset(ones[:], 1.0).then_inc(s_const, 1)
                pool.memset(zrow[:], 0.0).then_inc(s_zr, 1)
                pool.wait_ge(s_const, 4)
                pool.affine_select(out=ident[:], in_=ident[:], compare_op=ALU.not_equal, fill=1.0, base=0,
                                   pattern=[[-1, P]], channel_multiplier=1).then_inc(s_const, 1)
                pool.wait_ge(s_const, 5)
                pool.tensor_copy(ident16[:], ident[:]).then_inc(s_const, 1)

                def deviation(n):
                    pool.wait_ge(mv_ready, n + 1)
                    pool.tensor_tensor(var_e[:], mv[:, 1:2], eps_c[:], ALU.add).then_inc(ve_ready, 1)
                    pool.wait_ge(ve_ready, n + 1)
                    pool.tensor_tensor(rstd[:], var_e[:], nhalf[:], ALU.pow).then_inc(rstd_ready, 1)

                def q_low(g, k):
                    pool.wait_ge(q_hi, G4 * g + k + 1)
                    pool.tensor_tensor(q_st[:, k % 2, :, 1, :], q_f[:, k % 2].rearrange("p (j c) -> p j c", c=P),
                                       q_st[:, k % 2, :, 0, :], ALU.subtract).then_inc(q_lo, 1)

                for n in range(2 * G4):
                    deviation(n)

                def step(g, more_x):
                    for k in range(G4):
                        if more_x:
                            deviation(G4 * (g + 2) + k)
                        q_low(g, k)

                with pool.Fori(0, NG - 2) as g:
                    step(g, True)
                step(NG - 2, False)
                step(NG - 1, False)

            @block.scalar
            def _(act):
                act.dma_start(bq_c[:], bq.rearrange("(k p) -> p k", p=P), allow_slow_non_contiguous=True).then_inc(s_b, 16)
                act.dma_start(bv_c[:], bv.rearrange("(k p) -> p k", p=P), allow_slow_non_contiguous=True).then_inc(s_b, 16)
                act.dma_start(bo_1[:], bo.rearrange("(a d) -> a d", a=1)).then_inc(s_b, 16)
                for i in range(3):
                    act.dma_start(tail_f[TAIL * i:TAIL * (i + 1), :], ctx2[NK * P:S, :]).then_inc(s_tail, 16)
                act.wait_ge(s_zr, 1)
                for h in range(2):
                    act.dma_start(tbl_dram[h * E * CAP:(h + 1) * E * CAP].rearrange("(p r) c -> p (r c)", p=P),
                                  zrow[:]).then_inc(s_zero, 16)

                def product_high(u, out):
                    act.wait_ge(mm_pe, u + 1)
                    act.activation(out, bank[4 + u % 2][:], ACT.Copy, scale=W_S).then_inc(mm_hi, 1)

                def xT_high(g, k, b):
                    act.wait_ge(xT_pe, G4 * g + k + 1)
                    act.activation(xnT[:, b, :, 0, k * P:(k + 1) * P],
                                   bank[k % 2][:].rearrange("p (t c) -> p t c", c=P), ACT.Copy,
                                   scale=XN_S).then_inc(xT_hi, 1)

                def ctx_high(n, j, g1):
                    act.wait_ge(s_c[j], 16 * g1)
                    act.activation(vv[:, bass.ds(n, 1), 0, :].rearrange("p a d -> p (a d)"), c_raw[:, j, :],
                                   ACT.Copy, scale=CTX_S).then_inc(c_hi, 1)
                    act.wait_ge(c_pe, n + 1)
                    act.activation(kT[:, :, 0, bass.ds(n * P, P)],
                                   bank[2 + j % 2][:].rearrange("p (t c) -> p t c", c=P),
                                   ACT.Copy, scale=CTX_S).then_inc(c_hi, 1)

                def q_float(g, k):
                    act.wait_ge(mm_pe, KT + G4 * g + k + 1)
                    if k >= 2 or not isinstance(g, int) or g > 0:
                        act.wait_ge(q_lo, G4 * g + k - 1)
                    act.activation(q_f[:, k % 2], bank[4 + k % 2][:], ACT.Identity, bias=qb[:, k:k + 1],
                                   scale=Q_S / (XN_S * W_S)).then_inc(q_f_ready, 1)

                for k in range(G4):
                    xT_high(0, k, 0)
                for u in range(KT):
                    product_high(u, m_w[:, u, 0, :])
                act.wait_ge(qb_ready, 1)

                def step(g, b, more):
                    for k in range(G4):
                        if more:
                            xT_high(g + 1, k, 1 - b)
                        if k < 3:
                            ctx_high(3 * g + k, k, g + 1)
                        q_float(g, k)

                step(0, 0, True)
                with act.Fori(1, NG - 1, 2) as g:
                    step(g, 1, True)
                    step(g + 1, 0, True)
                step(NG - 1, 1, False)
                ctx_high(NK - 1, 0, NG + 1)
                act.wait_ge(kt_pe, 1)
                act.activation(kT[:, :, 0, NK * P:S], bank[7][:, 0:KT * TAIL].rearrange("p (t c) -> p t c", c=TAIL),
                               ACT.Copy, scale=CTX_S).then_inc(kt_hi, 1)
                for u in range(KT):
                    act.wait_ge(wo_pe, u + 1)
                    act.activation(woT[:, u, :], bank[u % 2][:], ACT.Copy).then_inc(wo_sb, 1)
                for u in range(KT):
                    act.wait_ge(mm_pe, KT + NT + u + 1)
                    act.activation(g_w[:, u, 0, :], bank[4 + u % 2][:], ACT.Copy, scale=W_S).then_inc(mm_hi, 1)
                act.wait_ge(bo_pe, 1)
                act.activation(bo_row[:], bank[6][:], ACT.Copy).then_inc(bo_done, 1)
                act.wait_ge(tail_step, 2)
                act.dma_start(v_tail[0:2 * TAIL, :], tail_hi[0:2 * TAIL, :]).then_inc(s_vt, 16)
                act.dma_start(v_tail[2 * TAIL:3 * TAIL, :], tail_lo[2 * TAIL:3 * TAIL, :]).then_inc(s_vt, 16)
                act.wait_ge(s_vt, 32)
                act.wait_ge(s_zero, 32)
                act.wait_ge(bo_done, 1)

            @block.vector
            def _(dve):
                def stats(n, k, s_load):
                    dve.wait_ge(s_x[k], s_load)
                    dve.bn_stats(st6[:], x_raw[:, k, :])
                    dve.drain()
                    dve.bn_aggr(mv[:], st6[:]).then_inc(mv_ready, 1)

                def normed(n, k):
                    dve.wait_ge(rstd_ready, n + 1)
                    dve.tensor_scalar(xs[:, k, :], x_raw[:, k, :], mv[:, 0:1], rstd[:],
                                      ALU.subtract, ALU.mult).then_inc(xs_ready, 1)

                def xT_low(g, k, b):
                    dve.wait_ge(xT_hi, G4 * g + k + 1)
                    dve.scalar_tensor_tensor(out=xnT[:, b, :, 1, k * P:(k + 1) * P],
                                             in0=bank[k % 2][:].rearrange("p (t c) -> p t c", c=P), scalar=XN_S,
                                             in1=xnT[:, b, :, 0, k * P:(k + 1) * P],
                                             op0=ALU.mult, op1=ALU.subtract).then_inc(xT_lo, 1)

                def ctx_low(n, j):
                    dve.wait_ge(c_hi, 2 * n + 2)
                    dve.scalar_tensor_tensor(out=vv[:, bass.ds(n, 1), 1, :].rearrange("p a d -> p (a d)"),
                                             in0=c_raw[:, j, :], scalar=CTX_S,
                                             in1=vv[:, bass.ds(n, 1), 0, :].rearrange("p a d -> p (a d)"),
                                             op0=ALU.mult, op1=ALU.subtract)
                    dve.scalar_tensor_tensor(out=kT[:, :, 1, bass.ds(n * P, P)],
                                             in0=bank[2 + j % 2][:].rearrange("p (t c) -> p t c", c=P), scalar=CTX_S,
                                             in1=kT[:, :, 0, bass.ds(n * P, P)],
                                             op0=ALU.mult, op1=ALU.subtract).then_inc(c_lo, 1)

                def q_high(g, k):
                    wait_for(dve, q_out[k % 2], 16 * (2 * g + k // 2))
                    dve.wait_ge(q_f_ready, G4 * g + k + 1)
                    dve.tensor_copy(q_st[:, k % 2, :, 0, :],
                                    q_f[:, k % 2].rearrange("p (j c) -> p j c", c=P)).then_inc(q_hi, 1)

                def product_low(u, out, hi, n_hi):
                    dve.wait_ge(mm_hi, n_hi)
                    dve.scalar_tensor_tensor(out=out, in0=bank[4 + u % 2][:], scalar=W_S, in1=hi,
                                             op0=ALU.mult, op1=ALU.subtract).then_inc(mm_free, 1)

                for k in range(G4):
                    stats(k, k, 16)
                    normed(k, k)
                for k in range(G4):
                    xT_low(0, k, 0)
                    stats(G4 + k, k, 32)
                    normed(G4 + k, k)
                for u in range(KT):
                    product_low(u, m_w[:, u, 1, :], m_w[:, u, 0, :], u + 1)
                dve.wait_ge(qb_pe, 1)
                dve.tensor_scalar(qb[:], bank[6][:, 0:KT], Q_S, None, ALU.mult).then_inc(qb_ready, 1)

                def step(g, b, more, more_x):
                    for k in range(G4):
                        if more_x:
                            stats(G4 * (g + 2) + k, k, 16 * (g + 3))
                        if more:
                            xT_low(g + 1, k, 1 - b)
                        if k < 3:
                            ctx_low(3 * g + k, k)
                        if more_x:
                            normed(G4 * (g + 2) + k, k)
                        q_high(g, k)

                step(0, 0, True, True)
                with dve.Fori(1, NG - 3, 2) as g:
                    step(g, 1, True, True)
                    step(g + 1, 0, True, True)
                step(NG - 3, 1, True, True)
                step(NG - 2, 0, True, False)
                step(NG - 1, 1, False, False)
                ctx_low(NK - 1, 0)
                dve.wait_ge(kt_hi, 1)
                dve.scalar_tensor_tensor(out=kT[:, :, 1, NK * P:S],
                                         in0=bank[7][:, 0:KT * TAIL].rearrange("p (t c) -> p t c", c=TAIL),
                                         scalar=CTX_S, in1=kT[:, :, 0, NK * P:S], op0=ALU.mult, op1=ALU.subtract)
                for k in range(KT):
                    dve.tensor_scalar(bv_b[:, k, :], ones[:], bv_c[:, k:k + 1], None, ALU.mult).then_inc(bvb, 1)
                for u in range(KT):
                    product_low(u, g_w[:, u, 1, :], g_w[:, u, 0, :], KT + u + 1)
                dve.wait_ge(s_tail, 48)
                dve.tensor_scalar(tail_hi[:], tail_f[:], CTX_S, None, ALU.mult).then_inc(tail_step, 1)
                dve.wait_ge(tail_step, 1)
                dve.scalar_tensor_tensor(out=tail_lo[:], in0=tail_f[:], scalar=CTX_S, in1=tail_hi[:],
                                         op0=ALU.mult, op1=ALU.subtract).then_inc(tail_step, 1)

            @block.tensor
            def _(pe):
                def xT(g, k):
                    pe.wait_ge(xs_ready, G4 * g + k + 1)
                    if not isinstance(g, int) or G4 * g + k >= 2:
                        pe.wait_ge(xT_lo, G4 * g + k - 1)
                    for t in range(KT):
                        last = pe.transpose(bank[k % 2][:, t * P:(t + 1) * P], xs[:, k, t * P:(t + 1) * P], ident[:])
                    last.then_inc(xT_pe, 1)

                def cT(n, j, g1):
                    pe.wait_ge(s_c[j], 16 * g1)
                    pe.wait_ge(c_lo, n if j == 0 else n - 1)
                    for t in range(KT):
                        last = pe.transpose(bank[2 + j % 2][:, t * P:(t + 1) * P], c_raw[:, j, t * P:(t + 1) * P], ident[:])
                    last.then_inc(c_pe, 1)

                def q_mm(g, k, b):
                    if k == 0:
                        pe.wait_ge(xT_lo, G4 * (g + 1))
                    if k >= 2 or not isinstance(g, int) or g > 0:
                        pe.wait_ge(q_f_ready, G4 * g + k - 1)
                    for t in range(KT):
                        last = three_passes(pe, bank[4 + k % 2][:],
                                            (m_w[:, t, 0, k * P:(k + 1) * P], m_w[:, t, 1, k * P:(k + 1) * P]),
                                            (xnT[:, b, t, 0, :], xnT[:, b, t, 1, :]), t == 0, t == KT - 1)
                    last.then_inc(mm_pe, 1)

                pe.wait_ge(s_const, 5)
                for k in range(G4):
                    xT(0, k)
                pe.wait_ge(s_w[0], 16)
                pe.wait_ge(s_w[1], 16)
                for u in range(KT):
                    if u >= 2:
                        pe.wait_ge(mm_free, u - 1)
                    for t in range(KT):
                        last = pe.matmul(bank[4 + u % 2][:], w_a[:, t, u * P:(u + 1) * P], w_b[:, t, :],
                                         start=(t == 0), stop=(t == KT - 1))
                    last.then_inc(mm_pe, 1)
                pe.wait_ge(s_b, 48)
                for u in range(KT):
                    for t in range(KT):
                        last = pe.matmul(bank[6][:, u:u + 1], w_b[:, t, u * P:(u + 1) * P], bq_c[:, t:t + 1],
                                         start=(t == 0), stop=(t == KT - 1))
                last.then_inc(qb_pe, 1)
                pe.wait_ge(mm_free, KT)

                def step(g, b, more):
                    for k in range(G4):
                        if more:
                            xT(g + 1, k)
                        if k < 3:
                            cT(3 * g + k, k, g + 1)
                        q_mm(g, k, b)

                def first_step():
                    for k in range(G4):
                        xT(1, k)
                        if k < 3:
                            pe.wait_ge(s_c[k], 16)
                            if k == 2:
                                pe.wait_ge(c_lo, 1)
                            for t in range(KT):
                                last = pe.transpose(bank[2 + k % 2][:, t * P:(t + 1) * P],
                                                    c_raw[:, k, t * P:(t + 1) * P], ident[:])
                            last.then_inc(c_pe, 1)
                        q_mm(0, k, 0)

                first_step()
                with pe.Fori(1, NG - 1, 2) as g:
                    step(g, 1, True)
                    step(g + 1, 0, True)
                step(NG - 1, 1, False)
                cT(NK - 1, 0, NG + 1)
                pe.wait_ge(s_tail, 48)
                for t in range(KT):
                    last = pe.transpose(bank[7][:, t * TAIL:(t + 1) * TAIL], tail_f[0:TAIL, t * P:(t + 1) * P],
                                        ident[0:TAIL, 0:TAIL])
                last.then_inc(kt_pe, 1)
                pe.wait_ge(s_w[2], 16)
                pe.wait_ge(s_w[3], 16)
                for u in range(KT):
                    if u >= 2:
                        pe.wait_ge(wo_sb, u - 1)
                    for t in range(KT):
                        last = pe.transpose(bank[u % 2][:, t * P:(t + 1) * P], w_b[:, t, u * P:(u + 1) * P], ident[:])
                    last.then_inc(wo_pe, 1)
                pe.wait_ge(wo_sb, KT)
                for u in range(KT):
                    if u >= 2:
                        pe.wait_ge(mm_free, KT + u - 1)
                    else:
                        pe.wait_ge(q_f_ready, NT - 1 + u)
                    for t in range(KT):
                        last = pe.matmul(bank[4 + u % 2][:], w_a[:, t, u * P:(u + 1) * P], woT[:, t, :],
                                         start=(t == 0), stop=(t == KT - 1))
                    last.then_inc(mm_pe, 1)
                pe.wait_ge(bvb, KT)
                for t in range(KT):
                    pe.matmul(bank[6][:], bv_b[:, t, :], woT[:, t, :], start=(t == 0), stop=False)
                pe.matmul(bank[6][:], ones[0:1, :], bo_1[:], start=False, stop=True).then_inc(bo_pe, 1)


def wait_for(engine, semaphore, n):
    if not isinstance(n, int) or n > 0:
        engine.wait_ge(semaphore, n)


def attend(nc, v):
    sb, sem = v["sb"], v["sem"]
    x_t, q_dram, x1_dram, rows_dram, w_router = (v[n] for n in ("x_t", "q_dram", "x1_dram", "rows_dram", "w_router"))
    tbl_dram, TW = v["tbl_dram"], v["TW"]
    D, S, KT, NT, NK, TAIL, E, CAP, SM = (v[n] for n in ("D", "S", "KT", "NT", "NK", "TAIL", "E", "CAP", "SM"))
    ident, nhalf, eps_c, bo_row = (v[n] for n in ("ident", "nhalf", "eps_c", "bo_row"))
    kT, vv, v_tail, g_w = v["kT"], v["vv"], v["v_tail"], v["g_w"]
    R12, PP, M12, SE, OH2, tot1 = (v[n] for n in ("R12", "PP", "M12", "SE", "OH2", "tot1"))
    NCH = -(-S // 512)
    NB = -(-NK // 4)
    width = [min(512, S - 512 * c) for c in range(NCH)]
    tiles = [min(4, NK - 4 * b) for b in range(NB)]
    SKIP = float(1 << 20)
    with ExitStack() as c_:
        def buf(name, shape, dt):
            return sb(name, shape, dt, c_)

        qt = buf("qt", [P, KT, 2 * P], F16)
        s_sb = buf("s_sb", [P, S], F32)
        p_sb = buf("p_sb", [P, S], F32)
        pT = buf("pT", [P, NK, 2, P], F16)
        mxc = buf("mxc", [P, NCH], F32)
        mx = buf("mx", [P, 1], F32)
        negb = buf("negb", [P, 1], F32)
        rsum = buf("rsum", [P, 1], F32)
        rinv = buf("rinv", [P, 1], F32)
        th16 = buf("th16", [P, TAIL], F16)
        tail3 = buf("tail3", [P, 3, TAIL], F32)
        tailT = buf("tailT", [3 * TAIL, P], F16)
        o_n = buf("o_n", [P, D], F32)
        oT = buf("oT", [P, KT, 2, P], F16)
        x_in = buf("x_in", [P, D], F32)
        xb = buf("xb", [P, D], F32)
        x1 = buf("x1", [P, D], F32)
        xs2 = buf("xs2", [P, D], F32)
        row16 = buf("row16", [P, 2 * D], F16)
        xT2 = buf("xT2", [P, KT, P], F32)
        st6 = buf("st6b", [P, 6], F32)
        mv = buf("mvb", [P, 2], F32)
        var_e = buf("var_eb", [P, 1], F32)
        rstd = buf("rstdb", [P, 1], F32)
        w_r = buf("w_r", [P, KT, E], F32)
        rev = buf("rev", [P, E], F32)
        lg = buf("lg", [P, E], F32)
        hit = buf("hit", [P, E], F32)
        lg2 = buf("lg2", [P, E], F32)
        m12 = buf("m12", [P, 2], F32)
        r12 = buf("r12", [P, 2], F32)
        negm = buf("negm", [P, 1], F32)
        rex = buf("rex", [P, E], F32)
        oh = buf("oh", [P, 2, E], BF16)
        acc_oh = buf("acc_oh", [P, 2, E], BF16)
        before = buf("before", [P, P], BF16)
        ones_b = buf("ones_b", [P, P], BF16)
        sel = buf("sel", [P, 2, E], F32)
        sg = buf("sg", [P, 2], F32)
        off = buf("off", [P, 2], F32)
        ia = buf("ia", [P, 2], F32)
        ib = buf("ib", [P, 2], F32)
        ic = buf("ic", [P, 2], F32)
        idf = buf("idf", [P, 2], F32)
        idx = buf("idx", [P, 2], I32)
        tok_all = buf("tok_all", [P, NT, TW], F32)
        tok = buf("tok", [P, TW], F32)
        sc = [c_.enter_context(nc.psum_tensor(f"sc{i}", [P, 512], F32)) for i in range(3)]
        pt = [c_.enter_context(nc.psum_tensor(f"pt{i}", [P, 512], F32)) for i in range(2)]
        acc = c_.enter_context(nc.psum_tensor("acc", [P, 512], F32))
        ps_t = c_.enter_context(nc.psum_tensor("ps_t", [P, 512], F32))
        ps_m = c_.enter_context(nc.psum_tensor("ps_m", [P, 512], F32))

        a_const = sem("a_const")
        a_wr = sem("a_wr")
        q_in = sem("q_in")
        sc_pe = sem("sc_pe")
        sc_ev = sem("sc_ev")
        bias_rdy = sem("bias_rdy")
        exp_done = sem("exp_done")
        tail_rdy = sem("tail_rdy")
        t_pe = sem("t_pe")
        pt_hi = sem("pt_hi")
        pt_lo = sem("pt_lo")
        pv_pe = sem("pv_pe")
        on_rdy = sem("on_rdy")
        oT_pe = sem("oT_pe")
        oT_hi = sem("oT_hi")
        oT_lo = sem("oT_lo")
        pj_pe = sem("pj_pe")
        x_ld = sem("x_ld")
        xb_rdy = sem("xb_rdy")
        x1_rdy = sem("x1_rdy")
        x1_out = sem("x1_out")
        mv_rdy = sem("mv_rdy")
        ve_rdy = sem("ve_rdy")
        rs_rdy = sem("rs_rdy")
        xs_rdy = sem("xs_rdy")
        xs_hi = sem("xs_hi")
        xs_lo = sem("xs_lo")
        xT_pe2 = sem("xT_pe2")
        xT_ev = sem("xT_ev")
        lg_pe = sem("lg_pe")
        oh_rdy = sem("oh_rdy")
        rx_done = sem("rx_done")
        pos_pe = sem("pos_pe")
        idx_rdy = sem("idx_rdy")
        scat = sem("scat")
        r_out = sem("r_out")
        tot_pe = sem("tot_pe")
        tot_rdy = sem("tot_rdy")

        with nc.Block() as block:
            @block.sync
            def _(sp):
                def load_q(t):
                    sp.dma_start(qt[:], q_dram[bass.ds(t, 1)].rearrange("a k p c -> p (a k) c")).then_inc(q_in, 16)

                def load_x(t):
                    sp.dma_start(x_in[:], x_t[bass.ds(t, 1)].rearrange("a p c -> p (a c)")).then_inc(x_ld, 16)

                def store_x1(t):
                    sp.wait_ge(x1_rdy, t + 1)
                    sp.dma_start(x1_dram[bass.ds(t, 1)].rearrange("a p c -> p (a c)"), x1[:]).then_inc(x1_out, 16)

                def store_rows(t):
                    sp.wait_ge(xs_lo, t + 1)
                    sp.dma_start(rows_dram[bass.ds(P * t, P), :], row16[:]).then_inc(r_out, 16)

                sp.dma_start(w_r[:], w_router.rearrange("(k p) e -> p k e", p=P)).then_inc(a_wr, 16)
                load_q(0)
                load_x(0)
                sp.wait_ge(sc_pe, NCH)
                load_q(1)

                def step(t, post, more):
                    if more:
                        sp.wait_ge(sc_pe, NCH * (t + 2))
                        load_q(t + 2)
                    if post:
                        store_x1(t - 1)
                        store_rows(t - 1)
                    sp.wait_ge(xb_rdy, t + 1)
                    if more or post:
                        load_x(t + 1)

                step(0, False, True)
                step(1, True, True)
                with sp.Fori(2, NT - 2) as t:
                    step(t, True, True)
                step(NT - 2, True, False)
                for t in (NT - 2, NT - 1):
                    store_x1(t)
                    store_rows(t)
                sp.wait_ge(x1_out, 16 * NT)
                sp.wait_ge(r_out, 16 * NT)

            @block.gpsimd
            def _(pool):
                pool.memset(before[:], 1.0).then_inc(a_const, 1)
                pool.memset(ones_b[:], 1.0).then_inc(a_const, 1)
                pool.memset(acc_oh[:], 0.0).then_inc(a_const, 1)
                pool.memset(sg[:, 0:1], 1.0).then_inc(a_const, 1)
                pool.memset(sg[:, 1:2], -1.0).then_inc(a_const, 1)
                pool.memset(off[:, 0:1], float(E * CAP)).then_inc(a_const, 1)
                pool.memset(off[:, 1:2], float(2 * E * CAP + CAP - 1)).then_inc(a_const, 1)
                pool.iota(rev[:], [[-1, E]], base=E, channel_multiplier=0,
                          allow_small_or_imprecise_dtypes=True).then_inc(a_const, 1)
                pool.iota(tok_all[:], [[P, NT], [0, TW]], base=0, channel_multiplier=1,
                          allow_small_or_imprecise_dtypes=True).then_inc(a_const, 1)
                pool.wait_ge(a_const, 9)
                pool.affine_select(out=before[:], in_=before[:], compare_op=ALU.is_gt, fill=0.0, base=0,
                                   pattern=[[1, P]], channel_multiplier=-1).then_inc(a_const, 1)

                def add_bias(t):
                    pool.wait_ge(x_ld, 16 * (t + 1))
                    wait_for(pool, x1_rdy, t)
                    pool.tensor_tensor(xb[:], x_in[:], bo_row[:], ALU.add).then_inc(xb_rdy, 1)

                def deviation(t):
                    pool.wait_ge(mv_rdy, t + 1)
                    pool.tensor_tensor(var_e[:], mv[:, 1:2], eps_c[:], ALU.add).then_inc(ve_rdy, 1)
                    pool.wait_ge(ve_rdy, t + 1)
                    pool.tensor_tensor(rstd[:], var_e[:], nhalf[:], ALU.pow).then_inc(rs_rdy, 1)

                def scatter(t):
                    wait_for(pool, scat, 32 * t)
                    pool.wait_ge(idx_rdy, t + 1)
                    pool.tensor_tensor(idf[:], ia[:], ic[:], ALU.add)
                    pool.tensor_copy(tok[:], tok_all[:, bass.ds(t, 1), :].rearrange("p a w -> p (a w)"))
                    pool.drain()
                    pool.tensor_copy(idx[:], idf[:])
                    pool.drain()
                    for k in range(2):
                        pool.indirect_dma_start(tbl_dram, bass.IndirectOffsetOnAxis(ap=idx[:, k:k + 1], axis=0),
                                                tok[:], None, bounds_check=2 * E * CAP - 1,
                                                oob_is_err=False).then_inc(scat, 16)

                def step(t):
                    deviation(t - 1)
                    add_bias(t)
                    scatter(t - 1)

                add_bias(0)
                step(1)
                with pool.Fori(2, NT) as t:
                    step(t)
                deviation(NT - 1)
                scatter(NT - 1)
                pool.wait_ge(scat, 32 * NT)

            @block.scalar
            def _(act):
                def high(t, b):
                    n = tiles[b]
                    act.wait_ge(t_pe, NB * t + b + 1)
                    act.activation(pT[:, 4 * b:4 * b + n, 0, :], pt[b % 2][:, 0:n * P].rearrange("p (j c) -> p j c", c=P),
                                   ACT.Copy).then_inc(pt_hi, 1)

                def exponentials(t):
                    act.wait_ge(bias_rdy, t + 1)
                    if not isinstance(t, int) or t > 0:
                        act.wait_ge(t_pe, NB * t)
                        act.wait_ge(tail_rdy, t)
                    act.activation(p_sb[:], s_sb[:], ACT.Exp, bias=negb[:], scale=SM / (CTX_S * Q_S),
                                   accum_out=rsum[:]).then_inc(exp_done, 1)

                def oT_high(t):
                    act.wait_ge(oT_pe, t + 1)
                    act.activation(oT[:, :, 0, :], ps_t[:].rearrange("p (j c) -> p j c", c=P), ACT.Copy).then_inc(oT_hi, 1)

                def rows_high(t):
                    act.wait_ge(xs_rdy, t + 1)
                    wait_for(act, r_out, 16 * t)
                    act.activation(row16[:, 0:D], xs2[:], ACT.Copy, scale=XN_S).then_inc(xs_hi, 1)

                def xT_copy(t):
                    act.wait_ge(xT_pe2, t + 1)
                    act.activation(xT2[:], ps_t[:].rearrange("p (j c) -> p j c", c=P), ACT.Copy).then_inc(xT_ev, 1)

                def router_sum(t):
                    act.wait_ge(oh_rdy, t + 1)
                    act.activation(rex[:], lg[:], ACT.Exp, bias=negm[:],
                                   accum_out=SE[:, bass.ds(t, 1)]).then_inc(rx_done, 1)

                def step(t, post, more):
                    if post:
                        oT_high(t - 1)
                    for b in range(3):
                        high(t, b)
                    if post:
                        rows_high(t - 1)
                    high(t, 3)
                    if post:
                        xT_copy(t - 1)
                    for b in range(4, NB):
                        high(t, b)
                    if post:
                        router_sum(t - 1)
                    if more:
                        exponentials(t + 1)

                exponentials(0)
                step(0, False, True)
                step(1, True, True)
                with act.Fori(2, NT - 1) as t:
                    step(t, True, True)
                step(NT - 1, True, False)
                oT_high(NT - 1)
                rows_high(NT - 1)
                xT_copy(NT - 1)
                router_sum(NT - 1)
                act.wait_ge(rx_done, NT)

            @block.vector
            def _(dve):
                def evacuate(t, c):
                    dve.wait_ge(sc_pe, NCH * t + c + 1)
                    if c == 0:
                        wait_for(dve, exp_done, t)
                    dve.tensor_scalar(s_sb[:, 512 * c:512 * c + width[c]], sc[c % 3][:, 0:width[c]], 1.0, None,
                                      ALU.mult, ALU.max, accum_out=mxc[:, c:c + 1]).then_inc(sc_ev, 1)

                def bias(t):
                    dve.drain()
                    dve.reduce_max(mx[:], mxc[:], AX_X)
                    dve.drain()
                    dve.tensor_scalar(negb[:], mx[:], -SM / (CTX_S * Q_S), PR_LN * LN2,
                                      ALU.mult, ALU.add).then_inc(bias_rdy, 1)

                def tail(t):
                    dve.wait_ge(exp_done, t + 1)
                    dve.reciprocal(rinv[:], rsum[:])
                    dve.tensor_copy(th16[:], p_sb[:, NK * P:S])
                    dve.drain()
                    dve.tensor_copy(tail3[:, 0, :], th16[:])
                    dve.tensor_copy(tail3[:, 2, :], th16[:])
                    dve.tensor_tensor(tail3[:, 1, :], p_sb[:, NK * P:S], th16[:], ALU.subtract).then_inc(tail_rdy, 1)

                def low(t, b):
                    n = tiles[b]
                    dve.wait_ge(pt_hi, NB * t + b + 1)
                    if b == NB - 1:
                        dve.tensor_copy(tailT[:], pt[b % 2][0:3 * TAIL, P:2 * P])
                    dve.tensor_tensor(pT[:, 4 * b:4 * b + n, 1, :], pt[b % 2][:, 0:n * P].rearrange("p (j c) -> p j c", c=P),
                                      pT[:, 4 * b:4 * b + n, 0, :], ALU.subtract).then_inc(pt_lo, 1)

                def divide(t):
                    dve.wait_ge(pv_pe, t + 1)
                    wait_for(dve, oT_pe, t)
                    dve.tensor_scalar(o_n[:], acc[:], rinv[:], None, ALU.mult).then_inc(on_rdy, 1)

                def oT_low(t):
                    dve.wait_ge(oT_hi, t + 1)
                    dve.tensor_tensor(oT[:, :, 1, :], ps_t[:].rearrange("p (j c) -> p j c", c=P), oT[:, :, 0, :],
                                      ALU.subtract).then_inc(oT_lo, 1)

                def residual(t):
                    dve.wait_ge(pj_pe, t + 1)
                    dve.wait_ge(xb_rdy, t + 1)
                    wait_for(dve, x1_out, 16 * t)
                    dve.scalar_tensor_tensor(out=x1[:], in0=ps_m[:], scalar=1.0 / (CTX_S * W_S), in1=xb[:],
                                             op0=ALU.mult, op1=ALU.add).then_inc(x1_rdy, 1)
                    dve.drain()
                    dve.bn_stats(st6[:], x1[:])
                    dve.drain()
                    dve.bn_aggr(mv[:], st6[:]).then_inc(mv_rdy, 1)

                def normed(t):
                    dve.wait_ge(rs_rdy, t + 1)
                    dve.tensor_scalar(xs2[:], x1[:], mv[:, 0:1], rstd[:], ALU.subtract, ALU.mult).then_inc(xs_rdy, 1)

                def rows_low(t):
                    dve.wait_ge(xs_hi, t + 1)
                    dve.scalar_tensor_tensor(out=row16[:, D:2 * D], in0=xs2[:], scalar=XN_S, in1=row16[:, 0:D],
                                             op0=ALU.mult, op1=ALU.subtract).then_inc(xs_lo, 1)

                def choose(k, logits):
                    dve.reduce_max(m12[:, k:k + 1], logits[:], AX_X)
                    dve.drain()
                    dve.scalar_tensor_tensor(out=hit[:], in0=logits[:], scalar=m12[:, k:k + 1], in1=rev[:],
                                             op0=ALU.is_equal, op1=ALU.mult)
                    dve.drain()
                    dve.reduce_max(r12[:, k:k + 1], hit[:], AX_X)
                    dve.drain()
                    return dve.tensor_scalar(oh[:, k, :], rev[:], r12[:, k:k + 1], None, ALU.is_equal)

                def route(t):
                    wait_for(dve, rx_done, t)
                    dve.wait_ge(lg_pe, t + 1)
                    dve.tensor_copy(lg[:], ps_m[:, 0:E])
                    dve.drain()
                    choose(0, lg)
                    dve.tensor_scalar(negm[:], m12[:, 0:1], -1.0, None, ALU.mult)
                    dve.drain()
                    dve.scalar_tensor_tensor(out=lg2[:], in0=oh[:, 0, :], scalar=-1e30, in1=lg[:],
                                             op0=ALU.mult, op1=ALU.add)
                    dve.drain()
                    choose(1, lg2).then_inc(oh_rdy, 1)
                    dve.tensor_copy(M12[:, bass.ds(t, 1), :].rearrange("p a k -> p (a k)"), m12[:])
                    dve.tensor_copy(R12[:, bass.ds(t, 1), :].rearrange("p a k -> p (a k)"), r12[:])

                def place(t):
                    dve.wait_ge(pos_pe, t + 1)
                    wait_for(dve, scat, 32 * t)
                    dve.tensor_tensor(sel[:], ps_m[:, 0:2 * E].rearrange("p (k e) -> p k e", k=2), oh[:], ALU.mult)
                    dve.tensor_tensor(acc_oh[:], acc_oh[:], oh[:], ALU.add)
                    dve.tensor_copy(OH2[:, bass.ds(t, 1), :].rearrange("p a e -> p (a e)"), oh[:, 1, :])
                    dve.scalar_tensor_tensor(out=ia[:], in0=r12[:], scalar=-float(CAP), in1=off[:],
                                             op0=ALU.mult, op1=ALU.add)
                    dve.drain()
                    dve.reduce_sum(ib[:], sel[:], AX_X)
                    dve.drain()
                    dve.tensor_copy(PP[:, bass.ds(t, 1), :].rearrange("p a k -> p (a k)"), ib[:])
                    dve.tensor_scalar(ic[:], ib[:], float(CAP), SKIP, ALU.is_ge, ALU.mult)
                    dve.tensor_tensor(ib[:], ib[:], sg[:], ALU.mult)
                    dve.drain()
                    dve.tensor_tensor(ia[:], ia[:], ib[:], ALU.add).then_inc(idx_rdy, 1)

                def step(t, post, more):
                    if post:
                        divide(t - 1)
                    for c in range(NCH if more else 0):
                        evacuate(t + 1, c)
                        if c == 2 and post:
                            oT_low(t - 1)
                    if more:
                        bias(t + 1)
                    elif post:
                        oT_low(t - 1)
                    tail(t)
                    low(t, 0)
                    low(t, 1)
                    if post:
                        residual(t - 1)
                    low(t, 2)
                    if post:
                        normed(t - 1)
                        rows_low(t - 1)
                    low(t, 3)
                    low(t, 4)
                    if post:
                        route(t - 1)
                    low(t, 5)
                    low(t, 6)
                    if post:
                        place(t - 1)

                dve.wait_ge(a_const, 10)
                for c in range(NCH):
                    evacuate(0, c)
                bias(0)
                step(0, False, True)
                step(1, True, True)
                with dve.Fori(2, NT - 1) as t:
                    step(t, True, True)
                step(NT - 1, True, False)
                divide(NT - 1)
                oT_low(NT - 1)
                residual(NT - 1)
                normed(NT - 1)
                rows_low(NT - 1)
                route(NT - 1)
                place(NT - 1)
                dve.wait_ge(tot_pe, 1)
                dve.tensor_copy(tot1[:], ps_t[:, 0:E]).then_inc(tot_rdy, 1)

            @block.tensor
            def _(pe):
                def scores(t, c):
                    if c == 0:
                        pe.wait_ge(q_in, 16 * (t + 1))
                    wait_for(pe, sc_ev, NCH * t if c < 3 else NCH * t + c - 2)
                    for k in range(KT):
                        q_hi, q_lo = qt[:, k, 0:P], qt[:, k, P:2 * P]
                        lo, hi = 512 * c, 512 * c + width[c]
                        last = three_passes(pe, sc[c % 3][:, 0:width[c]], (q_hi, q_lo),
                                            (kT[:, k, 0, lo:hi], kT[:, k, 1, lo:hi]), k == 0, k == KT - 1)
                    last.then_inc(sc_pe, 1)

                def transposed(t, b):
                    wait_for(pe, pt_lo, NB * t if b < 2 else NB * t + b - 1)
                    if b == 0:
                        pe.wait_ge(exp_done, t + 1)
                    for j in range(tiles[b]):
                        k = 4 * b + j
                        last = pe.transpose(pt[b % 2][:, j * P:(j + 1) * P], p_sb[:, k * P:(k + 1) * P], ident[:])
                    if b == NB - 1:
                        pe.wait_ge(tail_rdy, t + 1)
                        last = pe.transpose(pt[b % 2][0:3 * TAIL, P:2 * P], tail3[:].rearrange("p a k -> p (a k)"), ident[:])
                    last.then_inc(t_pe, 1)

                def times_context(t, b):
                    if b == 0:
                        wait_for(pe, on_rdy, t)
                    pe.wait_ge(pt_lo, NB * t + b + 1)
                    for j in range(tiles[b]):
                        k = 4 * b + j
                        three_passes(pe, acc[:], (pT[:, k, 0, :], pT[:, k, 1, :]), (vv[:, k, 0, :], vv[:, k, 1, :]),
                                     k == 0, False)
                    if b == NB - 1:
                        pe.matmul(acc[:], tailT[:], v_tail[:], start=False, stop=True).then_inc(pv_pe, 1)

                def oT_pe_(t):
                    pe.wait_ge(on_rdy, t + 1)
                    wait_for(pe, xT_ev, t)
                    for k in range(KT):
                        last = pe.transpose(ps_t[:, k * P:(k + 1) * P], o_n[:, k * P:(k + 1) * P], ident[:])
                    last.then_inc(oT_pe, 1)

                def project(t):
                    pe.wait_ge(oT_lo, t + 1)
                    wait_for(pe, idx_rdy, t)
                    for k in range(KT):
                        last = three_passes(pe, ps_m[:], (oT[:, k, 0, :], oT[:, k, 1, :]), (g_w[:, k, 0, :], g_w[:, k, 1, :]),
                                            k == 0, k == KT - 1)
                    last.then_inc(pj_pe, 1)

                def xT_pe_(t):
                    pe.wait_ge(xs_rdy, t + 1)
                    for k in range(KT):
                        last = pe.transpose(ps_t[:, k * P:(k + 1) * P], xs2[:, k * P:(k + 1) * P], ident[:])
                    last.then_inc(xT_pe2, 1)

                def logits(t):
                    pe.wait_ge(xT_ev, t + 1)
                    for k in range(KT):
                        last = pe.matmul(ps_m[:, 0:E], xT2[:, k, :], w_r[:, k, :], start=(k == 0), stop=(k == KT - 1))
                    last.then_inc(lg_pe, 1)

                def places(t):
                    pe.wait_ge(oh_rdy, t + 1)
                    pe.matmul(ps_m[:, 0:2 * E], before[:], oh[:].rearrange("p k e -> p (k e)"), start=True, stop=False)
                    pe.matmul(ps_m[:, 0:2 * E], ones_b[:], acc_oh[:].rearrange("p k e -> p (k e)"),
                              start=False, stop=True).then_inc(pos_pe, 1)

                def step(t, post, more):
                    for c in range(NCH if more else 0):
                        scores(t + 1, c)
                        if c == 1 and post:
                            oT_pe_(t - 1)
                    if post and not more:
                        oT_pe_(t - 1)
                    transposed(t, 0)
                    transposed(t, 1)
                    if post:
                        project(t - 1)
                    for b in range(NB):
                        times_context(t, b)
                        if b + 2 < NB:
                            transposed(t, b + 2)
                        if post and b == 2:
                            xT_pe_(t - 1)
                        if post and b == 3:
                            logits(t - 1)
                        if post and b == 5:
                            places(t - 1)

                pe.wait_ge(a_const, 10)
                pe.wait_ge(a_wr, 16)
                for c in range(NCH):
                    scores(0, c)
                step(0, False, True)
                step(1, True, True)
                with pe.Fori(2, NT - 1) as t:
                    step(t, True, True)
                step(NT - 1, True, False)
                oT_pe_(NT - 1)
                project(NT - 1)
                xT_pe_(NT - 1)
                logits(NT - 1)
                places(NT - 1)
                pe.wait_ge(idx_rdy, NT)
                pe.matmul(ps_t[:, 0:E], ones_b[:], acc_oh[:, 0, :], start=True, stop=True).then_inc(tot_pe, 1)


def experts(nc, v):
    sb, sem = v["sb"], v["sem"]
    w_fc, w_gate, w_proj, out_t = (v[n] for n in ("w_fc", "w_gate", "w_proj", "out_t"))
    x1_dram, rows_dram, eo_dram = (v[n] for n in ("x1_dram", "rows_dram", "eo_dram"))
    tbl_dram, TW, T, ident = v["tbl_dram"], v["TW"], v["T"], v["ident"]
    D, KT, NT, E, CAP, H = (v[n] for n in ("D", "KT", "NT", "E", "CAP", "H"))
    ident16 = v["ident16"]
    R12, PP, M12, SE, OH2, tot1 = (v[n] for n in ("R12", "PP", "M12", "SE", "OH2", "tot1"))
    J = CAP // P
    HT = H // P
    SETS, PER = 4, 2
    with ExitStack() as c_:
        def buf(name, shape, dt):
            return sb(name, shape, dt, c_)

        x1s = buf("x1s", [P, NT, D], F32)
        crow = buf("crow", [P, NT, 2], F32)
        pw = buf("pw", [P, NT, 2], F32)
        ee = buf("ee", [P, NT, 2], F32)
        tmp2 = buf("tmp2", [P, NT, 2], F32)
        sel2 = buf("sel2", [P, NT, E], F32)
        t1m = buf("t1m", [P, E], F32)
        tsel = buf("tsel", [P, NT], F32)
        tbl = buf("tbl", [E * J, 2, P * TW], F32)
        up_t = buf("up_t", [P, E * J], F32)
        rr = buf("rr", [P, E, J], F32)
        cmp = buf("cmp", [P, E, J], F32)
        grow = buf("grow", [P, E, J], F32)
        gidx = buf("gidx", [P, E, J], I32)
        rows = buf("rows", [P, J, 2 * D], F16)
        xT = buf("xTe", [P, KT, 2, CAP], F16)
        raw_g = buf("raw_g", [P, KT, H], F32)
        raw_f = buf("raw_f", [P, KT, H], F32)
        raw_p = buf("raw_p", [P, HT, D], F32)
        wg = buf("wg", [P, 2, KT, 2, H], F16)
        wf = buf("wf", [P, 2, KT, 2, H], F16)
        wp = buf("wp", [P, HT, 2, D], F16)
        th = buf("th", [P, HT, CAP], F32)
        gs = buf("gs", [P, HT, CAP], F32)
        hf = buf("hf", [P, HT, CAP], F32)
        hT = buf("hT", [P, 2, HT, 2, CAP], F16)
        o_sb = buf("o_sb", [P, J, D], F32)
        cidx = buf("cidx", [P, NT, 2], I32)
        cw = buf("cw", [P, SETS, PER * 2], F32)
        got = buf("got", [P, SETS, PER * 2, D], F32)
        pg = [c_.enter_context(nc.psum_tensor(f"pg{i}", [P, 512], F32)) for i in range(4)]
        px = [c_.enter_context(nc.psum_tensor(f"px{i}", [P, 1024], F16)) for i in range(2)]
        po = [c_.enter_context(nc.psum_tensor(f"po{i}", [P, 512], F32)) for i in range(2)]

        e_const = sem("e_const")
        tbl_in = sem("tbl_in")
        tbl_pe = sem("tbl_pe")
        grow_rdy = sem("grow_rdy")
        crow_rdy = sem("crow_rdy")
        pe2 = sem("pe2")
        d_rdy = sem("d_rdy")
        x1_in = sem("x1_in")
        gf_rdy = sem("gf_rdy")
        g_in = [sem(f"g_in{i}") for i in range(J)]
        wg_in, wf_in, wp_in = sem("wg_in"), sem("wf_in"), sem("wp_in")
        wgh, wgl = sem("wgh"), sem("wgl")
        wph, wpl = sem("wph"), sem("wpl")
        x_pe, x_ev = sem("x_pe"), sem("x_ev")
        x_ev2 = sem("x_ev2")
        u_pe = sem("u_pe")
        th_rdy = sem("th_rdy")
        h_rdy = sem("h_rdy")
        o_pe, o_ev = sem("o_pe"), sem("o_ev")
        o_out = [sem(f"o_out{i}") for i in range(J)]
        c_in = [sem(f"c_in{i}") for i in range(SETS)]
        c_use = sem("c_use")
        y_out = sem("y_out")

        with nc.Block() as block:
            @block.sync
            def _(sp):
                def load_gf(e):
                    sp.dma_start(raw_g[:], w_gate[bass.ds(e, 1)].rearrange("a (k p) h -> p (a k) h", p=P)).then_inc(wg_in, 16)
                    sp.dma_start(raw_f[:], w_fc[bass.ds(e, 1)].rearrange("a (k p) h -> p (a k) h", p=P)).then_inc(wf_in, 16)

                def load_p(e):
                    sp.dma_start(raw_p[:], w_proj[bass.ds(e, 1)].rearrange("a (k p) d -> p (a k) d", p=P)).then_inc(wp_in, 16)

                def store(e, j):
                    sp.wait_ge(o_ev, J * e + j + 1)
                    sp.dma_start(eo_dram[bass.ds(CAP * e + P * j, P), :], o_sb[:, j, :]).then_inc(o_out[j], 16)

                for h in range(2):
                    sp.dma_start(tbl[:, h, :], tbl_dram[h * E * CAP:(h + 1) * E * CAP].rearrange("(m c) w -> m (c w)", c=P))\
                      .then_inc(tbl_in, 16)
                load_gf(0)
                load_p(0)
                for n in range(4):
                    sp.dma_start(x1s[:, 8 * n:8 * n + 8, :],
                                 x1_dram[8 * n:8 * n + 8].rearrange("n p d -> p n d")).then_inc(x1_in, 16)
                def step(e, before, more_gf, more_p):
                    if more_gf:
                        sp.wait_ge(wgl, 2 * (e + 2))
                        load_gf(e + 2)
                    if before:
                        for j in range(J):
                            store(e - 1, j)
                    if more_p:
                        sp.wait_ge(wpl, e + 1)
                        load_p(e + 1)

                sp.wait_ge(wgl, 2)
                load_gf(1)
                step(0, False, True, True)
                with sp.Fori(1, E - 2) as e:
                    step(e, True, True, True)
                step(E - 2, True, False, True)
                step(E - 1, True, False, False)
                for j in range(J):
                    store(E - 1, j)
                with sp.Fori(0, NT // PER) as n:
                    sp.wait_ge(c_use, n + 1)
                    sp.dma_start(out_t[bass.ds(PER * n, PER)].rearrange("n p d -> p n d"),
                                 x1s[:, bass.ds(PER * n, PER), :]).then_inc(y_out, 16)
                sp.wait_ge(y_out, 16 * (NT // PER))

            @block.gpsimd
            def _(pool):
                pool.iota(rr[:], [[0, E], [P, J]], base=0, channel_multiplier=1,
                          allow_small_or_imprecise_dtypes=True).then_inc(e_const, 1)

                def gather(e):
                    for j in range(J):
                        wait_for(pool, x_pe, J * (e - 1) + j + 1)
                        pool.indirect_dma_start(rows[:, j, :], None, rows_dram,
                                                bass.IndirectOffsetOnAxis(ap=gidx[:, e, j:j + 1], axis=0),
                                                bounds_check=T - 1, oob_is_err=False).then_inc(g_in[j], 16)

                def collect(n):
                    wait_for(pool, c_use, n - SETS + 1)
                    for j in range(PER):
                        for k in range(2):
                            pool.indirect_dma_start(got[:, n % SETS, 2 * j + k, :], None, eo_dram,
                                                    bass.IndirectOffsetOnAxis(ap=cidx[:, PER * n + j, k:k + 1], axis=0),
                                                    bounds_check=E * CAP - 1, oob_is_err=False).then_inc(c_in[n % SETS], 16)

                pool.wait_ge(grow_rdy, 1)
                for e in range(E):
                    gather(e)
                pool.wait_ge(crow_rdy, 1)
                for j in range(J):
                    pool.wait_ge(o_out[j], 16 * E)
                for n in range(NT // PER):
                    collect(n)

            @block.scalar
            def _(act):
                def gf_high(e, b):
                    wait_for(act, u_pe, 4 * (e - 1))
                    act.wait_ge(wg_in, 16 * (e + 1))
                    act.activation(wg[:, b, :, 0, :], raw_g[:], ACT.Copy, scale=W_S).then_inc(wgh, 1)
                    act.wait_ge(wf_in, 16 * (e + 1))
                    act.activation(wf[:, b, :, 0, :], raw_f[:], ACT.Copy, scale=W_S).then_inc(wgh, 1)

                def p_high(e):
                    wait_for(act, o_pe, J * e)
                    act.wait_ge(wp_in, 16 * (e + 1))
                    act.activation(wp[:, :, 0, :], raw_p[:], ACT.Copy, scale=W_S).then_inc(wph, 1)

                def rows_in(e, j):
                    act.wait_ge(x_pe, J * e + j + 1)
                    act.activation(xT[:].rearrange("p k h c -> p (k h) c")[:, :, P * j:P * (j + 1)],
                                   px[j % 2][:].rearrange("p (m c) -> p m c", c=P), ACT.Copy).then_inc(x_ev, 1)

                def gate_tanh(e, h):
                    act.wait_ge(u_pe, 4 * e + 2 * h + 1)
                    wait_for(act, h_rdy, 2 * e)
                    act.activation(th[:, h, :], pg[2 * h][:], ACT.Tanh, scale=0.5 / (XN_S * W_S)).then_inc(th_rdy, 1)

                def out_rows(e, j):
                    act.wait_ge(o_pe, J * e + j + 1)
                    wait_for(act, o_out[j], 16 * e)
                    act.activation(o_sb[:, j, :], po[j % 2][:], ACT.Copy, scale=1.0 / (H_S * W_S)).then_inc(o_ev, 1)

                act.wait_ge(d_rdy, 1)
                act.activation(tmp2[:, :, 1], tmp2[:, :, 0], ACT.Exp).then_inc(pe2, 1)
                gf_high(0, 0)
                rows_in(0, 0)
                rows_in(0, 2)

                def step(e, b, down, more):
                    if more:
                        gf_high(e + 1, 1 - b)
                    gate_tanh(e, 0)
                    gate_tanh(e, 1)
                    if more:
                        rows_in(e + 1, 0)
                        rows_in(e + 1, 2)
                    if down:
                        for j in range(J):
                            out_rows(e - 1, j)
                    p_high(e)

                step(0, 0, False, True)
                step(1, 1, True, True)
                with act.Fori(1, E // 2 - 1) as m:
                    for b in range(2):
                        step(2 * m + b, b, True, True)
                step(E - 2, 0, True, True)
                step(E - 1, 1, True, False)
                for j in range(J):
                    out_rows(E - 1, j)
                act.wait_ge(o_ev, J * E)

            @block.vector
            def _(dve):
                def gf_low(e, b):
                    for raw, w, n in ((raw_g, wg, 1), (raw_f, wf, 2)):
                        dve.wait_ge(wgh, 2 * e + n)
                        dve.scalar_tensor_tensor(out=w[:, b, :, 1, :], in0=raw[:], scalar=W_S, in1=w[:, b, :, 0, :],
                                                 op0=ALU.mult, op1=ALU.subtract).then_inc(wgl, 1)

                def p_low(e):
                    dve.wait_ge(wph, e + 1)
                    dve.scalar_tensor_tensor(out=wp[:, :, 1, :], in0=raw_p[:], scalar=W_S, in1=wp[:, :, 0, :],
                                             op0=ALU.mult, op1=ALU.subtract).then_inc(wpl, 1)

                def rows_in(e, j):
                    dve.wait_ge(x_pe, J * e + j + 1)
                    dve.tensor_copy(xT[:].rearrange("p k h c -> p (k h) c")[:, :, P * j:P * (j + 1)],
                                    px[j % 2][:].rearrange("p (m c) -> p m c", c=P)).then_inc(x_ev2, 1)

                def hidden(e, h, b):
                    dve.wait_ge(th_rdy, 2 * e + h + 1)
                    dve.scalar_tensor_tensor(out=gs[:, h, :], in0=th[:, h, :], scalar=1.0, in1=pg[2 * h][:],
                                             op0=ALU.add, op1=ALU.mult)
                    dve.drain()
                    dve.wait_ge(u_pe, 4 * e + 2 * h + 2)
                    dve.scalar_tensor_tensor(out=hf[:, h, :], in0=pg[2 * h + 1][:], scalar=0.5 * H_S / (XN_S * W_S) ** 2,
                                             in1=gs[:, h, :], op0=ALU.mult, op1=ALU.mult)
                    dve.drain()
                    wait_for(dve, o_pe, J * (e - 1))
                    dve.tensor_copy(hT[:, b, h, 0, :], hf[:, h, :])
                    dve.drain()
                    dve.tensor_tensor(hT[:, b, h, 1, :], hf[:, h, :], hT[:, b, h, 0, :], ALU.subtract).then_inc(h_rdy, 1)

                dve.wait_ge(e_const, 1)
                dve.tensor_tensor(cmp[:], rr[:], tot1[:].unsqueeze(2).to_broadcast([P, E, J]), ALU.is_ge)
                dve.wait_ge(tbl_pe, 1)
                lower = pg[0][:, 0:E * J].rearrange("p (e j) -> p e j", j=J)
                dve.tensor_copy(up_t[:], pg[0][:, E * J:2 * E * J])
                dve.drain()
                dve.tensor_tensor(grow[:], up_t[:].rearrange("p (e j) -> p e j", j=J), lower, ALU.subtract)
                dve.drain()
                dve.tensor_tensor(cmp[:], cmp[:], grow[:], ALU.mult)
                dve.drain()
                dve.tensor_tensor(gidx[:], cmp[:], lower, ALU.add).then_inc(grow_rdy, 1)
                dve.tensor_tensor(tmp2[:, :, 0], M12[:, :, 1], M12[:, :, 0], ALU.subtract).then_inc(d_rdy, 1)
                gf_low(0, 0)
                rows_in(0, 1)
                rows_in(0, 3)
                dve.tensor_scalar(ee[:], R12[:], -float(CAP), float(E * CAP), ALU.mult, ALU.add)
                dve.tensor_scalar(t1m[:], tot1[:], float(CAP - 1), None, ALU.min)
                dve.drain()
                dve.tensor_tensor(sel2[:], OH2[:], t1m[:].unsqueeze(1).to_broadcast([P, NT, E]), ALU.mult)
                dve.drain()
                dve.reduce_sum(tsel[:], sel2[:], AX_X)
                dve.scalar_tensor_tensor(out=crow[:, :, 0], in0=PP[:, :, 0], scalar=float(CAP - 1), in1=ee[:, :, 0],
                                         op0=ALU.min, op1=ALU.add)
                dve.tensor_scalar(crow[:, :, 1], PP[:, :, 1], -1.0, float(CAP - 1), ALU.mult, ALU.add)
                dve.drain()
                dve.tensor_tensor(crow[:, :, 1], crow[:, :, 1], tsel[:], ALU.max)
                dve.reciprocal(pw[:, :, 0], SE[:])
                dve.wait_ge(pe2, 1)
                dve.drain()
                dve.tensor_tensor(crow[:, :, 1], crow[:, :, 1], ee[:, :, 1], ALU.add)
                dve.tensor_tensor(pw[:, :, 1], tmp2[:, :, 1], pw[:, :, 0], ALU.mult)
                dve.drain()
                dve.tensor_copy(cidx[:], crow[:]).then_inc(crow_rdy, 1)

                def step(e, b, more):
                    if more:
                        gf_low(e + 1, 1 - b)
                    hidden(e, 0, b)
                    if more:
                        rows_in(e + 1, 1)
                    hidden(e, 1, b)
                    if more:
                        rows_in(e + 1, 3)
                    p_low(e)

                for b in range(2):
                    step(b, b, True)
                with dve.Fori(1, E // 2 - 1) as m:
                    for b in range(2):
                        step(2 * m + b, b, True)
                step(E - 2, 0, True)
                step(E - 1, 1, False)
                dve.wait_ge(x1_in, 64)

                with dve.Fori(0, NT // (PER * SETS)) as m:
                    for i in range(SETS):
                        n = SETS * m + i
                        dve.tensor_copy(cw[:, i, :], pw[:, bass.ds(PER * n, PER), :].rearrange("p n k -> p (n k)"))
                        dve.drain()
                        dve.wait_ge(c_in[i], 2 * PER * 16 * (m + 1))
                        for q in range(2):
                            for j in range(PER):
                                y = x1s[:, bass.ds(PER * n + j, 1), :].rearrange("p a d -> p (a d)")
                                last = dve.scalar_tensor_tensor(out=y, in0=got[:, i, 2 * j + q, :],
                                                                scalar=cw[:, i, 2 * j + q:2 * j + q + 1], in1=y,
                                                                op0=ALU.mult, op1=ALU.add)
                            if q == 0:
                                dve.drain()
                        last.then_inc(c_use, 1)

            @block.tensor
            def _(pe):
                def rows_T(e, j):
                    pe.wait_ge(g_in[j], 16 * (e + 1))
                    if j < 2:
                        wait_for(pe, x_ev if j % 2 == 0 else x_ev2, 2 * e)
                    else:
                        pe.wait_ge(x_ev if j % 2 == 0 else x_ev2, 2 * e + 1)
                    for k in range(KT):
                        for h in range(2):
                            m = 2 * k + h
                            last = pe.transpose(px[j % 2][:, m * P:(m + 1) * P],
                                                rows[:, j, h * D + k * P:h * D + (k + 1) * P], ident16[:])
                    last.then_inc(x_pe, 1)

                def up(e, u, b):
                    h, w = u // 2, (wg, wf)[u % 2]
                    if u == 0:
                        pe.wait_ge(x_ev, 2 * (e + 1))
                        pe.wait_ge(x_ev2, 2 * (e + 1))
                        pe.wait_ge(wgl, 2 * (e + 1))
                        wait_for(pe, h_rdy, 2 * e)
                    for k in range(KT):
                        last = three_passes(pe, pg[u][:],
                                            (w[:, b, k, 0, h * P:(h + 1) * P], w[:, b, k, 1, h * P:(h + 1) * P]),
                                            (xT[:, k, 0, :], xT[:, k, 1, :]), k == 0, k == KT - 1)
                    last.then_inc(u_pe, 1)

                def down(e, j, b):
                    if j == 0:
                        pe.wait_ge(h_rdy, 2 * (e + 1))
                        pe.wait_ge(wpl, e + 1)
                    wait_for(pe, o_ev, J * e + j - 1)
                    for k in range(HT):
                        last = three_passes(pe, po[j % 2][:],
                                            (hT[:, b, k, 0, j * P:(j + 1) * P], hT[:, b, k, 1, j * P:(j + 1) * P]),
                                            (wp[:, k, 0, :], wp[:, k, 1, :]), k == 0, k == HT - 1)
                    last.then_inc(o_pe, 1)

                def step(e, b, before, more):
                    for u in range(4):
                        up(e, u, b)
                    if more:
                        for j in range(J):
                            rows_T(e + 1, j)
                    if before:
                        for j in range(J):
                            down(e - 1, j, 1 - b)

                pe.wait_ge(tbl_in, 32)
                for h in range(2):
                    last = pe.transpose(pg[0][:, h * E * J:(h + 1) * E * J],
                                        tbl[:, h, :].rearrange("m (c w) -> m c w", w=TW)[:, :, 0], ident[0:E * J, 0:E * J])
                last.then_inc(tbl_pe, 1)
                for j in range(J):
                    rows_T(0, j)
                pe.wait_ge(grow_rdy, 1)
                step(0, 0, False, True)
                step(1, 1, True, True)
                with pe.Fori(1, E // 2 - 1) as m:
                    for b in range(2):
                        step(2 * m + b, b, True, True)
                step(E - 2, 0, True, True)
                step(E - 1, 1, True, False)
                for j in range(J):
                    down(E - 1, j, 1)


_INS = ["x", "ctx_1024", "L0_xattn_Wk", "L0_xattn_Wv", "L0_xattn_bv", "L0_xattn_Wq", "L0_xattn_bq", "L0_xattn_Wo",
        "L0_xattn_bo", "L0_ffn_w_router", "L0_ffn_w_fc", "L0_ffn_w_gate", "L0_ffn_w_proj"]


def kernel(**inputs):
    import numpy as _np
    import concourse.bacc as _bacc
    from concourse import mybir as _mybir
    from concourse.bass_utils import run_bass_kernel_spmd as _run

    nc = _bacc.Bacc("TRN2", target_bir_lowering=False, num_devices=1)
    arrays, args = {}, []
    for name in _INS:
        a = _np.ascontiguousarray(inputs[name])
        arrays[f"in_{name}_dram"] = a
        args.append(nc.dram_tensor(f"in_{name}_dram", a.shape, _mybir.dt.from_np(a.dtype), kind="ExternalInput").ap())
    out = nc.dram_tensor("out_0_dram", inputs["x"].shape, _mybir.dt.float32, kind="ExternalOutput").ap()
    build(nc, *args, out)
    r = _run(nc, [arrays], core_ids=[0])
    return r.results[0]["out_0_dram"]
```

```python
from contextlib import ExitStack

import concourse.bass as bass
from concourse import mybir

ALU = mybir.AluOpType
ACT = mybir.ActivationFunctionType
AX_X = mybir.AxisListType.X
F32, F16, BF16, I32 = mybir.dt.float32, mybir.dt.float16, mybir.dt.bfloat16, mybir.dt.int32

P = 128
EPS = 1e-5

XN_S = 2.0 ** 10
W_S = 2.0 ** 10
CTX_S = 2.0 ** 7
Q_S = 2.0 ** 7
PR_LN = 15
H_S = 2.0 ** 4
LN2 = 0.6931471805599453


def three_passes(pe, out, stationary, moving, first, last):
    s_hi, s_lo = stationary
    m_hi, m_lo = moving
    pe.matmul(out, s_hi, m_hi, start=first, stop=False)
    pe.matmul(out, s_hi, m_lo, start=False, stop=False)
    return pe.matmul(out, s_lo, m_hi, start=False, stop=last)


def build(nc, x, ctx_in, Wk, Wv, bv, Wq, bq, Wo, bo, w_router, w_fc, w_gate, w_proj, out):
    _, T, D = x.shape
    S = ctx_in.shape[1]
    E, _, H = w_fc.shape
    KT = D // P
    NT = T // P
    G4 = 4
    NG = NT // G4
    NK = S // P
    TAIL = S - NK * P
    CAP = 2 * T // E
    SM = float(D) ** -0.5
    assert D == 512 and 0 < TAIL <= 42 and CAP == 512 and NK == 3 * NG + 1 and H == 2 * P

    x_t = x.rearrange("a (n p) d -> (a n) p d", p=P)
    ctx2 = ctx_in.rearrange("a s d -> (a s) d")
    out_t = out.rearrange("a (n p) d -> (a n) p d", p=P)

    q_dram = nc.dram_tensor("q_dram", [NT, KT, P, 2 * P], F16, kind="Internal").ap()
    x1_dram = nc.dram_tensor("x1_dram", [NT, P, D], F32, kind="Internal").ap()
    rows_dram = nc.dram_tensor("rows_dram", [T, 2 * D], F16, kind="Internal").ap()
    TW = 16
    tbl_dram = nc.dram_tensor("tbl_dram", [2 * E * CAP, TW], F32, kind="Internal").ap()
    eo_dram = nc.dram_tensor("eo_dram", [E * CAP, D], F32, kind="Internal").ap()

    with ExitStack() as whole:
        def sem(name):
            return whole.enter_context(nc.semaphore(name))

        def sb(name, shape, dt, ctx=whole):
            return ctx.enter_context(nc.sbuf_tensor(name, shape, dt))

        ident = sb("ident", [P, P], F32)
        ident16 = sb("ident16", [P, P], F16)
        nhalf = sb("nhalf", [P, 1], F32)
        eps_c = sb("eps_c", [P, 1], F32)
        bo_row = sb("bo_row", [P, D], F32)
        R12 = sb("R12", [P, NT, 2], F32)
        PP = sb("PP", [P, NT, 2], F32)
        M12 = sb("M12", [P, NT, 2], F32)
        SE = sb("SE", [P, NT], F32)
        OH2 = sb("OH2", [P, NT, E], BF16)
        tot1 = sb("tot1", [P, E], F32)
        s_const = sem("s_const")

        with ExitStack() as attn:
            kT = sb("kT", [P, KT, 2, S], F16, attn)
            vv = sb("vv", [P, NK, 2, D], F16, attn)
            v_tail = sb("v_tail", [3 * TAIL, D], F16, attn)
            setup(nc, locals())
            attend(nc, locals())
        experts(nc, locals())
    return nc


def setup(nc, v):
    sb, sem = v["sb"], v["sem"]
    x_t, ctx2, q_dram, tbl_dram, TW = (v[n] for n in ("x_t", "ctx2", "q_dram", "tbl_dram", "TW"))
    Wk, Wv, bv, Wq, bq, Wo, bo = (v[n] for n in ("Wk", "Wv", "bv", "Wq", "bq", "Wo", "bo"))
    D, S, KT, NT, G4, NG, NK, TAIL, E, CAP = (v[n] for n in ("D", "S", "KT", "NT", "G4", "NG", "NK", "TAIL", "E", "CAP"))
    ident, ident16, nhalf, eps_c, bo_row, s_const = (v[n] for n in ("ident", "ident16", "nhalf", "eps_c", "bo_row", "s_const"))
    kT, vv, v_tail = v["kT"], v["vv"], v["v_tail"]
    with ExitStack() as c:
        x_raw = sb("x_raw", [P, G4, D], F32, c)
        xs = sb("xs", [P, G4, D], F32, c)
        c_raw = sb("c_raw", [P, 3, D], F32, c)
        xnT = sb("xnT", [P, 2, KT, 2, G4 * P], F16, c)
        q_f = sb("q_f", [P, 2, G4 * P], F32, c)
        q_st = sb("q_st", [P, 2, G4, 2, P], F16, c)
        m_w = sb("m_w", [P, KT, 2, D], F16, c)
        g_w = sb("g_w", [P, KT, 2, D], F16, c)
        w_a = sb("w_a", [P, KT, D], F32, c)
        w_b = sb("w_b", [P, KT, D], F32, c)
        w_c = sb("w_c", [P, KT, D], F32, c)
        woT = sb("woT", [P, KT, D], F32, c)
        bq_c = sb("bq_c", [P, KT], F32, c)
        bv_c = sb("bv_c", [P, KT], F32, c)
        bo_1 = sb("bo_1", [1, D], F32, c)
        ones = sb("ones", [P, P], F32, c)
        bv_b = q_f[:, 0, :].rearrange("p (k c) -> p k c", c=P)
        qb = sb("qb", [P, KT], F32, c)
        st6 = sb("st6", [P, 6], F32, c)
        mv = sb("mv", [P, 2], F32, c)
        var_e = sb("var_e", [P, 1], F32, c)
        rstd = sb("rstd", [P, 1], F32, c)
        ZW = E * CAP * TW // P // 4
        zrow = sb("zrow", [P, ZW], F32, c)
        tail_f = sb("tail_f", [TAIL, D], F32, c)
        tail_hi = sb("tail_hi", [TAIL, D], F16, c)
        tail_lo = sb("tail_lo", [TAIL, D], F16, c)
        bank = [c.enter_context(nc.psum_tensor(f"bank{i}", [P, 512], F32)) for i in range(8)]

        s_w = [sem(f"s_w{i}") for i in range(4)]
        s_b = sem("s_b")
        s_x = [sem(f"s_x{i}") for i in range(G4)]
        s_c = [sem(f"s_c{i}") for i in range(3)]
        s_tail = sem("s_tail")
        s_zero = sem("s_zero")
        s_zr = sem("s_zr")
        mv_ready = sem("mv_ready")
        ve_ready = sem("ve_ready")
        rstd_ready = sem("rstd_ready")
        xs_ready = sem("xs_ready")
        xT_pe = sem("xT_pe")
        xT_hi = sem("xT_hi")
        xT_lo = sem("xT_lo")
        c_pe = sem("c_pe")
        c_hi = sem("c_hi")
        c_lo = sem("c_lo")
        v_pe = sem("v_pe")
        v_hi = sem("v_hi")
        v_lo = sem("v_lo")
        mm_pe = sem("mm_pe")
        mm_hi = sem("mm_hi")
        mm_free = sem("mm_free")
        qb_pe = sem("qb_pe")
        qb_ready = sem("qb_ready")
        q_f_ready = sem("q_f_ready")
        q_hi = sem("q_hi")
        q_lo = sem("q_lo")
        q_out = [sem(f"q_out{i}") for i in range(2)]
        wo_pe = sem("wo_pe")
        wo_sb = sem("wo_sb")
        bvb = sem("bvb")
        bo_pe = sem("bo_pe")
        bo_done = sem("bo_done")
        tail_step = sem("tail_step")
        vt_pe = sem("vt_pe")
        kt_pe = sem("kt_pe")
        kt_hi, kt_lo = sem("kt_hi"), sem("kt_lo")
        s_vt = sem("s_vt")
        w_free = sem("w_free")

        with nc.Block() as block:
            @block.sync
            def _(sp):
                def load_x(n, k):
                    sp.dma_start(x_raw[:, k, :], x_t[n, :, :]).then_inc(s_x[k], 16)

                def load_c(n, j):
                    sp.dma_start(c_raw[:, j, :], ctx2[bass.ds(n * P, P), :]).then_inc(s_c[j], 16)

                sp.dma_start(w_b[:], Wo.rearrange("(k p) d -> p k d", p=P)).then_inc(s_w[0], 16)
                sp.dma_start(w_a[:], Wv.rearrange("(k p) d -> p k d", p=P)).then_inc(s_w[1], 16)
                for k in range(G4):
                    load_x(k, k)
                sp.dma_start(w_c[:], Wk.rearrange("(k p) d -> p k d", p=P)).then_inc(s_w[2], 16)
                sp.wait_ge(wo_pe, KT)
                sp.dma_start(w_b[:], Wq.rearrange("(k p) d -> p k d", p=P)).then_inc(s_w[3], 16)
                for j in range(3):
                    load_c(j, j)

                def store_q(g, k):
                    sp.wait_ge(q_hi, G4 * g + k + 1)
                    sp.wait_ge(q_lo, G4 * g + k + 1)
                    sp.dma_start(q_dram[bass.ds(g * G4, G4), k].rearrange("j p c -> p j c"),
                                 q_st[:, k % 2].rearrange("p j h c -> p j (h c)")).then_inc(q_out[k % 2], 16)

                for n in range(G4, 3 * G4):
                    sp.wait_ge(xs_ready, n - G4 + 1)
                    load_x(n, n % G4)
                def step(g, more_x, more_c):
                    for k in range(G4):
                        if more_c and k < 3:
                            sp.wait_ge(c_pe, 3 * g + k + 1)
                            load_c(3 * (g + 1) + k, k)
                        store_q(g, k)
                        if more_x:
                            sp.wait_ge(xs_ready, G4 * (g + 2) + k + 1)
                            load_x(G4 * (g + 3) + k, k)

                with sp.Fori(0, NG - 3) as g:
                    step(g, True, True)
                step(NG - 3, False, True)
                step(NG - 2, False, True)
                sp.wait_ge(c_pe, 3 * (NG - 1) + 1)
                load_c(NK - 1, 0)
                step(NG - 1, False, False)
                for i in range(2):
                    sp.wait_ge(q_out[i], 16 * NG * 2)

            @block.gpsimd
            def _(pool):
                pool.memset(ident[:], 0.0).then_inc(s_const, 1)
                pool.memset(nhalf[:], -0.5).then_inc(s_const, 1)
                pool.memset(eps_c[:], EPS).then_inc(s_const, 1)
                pool.memset(ones[:], 1.0).then_inc(s_const, 1)
                pool.memset(zrow[:], 0.0).then_inc(s_zr, 1)
                pool.wait_ge(s_const, 4)
                pool.affine_select(out=ident[:], in_=ident[:], compare_op=ALU.not_equal, fill=1.0, base=0,
                                   pattern=[[-1, P]], channel_multiplier=1).then_inc(s_const, 1)
                pool.wait_ge(s_const, 5)
                pool.tensor_copy(ident16[:], ident[:]).then_inc(s_const, 1)

                def deviation(n):
                    pool.wait_ge(mv_ready, n + 1)
                    pool.tensor_tensor(var_e[:], mv[:, 1:2], eps_c[:], ALU.add).then_inc(ve_ready, 1)
                    pool.wait_ge(ve_ready, n + 1)
                    pool.tensor_tensor(rstd[:], var_e[:], nhalf[:], ALU.pow).then_inc(rstd_ready, 1)

                def q_low(g, k):
                    pool.wait_ge(q_hi, G4 * g + k + 1)
                    pool.tensor_tensor(q_st[:, k % 2, :, 1, :], q_f[:, k % 2].rearrange("p (j c) -> p j c", c=P),
                                       q_st[:, k % 2, :, 0, :], ALU.subtract).then_inc(q_lo, 1)

                for n in range(2 * G4):
                    deviation(n)

                def step(g, more_x):
                    for k in range(G4):
                        if more_x:
                            deviation(G4 * (g + 2) + k)
                        q_low(g, k)

                with pool.Fori(0, NG - 2) as g:
                    step(g, True)
                step(NG - 2, False)
                step(NG - 1, False)

            @block.scalar
            def _(act):
                act.dma_start(bq_c[:], bq.rearrange("(k p) -> p k", p=P), allow_slow_non_contiguous=True).then_inc(s_b, 16)
                act.dma_start(bv_c[:], bv.rearrange("(k p) -> p k", p=P), allow_slow_non_contiguous=True).then_inc(s_b, 16)
                act.dma_start(bo_1[:], bo.rearrange("(a d) -> a d", a=1)).then_inc(s_b, 16)
                act.dma_start(tail_f[:], ctx2[NK * P:S, :]).then_inc(s_tail, 16)
                act.wait_ge(s_zr, 1)
                n_zero = P * ZW // TW
                for h in range(8):
                    act.dma_start(tbl_dram[h * n_zero:(h + 1) * n_zero].rearrange("(p r) c -> p (r c)", p=P),
                                  zrow[:]).then_inc(s_zero, 16)

                def product_high(u, out):
                    act.wait_ge(mm_pe, u + 1)
                    act.activation(out, bank[4 + u % 2][:], ACT.Copy, scale=W_S).then_inc(mm_hi, 1)

                def xT_high(g, k, b):
                    act.wait_ge(xT_pe, G4 * g + k + 1)
                    act.activation(xnT[:, b, :, 0, k * P:(k + 1) * P],
                                   bank[k % 2][:].rearrange("p (t c) -> p t c", c=P), ACT.Copy,
                                   scale=XN_S).then_inc(xT_hi, 1)

                def values_high(n, j):
                    act.wait_ge(v_pe, n + 1)
                    act.activation(vv[:, bass.ds(n, 1), 0, :].rearrange("p a d -> p (a d)"), bank[6 + j % 2][:],
                                   ACT.Copy, scale=1.0 / W_S).then_inc(v_hi, 1)

                def ctx_high(n, j):
                    act.wait_ge(c_pe, n + 1)
                    act.activation(kT[:, :, 0, bass.ds(n * P, P)],
                                   bank[2 + j % 2][:].rearrange("p (t c) -> p t c", c=P),
                                   ACT.Copy, scale=CTX_S).then_inc(c_hi, 1)

                def q_float(g, k):
                    act.wait_ge(mm_pe, 2 * KT + G4 * g + k + 1)
                    if k >= 2 or not isinstance(g, int) or g > 0:
                        act.wait_ge(q_lo, G4 * g + k - 1)
                    act.activation(q_f[:, k % 2], bank[4 + k % 2][:], ACT.Identity, bias=qb[:, k:k + 1],
                                   scale=Q_S / (XN_S * W_S)).then_inc(q_f_ready, 1)

                for u in range(KT):
                    act.wait_ge(wo_pe, u + 1)
                    act.activation(woT[:, u, :], bank[2 + u % 2][:], ACT.Copy).then_inc(wo_sb, 1)
                for u in range(KT):
                    product_high(u, g_w[:, u, 0, :])
                for k in range(G4):
                    xT_high(0, k, 0)
                act.wait_ge(bo_pe, 1)
                act.activation(bo_row[:], bank[6][:], ACT.Copy).then_inc(bo_done, 1)
                for u in range(KT):
                    product_high(KT + u, m_w[:, u, 0, :])
                act.wait_ge(kt_pe, 1)
                act.activation(kT[:, :, 0, NK * P:S], bank[3][:, 0:KT * TAIL].rearrange("p (t c) -> p t c", c=TAIL),
                               ACT.Copy, scale=CTX_S).then_inc(kt_hi, 1)
                act.wait_ge(vt_pe, 1)
                act.activation(tail_hi[:], bank[7][0:TAIL, :], ACT.Copy, scale=1.0 / W_S).then_inc(tail_step, 1)
                act.wait_ge(tail_step, 2)
                for i, part in enumerate((tail_hi, tail_hi, tail_lo)):
                    act.dma_start(v_tail[TAIL * i:TAIL * (i + 1), :], part[:]).then_inc(s_vt, 16)
                act.wait_ge(qb_ready, 1)

                def step(g, b, more):
                    for k in range(G4):
                        if more:
                            xT_high(g + 1, k, 1 - b)
                        if k < 3:
                            ctx_high(3 * g + k, k)
                        elif not more:
                            ctx_high(NK - 1, 0)
                        if k > 0:
                            values_high(3 * g + k - 1, k - 1)
                        q_float(g, k)

                step(0, 0, True)
                with act.Fori(1, NG - 1, 2) as g:
                    step(g, 1, True)
                    step(g + 1, 0, True)
                step(NG - 1, 1, False)
                values_high(NK - 1, 0)
                act.wait_ge(s_vt, 48)
                act.wait_ge(s_zero, 16 * 8)
                act.wait_ge(bo_done, 1)

            @block.vector
            def _(dve):
                def stats(n, k, s_load):
                    dve.wait_ge(s_x[k], s_load)
                    dve.bn_stats(st6[:], x_raw[:, k, :])
                    dve.drain()
                    dve.bn_aggr(mv[:], st6[:]).then_inc(mv_ready, 1)

                def normed(n, k):
                    dve.wait_ge(rstd_ready, n + 1)
                    dve.tensor_scalar(xs[:, k, :], x_raw[:, k, :], mv[:, 0:1], rstd[:],
                                      ALU.subtract, ALU.mult).then_inc(xs_ready, 1)

                def xT_low(g, k, b):
                    dve.wait_ge(xT_hi, G4 * g + k + 1)
                    dve.scalar_tensor_tensor(out=xnT[:, b, :, 1, k * P:(k + 1) * P],
                                             in0=bank[k % 2][:].rearrange("p (t c) -> p t c", c=P), scalar=XN_S,
                                             in1=xnT[:, b, :, 0, k * P:(k + 1) * P],
                                             op0=ALU.mult, op1=ALU.subtract).then_inc(xT_lo, 1)

                def values_low(n, j):
                    dve.wait_ge(v_hi, n + 1)
                    dve.scalar_tensor_tensor(out=vv[:, bass.ds(n, 1), 1, :].rearrange("p a d -> p (a d)"),
                                             in0=bank[6 + j % 2][:], scalar=1.0 / W_S,
                                             in1=vv[:, bass.ds(n, 1), 0, :].rearrange("p a d -> p (a d)"),
                                             op0=ALU.mult, op1=ALU.subtract).then_inc(v_lo, 1)

                def ctx_low(n, j):
                    dve.wait_ge(c_hi, n + 1)
                    dve.scalar_tensor_tensor(out=kT[:, :, 1, bass.ds(n * P, P)],
                                             in0=bank[2 + j % 2][:].rearrange("p (t c) -> p t c", c=P), scalar=CTX_S,
                                             in1=kT[:, :, 0, bass.ds(n * P, P)],
                                             op0=ALU.mult, op1=ALU.subtract).then_inc(c_lo, 1)

                def q_high(g, k):
                    wait_for(dve, q_out[k % 2], 16 * (2 * g + k // 2))
                    dve.wait_ge(q_f_ready, G4 * g + k + 1)
                    dve.tensor_copy(q_st[:, k % 2, :, 0, :],
                                    q_f[:, k % 2].rearrange("p (j c) -> p j c", c=P)).then_inc(q_hi, 1)

                def product_low(u, out, hi, n_hi):
                    dve.wait_ge(mm_hi, n_hi)
                    dve.scalar_tensor_tensor(out=out, in0=bank[4 + u % 2][:], scalar=W_S, in1=hi,
                                             op0=ALU.mult, op1=ALU.subtract).then_inc(mm_free, 1)

                for k in range(G4):
                    stats(k, k, 16)
                    normed(k, k)
                dve.wait_ge(s_b, 48)
                for k in range(KT):
                    dve.tensor_scalar(bv_b[:, k, :], ones[:], bv_c[:, k:k + 1], None, ALU.mult).then_inc(bvb, 1)
                for u in range(KT):
                    product_low(u, g_w[:, u, 1, :], g_w[:, u, 0, :], u + 1)
                for k in range(G4):
                    xT_low(0, k, 0)
                for k in range(G4):
                    stats(G4 + k, k, 32)
                    normed(G4 + k, k)
                for u in range(KT):
                    product_low(u, m_w[:, u, 1, :], m_w[:, u, 0, :], KT + u + 1)
                dve.wait_ge(qb_pe, 1)
                dve.tensor_scalar(qb[:], bank[7][:, 0:KT], Q_S, None, ALU.mult).then_inc(qb_ready, 1)
                dve.wait_ge(kt_hi, 1)
                dve.scalar_tensor_tensor(out=kT[:, :, 1, NK * P:S],
                                         in0=bank[3][:, 0:KT * TAIL].rearrange("p (t c) -> p t c", c=TAIL),
                                         scalar=CTX_S, in1=kT[:, :, 0, NK * P:S],
                                         op0=ALU.mult, op1=ALU.subtract).then_inc(kt_lo, 1)
                dve.wait_ge(tail_step, 1)
                dve.scalar_tensor_tensor(out=tail_lo[:], in0=bank[7][0:TAIL, :], scalar=1.0 / W_S, in1=tail_hi[:],
                                         op0=ALU.mult, op1=ALU.subtract).then_inc(tail_step, 1)

                def step(g, b, more, more_x):
                    for k in range(G4):
                        if more_x:
                            stats(G4 * (g + 2) + k, k, 16 * (g + 3))
                        if more:
                            xT_low(g + 1, k, 1 - b)
                        if k < 3:
                            ctx_low(3 * g + k, k)
                        elif not more:
                            ctx_low(NK - 1, 0)
                        if k > 0:
                            values_low(3 * g + k - 1, k - 1)
                        if more_x:
                            normed(G4 * (g + 2) + k, k)
                        q_high(g, k)

                step(0, 0, True, True)
                with dve.Fori(1, NG - 3, 2) as g:
                    step(g, 1, True, True)
                    step(g + 1, 0, True, True)
                step(NG - 3, 1, True, True)
                step(NG - 2, 0, True, False)
                step(NG - 1, 1, False, False)
                values_low(NK - 1, 0)

            @block.tensor
            def _(pe):
                def xT(g, k):
                    pe.wait_ge(xs_ready, G4 * g + k + 1)
                    if not isinstance(g, int) or G4 * g + k >= 2:
                        pe.wait_ge(xT_lo, G4 * g + k - 1)
                    for t in range(KT):
                        last = pe.transpose(bank[k % 2][:, t * P:(t + 1) * P], xs[:, k, t * P:(t + 1) * P], ident[:])
                    last.then_inc(xT_pe, 1)

                def cT(n, j, g1):
                    pe.wait_ge(s_c[j], 16 * g1)
                    wait_for(pe, c_lo, n if j == 0 else n - 1)
                    for t in range(KT):
                        last = pe.transpose(bank[2 + j % 2][:, t * P:(t + 1) * P], c_raw[:, j, t * P:(t + 1) * P], ident[:])
                    last.then_inc(c_pe, 1)

                def q_mm(g, k, b):
                    if k == 0:
                        pe.wait_ge(xT_lo, G4 * (g + 1))
                    if k >= 2 or not isinstance(g, int) or g > 0:
                        pe.wait_ge(q_f_ready, G4 * g + k - 1)
                    for t in range(KT):
                        last = three_passes(pe, bank[4 + k % 2][:],
                                            (m_w[:, t, 0, k * P:(k + 1) * P], m_w[:, t, 1, k * P:(k + 1) * P]),
                                            (xnT[:, b, t, 0, :], xnT[:, b, t, 1, :]), t == 0, t == KT - 1)
                    last.then_inc(mm_pe, 1)

                def times_g(out, n_rows, col, done):
                    for t in range(KT):
                        last = three_passes(pe, out, (kT[:, t, 0, bass.ds(col, n_rows)], kT[:, t, 1, bass.ds(col, n_rows)]),
                                            (g_w[:, t, 0, :], g_w[:, t, 1, :]), t == 0, t == KT - 1)
                    last.then_inc(done, 1)

                def values(n, j):
                    pe.wait_ge(c_lo, n + 1)
                    wait_for(pe, v_lo, n if j == 0 else n - 1)
                    if isinstance(n, int) and n == 1:
                        pe.wait_ge(tail_step, 2)
                    times_g(bank[6 + j % 2][:], P, n * P, v_pe)

                def weight_product(u, a, b, first):
                    wait_for(pe, mm_free, first + u - 1)
                    for t in range(KT):
                        last = pe.matmul(bank[4 + u % 2][:], a[:, t, u * P:(u + 1) * P], b[:, t, :],
                                         start=(t == 0), stop=(t == KT - 1))
                    last.then_inc(mm_pe, 1)

                pe.wait_ge(s_const, 5)
                pe.wait_ge(s_w[0], 16)
                for u in range(KT):
                    if u >= 2:
                        pe.wait_ge(wo_sb, u - 1)
                    for t in range(KT):
                        last = pe.transpose(bank[2 + u % 2][:, t * P:(t + 1) * P], w_b[:, t, u * P:(u + 1) * P], ident[:])
                    last.then_inc(wo_pe, 1)
                pe.wait_ge(s_w[1], 16)
                pe.wait_ge(wo_sb, KT)
                for u in range(KT):
                    weight_product(u, w_a, woT, 0)
                for k in range(G4):
                    xT(0, k)
                pe.wait_ge(s_b, 48)
                pe.wait_ge(bvb, KT)
                for t in range(KT):
                    pe.matmul(bank[6][:], bv_b[:, t, :], woT[:, t, :], start=(t == 0), stop=False)
                pe.matmul(bank[6][:], ones[0:1, :], bo_1[:], start=False, stop=True).then_inc(bo_pe, 1)
                pe.wait_ge(s_tail, 16)
                for t in range(KT):
                    last = pe.transpose(bank[3][:, t * TAIL:(t + 1) * TAIL], tail_f[:, t * P:(t + 1) * P],
                                        ident[0:TAIL, 0:TAIL])
                last.then_inc(kt_pe, 1)
                pe.wait_ge(s_w[2], 16)
                pe.wait_ge(s_w[3], 16)
                for u in range(KT):
                    weight_product(u, w_b, w_c, KT)
                for u in range(KT):
                    for t in range(KT):
                        last = pe.matmul(bank[7][:, u:u + 1], w_c[:, t, u * P:(u + 1) * P], bq_c[:, t:t + 1],
                                         start=(t == 0), stop=(t == KT - 1))
                last.then_inc(qb_pe, 1)
                pe.wait_ge(mm_free, 2 * KT)
                pe.wait_ge(bo_done, 1)
                pe.wait_ge(qb_ready, 1)
                pe.wait_ge(kt_lo, 1)
                times_g(bank[7][0:TAIL, :], TAIL, NK * P, vt_pe)

                def step(g, b, more):
                    for k in range(G4):
                        if more:
                            xT(g + 1, k)
                        if k < 3:
                            cT(3 * g + k, k, g + 1)
                        elif not more:
                            cT(NK - 1, 0, NG + 1)
                        if k > 0:
                            values(3 * g + k - 1, k - 1)
                        q_mm(g, k, b)

                step(0, 0, True)
                with pe.Fori(1, NG - 1, 2) as g:
                    step(g, 1, True)
                    step(g + 1, 0, True)
                step(NG - 1, 1, False)
                values(NK - 1, 0)


def wait_for(engine, semaphore, n):
    if not isinstance(n, int) or n > 0:
        engine.wait_ge(semaphore, n)


def attend(nc, v):
    sb, sem = v["sb"], v["sem"]
    x_t, q_dram, x1_dram, rows_dram, w_router = (v[n] for n in ("x_t", "q_dram", "x1_dram", "rows_dram", "w_router"))
    tbl_dram, TW = v["tbl_dram"], v["TW"]
    D, S, KT, NT, NK, TAIL, E, CAP, SM = (v[n] for n in ("D", "S", "KT", "NT", "NK", "TAIL", "E", "CAP", "SM"))
    ident, nhalf, eps_c, bo_row = (v[n] for n in ("ident", "nhalf", "eps_c", "bo_row"))
    kT, vv, v_tail = v["kT"], v["vv"], v["v_tail"]
    R12, PP, M12, SE, OH2, tot1 = (v[n] for n in ("R12", "PP", "M12", "SE", "OH2", "tot1"))
    NCH = -(-S // 512)
    width = [min(512, S - 512 * c) for c in range(NCH)]
    SKIP = float(1 << 20)
    with ExitStack() as c_:
        def buf(name, shape, dt):
            return sb(name, shape, dt, c_)

        qt = buf("qt", [P, KT, 2 * P], F16)
        s_sb = buf("s_sb", [P, S], F32)
        p_sb = buf("p_sb", [P, S], F32)
        p_hl = buf("p_hl", [P, 2, NK * P], F16)
        pT = buf("pT", [P, 2, NK, P], F16)
        mxc = buf("mxc", [P, NCH], F32)
        mx = buf("mx", [P, 1], F32)
        negb = buf("negb", [P, 1], F32)
        rsum = buf("rsum", [P, 1], F32)
        rs_v = buf("rs_v", [P, 1], F32)
        rinv = buf("rinv", [P, 1], F32)
        th16 = buf("th16", [P, TAIL], F16)
        tail3 = buf("tail3", [P, 3, TAIL], F32)
        tailT = buf("tailT", [3 * TAIL, P], F16)
        x_in = buf("x_in", [P, D], F32)
        xb = buf("xb", [P, D], F32)
        x1 = buf("x1", [P, D], F32)
        xs2 = buf("xs2", [P, D], F32)
        row16 = buf("row16", [P, 2 * D], F16)
        xT2 = buf("xT2", [P, KT, P], F32)
        st6 = buf("st6b", [P, 6], F32)
        mv = buf("mvb", [P, 2], F32)
        var_e = buf("var_eb", [P, 1], F32)
        rstd = buf("rstdb", [P, 1], F32)
        w_r = buf("w_r", [P, KT, E], F32)
        rev = buf("rev", [P, E], F32)
        lg = buf("lg", [P, E], F32)
        hit = buf("hit", [P, E], F32)
        lg2 = buf("lg2", [P, E], F32)
        m12 = buf("m12", [P, 2], F32)
        r12 = buf("r12", [P, 2], F32)
        negm = buf("negm", [P, 1], F32)
        rex = buf("rex", [P, E], F32)
        oh = buf("oh", [P, 2, E], BF16)
        acc_oh = buf("acc_oh", [P, 2, E], BF16)
        before = buf("before", [P, P], BF16)
        ones_b = buf("ones_b", [P, P], BF16)
        sel = buf("sel", [P, 2, E], F32)
        sg = buf("sg", [P, 2], F32)
        off = buf("off", [P, 2], F32)
        ia = buf("ia", [P, 2], F32)
        ib = buf("ib", [P, 2], F32)
        ic = buf("ic", [P, 2], F32)
        idf = buf("idf", [P, 2], F32)
        idx = buf("idx", [P, 2], I32)
        tok_all = buf("tok_all", [P, NT, TW], F32)
        tok = buf("tok", [P, TW], F32)
        sc = [c_.enter_context(nc.psum_tensor(f"sc{i}", [P, 512], F32)) for i in range(3)]
        ps_l = c_.enter_context(nc.psum_tensor("ps_l", [P, 512], F32))
        acc = c_.enter_context(nc.psum_tensor("acc", [P, 512], F32))
        ps_t = c_.enter_context(nc.psum_tensor("ps_t", [P, 512], F32))
        ps_m = c_.enter_context(nc.psum_tensor("ps_m", [P, 512], F32))

        a_const = sem("a_const")
        a_wr = sem("a_wr")
        q_in = sem("q_in")
        sc_pe = sem("sc_pe")
        sc_ev = sem("sc_ev")
        bias_rdy = sem("bias_rdy")
        exp_done = sem("exp_done")
        p_hi = sem("p_hi")
        p_lo = sem("p_lo")
        pT_in = sem("pT_in")
        rinv_rdy = sem("rinv_rdy")
        tail_rdy = sem("tail_rdy")
        tl_pe = sem("tl_pe")
        tl_rdy = sem("tl_rdy")
        pv_pe = sem("pv_pe")
        x_ld = sem("x_ld")
        xb_rdy = sem("xb_rdy")
        x1_rdy = sem("x1_rdy")
        x1_out = sem("x1_out")
        mv_rdy = sem("mv_rdy")
        ve_rdy = sem("ve_rdy")
        rs_rdy = sem("rs_rdy")
        xs_rdy = sem("xs_rdy")
        xs_hi = sem("xs_hi")
        xs_lo = sem("xs_lo")
        xT_pe2 = sem("xT_pe2")
        xT_ev = sem("xT_ev")
        lg_pe = sem("lg_pe")
        oh_rdy = sem("oh_rdy")
        rx_done = sem("rx_done")
        pos_pe = sem("pos_pe")
        idx_rdy = sem("idx_rdy")
        scat = sem("scat")
        r_out = sem("r_out")
        tot_pe = sem("tot_pe")
        tot_rdy = sem("tot_rdy")

        with nc.Block() as block:
            @block.sync
            def _(sp):
                def load_q(t):
                    sp.dma_start(qt[:], q_dram[bass.ds(t, 1)].rearrange("a k p c -> p (a k) c")).then_inc(q_in, 16)

                def load_x(t):
                    sp.dma_start(x_in[:], x_t[bass.ds(t, 1)].rearrange("a p c -> p (a c)")).then_inc(x_ld, 16)

                def store_x1(t):
                    sp.wait_ge(x1_rdy, t + 1)
                    sp.dma_start(x1_dram[bass.ds(t, 1)].rearrange("a p c -> p (a c)"), x1[:]).then_inc(x1_out, 16)

                def store_rows(t):
                    sp.wait_ge(xs_lo, t + 1)
                    sp.dma_start(rows_dram[bass.ds(P * t, P), :], row16[:]).then_inc(r_out, 16)

                load_q(0)
                sp.dma_start(w_r[:], w_router.rearrange("(k p) e -> p k e", p=P)).then_inc(a_wr, 16)
                load_x(0)
                sp.wait_ge(sc_pe, NCH)
                load_q(1)

                def transpose_p(t, more):
                    sp.wait_ge(p_hi, t + 1)
                    sp.wait_ge(p_lo, t + 1)
                    wait_for(sp, pv_pe, t)
                    if more:
                        sp.wait_ge(xb_rdy, t + 1)
                        load_x(t + 1)
                    for h in range(2):
                        sp.dma_start_transpose(pT[:, h], p_hl[:, h]).then_inc(pT_in, 16)

                def step(t, post, more):
                    transpose_p(t, True)
                    if post:
                        store_x1(t - 1)
                        store_rows(t - 1)
                    if more:
                        sp.wait_ge(sc_pe, NCH * (t + 2))
                        load_q(t + 2)

                step(0, False, True)
                step(1, True, True)
                with sp.Fori(2, NT - 2) as t:
                    step(t, True, True)
                step(NT - 2, True, False)
                transpose_p(NT - 1, False)
                for t in (NT - 2, NT - 1):
                    store_x1(t)
                    store_rows(t)
                sp.wait_ge(x1_out, 16 * NT)
                sp.wait_ge(r_out, 16 * NT)

            @block.gpsimd
            def _(pool):
                pool.memset(before[:], 1.0).then_inc(a_const, 1)
                pool.memset(ones_b[:], 1.0).then_inc(a_const, 1)
                pool.memset(acc_oh[:], 0.0).then_inc(a_const, 1)
                pool.memset(sg[:, 0:1], 1.0).then_inc(a_const, 1)
                pool.memset(sg[:, 1:2], -1.0).then_inc(a_const, 1)
                pool.memset(off[:, 0:1], float(E * CAP)).then_inc(a_const, 1)
                pool.memset(off[:, 1:2], float(2 * E * CAP + CAP - 1)).then_inc(a_const, 1)
                pool.iota(rev[:], [[-1, E]], base=E, channel_multiplier=0,
                          allow_small_or_imprecise_dtypes=True).then_inc(a_const, 1)
                pool.iota(tok_all[:], [[P, NT], [0, TW]], base=0, channel_multiplier=1,
                          allow_small_or_imprecise_dtypes=True).then_inc(a_const, 1)
                pool.wait_ge(a_const, 9)
                pool.affine_select(out=before[:], in_=before[:], compare_op=ALU.is_gt, fill=0.0, base=0,
                                   pattern=[[1, P]], channel_multiplier=-1).then_inc(a_const, 1)

                def add_bias(t):
                    pool.wait_ge(x_ld, 16 * (t + 1))
                    wait_for(pool, x1_rdy, t)
                    pool.tensor_tensor(xb[:], x_in[:], bo_row[:], ALU.add).then_inc(xb_rdy, 1)

                def deviation(t):
                    pool.wait_ge(mv_rdy, t + 1)
                    pool.tensor_tensor(var_e[:], mv[:, 1:2], eps_c[:], ALU.add).then_inc(ve_rdy, 1)
                    pool.wait_ge(ve_rdy, t + 1)
                    pool.tensor_tensor(rstd[:], var_e[:], nhalf[:], ALU.pow).then_inc(rs_rdy, 1)

                def scatter(t):
                    wait_for(pool, scat, 32 * t)
                    pool.wait_ge(idx_rdy, t + 1)
                    pool.tensor_tensor(idf[:], ia[:], ic[:], ALU.add)
                    pool.tensor_copy(tok[:], tok_all[:, bass.ds(t, 1), :].rearrange("p a w -> p (a w)"))
                    pool.drain()
                    pool.tensor_copy(idx[:], idf[:])
                    pool.drain()
                    for k in range(2):
                        pool.indirect_dma_start(tbl_dram, bass.IndirectOffsetOnAxis(ap=idx[:, k:k + 1], axis=0),
                                                tok[:], None, bounds_check=2 * E * CAP - 1,
                                                oob_is_err=False).then_inc(scat, 16)

                def step(t):
                    deviation(t - 1)
                    add_bias(t)
                    scatter(t - 1)

                add_bias(0)
                step(1)
                with pool.Fori(2, NT) as t:
                    step(t)
                deviation(NT - 1)
                scatter(NT - 1)
                pool.wait_ge(scat, 32 * NT)

            @block.scalar
            def _(act):
                def exponentials(t):
                    act.wait_ge(bias_rdy, t + 1)
                    if not isinstance(t, int) or t > 0:
                        act.wait_ge(p_lo, t)
                        act.wait_ge(tail_rdy, t)
                        act.wait_ge(rinv_rdy, t)
                    act.activation(p_sb[:], s_sb[:], ACT.Exp, bias=negb[:], scale=SM / (CTX_S * Q_S),
                                   accum_out=rsum[:]).then_inc(exp_done, 1)
                    wait_for(act, pT_in, 32 * t)
                    act.wait_ge(exp_done, t + 1)
                    act.activation(p_hl[:, 0, :], p_sb[:, 0:NK * P], ACT.Copy).then_inc(p_hi, 1)

                def rows_high(t):
                    act.wait_ge(xs_rdy, t + 1)
                    wait_for(act, r_out, 16 * t)
                    act.activation(row16[:, 0:D], xs2[:], ACT.Copy, scale=XN_S).then_inc(xs_hi, 1)

                def xT_copy(t):
                    act.wait_ge(xT_pe2, t + 1)
                    act.activation(xT2[:], ps_t[:].rearrange("p (j c) -> p j c", c=P), ACT.Copy).then_inc(xT_ev, 1)

                def router_sum(t):
                    act.wait_ge(oh_rdy, t + 1)
                    act.activation(rex[:], lg[:], ACT.Exp, bias=negm[:],
                                   accum_out=SE[:, bass.ds(t, 1)]).then_inc(rx_done, 1)

                def step(t, post, more):
                    if post:
                        rows_high(t - 1)
                        xT_copy(t - 1)
                    if more:
                        exponentials(t + 1)
                    if post:
                        router_sum(t - 1)

                exponentials(0)
                step(0, False, True)
                step(1, True, True)
                with act.Fori(2, NT - 1) as t:
                    step(t, True, True)
                step(NT - 1, True, False)
                rows_high(NT - 1)
                xT_copy(NT - 1)
                router_sum(NT - 1)
                act.wait_ge(rx_done, NT)

            @block.vector
            def _(dve):
                def evacuate(t, c):
                    dve.wait_ge(sc_pe, NCH * t + c + 1)
                    if c == 0:
                        wait_for(dve, exp_done, t)
                    dve.tensor_scalar(s_sb[:, 512 * c:512 * c + width[c]], sc[c % 3][:, 0:width[c]], 1.0, None,
                                      ALU.mult, ALU.max, accum_out=mxc[:, c:c + 1]).then_inc(sc_ev, 1)

                def bias(t):
                    dve.drain()
                    dve.reduce_max(mx[:], mxc[:], AX_X)
                    dve.drain()
                    dve.tensor_scalar(negb[:], mx[:], -SM / (CTX_S * Q_S), PR_LN * LN2,
                                      ALU.mult, ALU.add).then_inc(bias_rdy, 1)

                def low(t):
                    dve.wait_ge(exp_done, t + 1)
                    dve.tensor_copy(th16[:], p_sb[:, NK * P:S])
                    dve.drain()
                    wait_for(dve, tl_pe, t)
                    dve.tensor_copy(tail3[:, 0, :], th16[:])
                    dve.tensor_copy(tail3[:, 2, :], th16[:])
                    dve.tensor_tensor(tail3[:, 1, :], p_sb[:, NK * P:S], th16[:], ALU.subtract).then_inc(tail_rdy, 1)
                    dve.wait_ge(p_hi, t + 1)
                    dve.tensor_tensor(p_hl[:, 1, :], p_sb[:, 0:NK * P], p_hl[:, 0, :], ALU.subtract).then_inc(p_lo, 1)

                def inverse(t):
                    dve.wait_ge(exp_done, t + 1)
                    dve.tensor_scalar(rs_v[:], rsum[:], CTX_S, None, ALU.mult)
                    dve.drain()
                    dve.reciprocal(rinv[:], rs_v[:]).then_inc(rinv_rdy, 1)

                def tail_in(t):
                    dve.wait_ge(tl_pe, t + 1)
                    dve.tensor_copy(tailT[:], ps_l[0:3 * TAIL, 0:P]).then_inc(tl_rdy, 1)

                def residual(t):
                    dve.wait_ge(pv_pe, t + 1)
                    dve.wait_ge(xb_rdy, t + 1)
                    wait_for(dve, x1_out, 16 * t)
                    dve.scalar_tensor_tensor(out=x1[:], in0=acc[:], scalar=rinv[:], in1=xb[:],
                                             op0=ALU.mult, op1=ALU.add).then_inc(x1_rdy, 1)
                    dve.drain()
                    dve.bn_stats(st6[:], x1[:])
                    dve.drain()
                    dve.bn_aggr(mv[:], st6[:]).then_inc(mv_rdy, 1)

                def normed(t):
                    dve.wait_ge(rs_rdy, t + 1)
                    dve.tensor_scalar(xs2[:], x1[:], mv[:, 0:1], rstd[:], ALU.subtract, ALU.mult).then_inc(xs_rdy, 1)

                def rows_low(t):
                    dve.wait_ge(xs_hi, t + 1)
                    dve.scalar_tensor_tensor(out=row16[:, D:2 * D], in0=xs2[:], scalar=XN_S, in1=row16[:, 0:D],
                                             op0=ALU.mult, op1=ALU.subtract).then_inc(xs_lo, 1)

                def choose(k, logits):
                    dve.reduce_max(m12[:, k:k + 1], logits[:], AX_X)
                    dve.drain()
                    dve.scalar_tensor_tensor(out=hit[:], in0=logits[:], scalar=m12[:, k:k + 1], in1=rev[:],
                                             op0=ALU.is_equal, op1=ALU.mult)
                    dve.drain()
                    dve.reduce_max(r12[:, k:k + 1], hit[:], AX_X)
                    dve.drain()
                    return dve.tensor_scalar(oh[:, k, :], rev[:], r12[:, k:k + 1], None, ALU.is_equal)

                def route(t):
                    wait_for(dve, rx_done, t)
                    dve.wait_ge(lg_pe, t + 1)
                    dve.tensor_copy(lg[:], ps_m[:, 0:E])
                    dve.drain()
                    choose(0, lg)
                    dve.tensor_scalar(negm[:], m12[:, 0:1], -1.0, None, ALU.mult)
                    dve.drain()
                    dve.scalar_tensor_tensor(out=lg2[:], in0=oh[:, 0, :], scalar=-1e30, in1=lg[:],
                                             op0=ALU.mult, op1=ALU.add)
                    dve.drain()
                    choose(1, lg2).then_inc(oh_rdy, 1)
                    dve.tensor_copy(M12[:, bass.ds(t, 1), :].rearrange("p a k -> p (a k)"), m12[:])
                    dve.tensor_copy(R12[:, bass.ds(t, 1), :].rearrange("p a k -> p (a k)"), r12[:])

                def place(t):
                    dve.wait_ge(pos_pe, t + 1)
                    wait_for(dve, scat, 32 * t)
                    dve.tensor_tensor(sel[:], ps_m[:, 0:2 * E].rearrange("p (k e) -> p k e", k=2), oh[:], ALU.mult)
                    dve.tensor_tensor(acc_oh[:], acc_oh[:], oh[:], ALU.add)
                    dve.tensor_copy(OH2[:, bass.ds(t, 1), :].rearrange("p a e -> p (a e)"), oh[:, 1, :])
                    dve.scalar_tensor_tensor(out=ia[:], in0=r12[:], scalar=-float(CAP), in1=off[:],
                                             op0=ALU.mult, op1=ALU.add)
                    dve.drain()
                    dve.reduce_sum(ib[:], sel[:], AX_X)
                    dve.drain()
                    dve.tensor_copy(PP[:, bass.ds(t, 1), :].rearrange("p a k -> p (a k)"), ib[:])
                    dve.tensor_scalar(ic[:], ib[:], float(CAP), SKIP, ALU.is_ge, ALU.mult)
                    dve.tensor_tensor(ib[:], ib[:], sg[:], ALU.mult)
                    dve.drain()
                    dve.tensor_tensor(ia[:], ia[:], ib[:], ALU.add).then_inc(idx_rdy, 1)

                def step(t, post, more):
                    if post:
                        residual(t - 1)
                    inverse(t)
                    for c in range(NCH if more else 0):
                        evacuate(t + 1, c)
                        if c == 2:
                            if post:
                                normed(t - 1)
                                rows_low(t - 1)
                            tail_in(t)
                    if not more:
                        normed(t - 1)
                        rows_low(t - 1)
                        tail_in(t)
                    if more:
                        bias(t + 1)
                    if post:
                        route(t - 1)
                    if more:
                        low(t + 1)
                    if post:
                        place(t - 1)

                dve.wait_ge(a_const, 10)
                for c in range(NCH):
                    evacuate(0, c)
                bias(0)
                low(0)
                step(0, False, True)
                step(1, True, True)
                with dve.Fori(2, NT - 1) as t:
                    step(t, True, True)
                step(NT - 1, True, False)
                residual(NT - 1)
                normed(NT - 1)
                rows_low(NT - 1)
                route(NT - 1)
                place(NT - 1)
                dve.wait_ge(tot_pe, 1)
                dve.tensor_copy(tot1[:], ps_t[:, 0:E]).then_inc(tot_rdy, 1)

            @block.tensor
            def _(pe):
                def scores(t, c):
                    if c == 0:
                        pe.wait_ge(q_in, 16 * (t + 1))
                    wait_for(pe, sc_ev, NCH * t if c < 3 else NCH * t + c - 2)
                    for k in range(KT):
                        q_hi, q_lo = qt[:, k, 0:P], qt[:, k, P:2 * P]
                        lo, hi = 512 * c, 512 * c + width[c]
                        last = three_passes(pe, sc[c % 3][:, 0:width[c]], (q_hi, q_lo),
                                            (kT[:, k, 0, lo:hi], kT[:, k, 1, lo:hi]), k == 0, k == KT - 1)
                    last.then_inc(sc_pe, 1)

                def tail_T(t):
                    pe.wait_ge(tail_rdy, t + 1)
                    wait_for(pe, tl_rdy, t)
                    pe.transpose(ps_l[0:3 * TAIL, 0:P], tail3[:].rearrange("p a k -> p (a k)"), ident[:]).then_inc(tl_pe, 1)

                def times_values(t, post):
                    wait_for(pe, x1_rdy, t)
                    pe.wait_ge(pT_in, 32 * (t + 1))
                    for k in range(NK):
                        three_passes(pe, acc[:], (pT[:, 0, k, :], pT[:, 1, k, :]), (vv[:, k, 0, :], vv[:, k, 1, :]),
                                     k == 0, False)
                        if post and k == NK // 2:
                            places(t - 1)
                    pe.wait_ge(tl_rdy, t + 1)
                    pe.matmul(acc[:], tailT[:], v_tail[:], start=False, stop=True).then_inc(pv_pe, 1)

                def xT_pe_(t):
                    pe.wait_ge(xs_rdy, t + 1)
                    for k in range(KT):
                        last = pe.transpose(ps_t[:, k * P:(k + 1) * P], xs2[:, k * P:(k + 1) * P], ident[:])
                    last.then_inc(xT_pe2, 1)

                def logits(t):
                    pe.wait_ge(xT_ev, t + 1)
                    wait_for(pe, idx_rdy, t)
                    for k in range(KT):
                        last = pe.matmul(ps_m[:, 0:E], xT2[:, k, :], w_r[:, k, :], start=(k == 0), stop=(k == KT - 1))
                    last.then_inc(lg_pe, 1)

                def places(t):
                    pe.wait_ge(oh_rdy, t + 1)
                    pe.matmul(ps_m[:, 0:2 * E], before[:], oh[:].rearrange("p k e -> p (k e)"), start=True, stop=False)
                    pe.matmul(ps_m[:, 0:2 * E], ones_b[:], acc_oh[:].rearrange("p k e -> p (k e)"),
                              start=False, stop=True).then_inc(pos_pe, 1)

                def step(t, post, more):
                    for c in range(NCH if more else 0):
                        scores(t + 1, c)
                        if c == 1:
                            tail_T(t)
                        if c == 4 and post:
                            xT_pe_(t - 1)
                    if not more:
                        tail_T(t)
                        xT_pe_(t - 1)
                    if post:
                        logits(t - 1)
                    times_values(t, post)

                for c in range(NCH):
                    scores(0, c)
                pe.wait_ge(a_const, 10)
                pe.wait_ge(a_wr, 16)
                step(0, False, True)
                step(1, True, True)
                with pe.Fori(2, NT - 1) as t:
                    step(t, True, True)
                step(NT - 1, True, False)
                xT_pe_(NT - 1)
                logits(NT - 1)
                places(NT - 1)
                pe.wait_ge(idx_rdy, NT)
                pe.matmul(ps_t[:, 0:E], ones_b[:], acc_oh[:, 0, :], start=True, stop=True).then_inc(tot_pe, 1)


def experts(nc, v):
    sb, sem = v["sb"], v["sem"]
    w_fc, w_gate, w_proj, out_t = (v[n] for n in ("w_fc", "w_gate", "w_proj", "out_t"))
    x1_dram, rows_dram, eo_dram = (v[n] for n in ("x1_dram", "rows_dram", "eo_dram"))
    tbl_dram, TW, T, ident = v["tbl_dram"], v["TW"], v["T"], v["ident"]
    D, KT, NT, E, CAP, H = (v[n] for n in ("D", "KT", "NT", "E", "CAP", "H"))
    ident16 = v["ident16"]
    R12, PP, M12, SE, OH2, tot1 = (v[n] for n in ("R12", "PP", "M12", "SE", "OH2", "tot1"))
    J = CAP // P
    HT = H // P
    XT = NT // E
    SETS, PER = 4, 2
    with ExitStack() as c_:
        def buf(name, shape, dt):
            return sb(name, shape, dt, c_)

        x1s = buf("x1s", [P, NT, D], F32)
        crow = buf("crow", [P, NT, 2], F32)
        pw = buf("pw", [P, NT, 2], F32)
        ee = buf("ee", [P, NT, 2], F32)
        tmp2 = buf("tmp2", [P, NT, 2], F32)
        sel2 = buf("sel2", [P, NT, E], F32)
        t1m = buf("t1m", [P, E], F32)
        tsel = buf("tsel", [P, NT], F32)
        tbl = buf("tbl", [E * J, 2, P * TW], F32)
        up_t = buf("up_t", [P, E * J], F32)
        rr = buf("rr", [P, E, J], F32)
        cmp = buf("cmp", [P, E, J], F32)
        grow = buf("grow", [P, E, J], F32)
        gidx = buf("gidx", [P, E, J], I32)
        rows = buf("rows", [P, J, 2 * D], F16)
        xT = buf("xTe", [P, KT, 2, CAP], F16)
        raw_g = buf("raw_g", [P, KT, H], F32)
        raw_f = buf("raw_f", [P, KT, H], F32)
        raw_p = buf("raw_p", [P, HT, D], F32)
        wg = buf("wg", [P, 2, KT, 2, H], F16)
        wf = buf("wf", [P, 2, KT, 2, H], F16)
        wp = buf("wp", [P, 2, HT, 2, D], F16)
        th = buf("th", [P, HT, CAP], F32)
        gs = buf("gs", [P, HT, CAP], F32)
        hf = buf("hf", [P, HT, CAP], F32)
        hT = buf("hT", [P, 2, HT, 2, CAP], F16)
        o_sb = buf("o_sb", [P, J, D], F32)
        cidx = buf("cidx", [P, NT, 2], I32)
        cw = buf("cw", [P, SETS, PER * 2], F32)
        got = buf("got", [P, SETS, PER * 2, D], F32)
        pg = [c_.enter_context(nc.psum_tensor(f"pg{i}", [P, 512], F32)) for i in range(4)]
        px = [c_.enter_context(nc.psum_tensor(f"px{i}", [P, 1024], F16)) for i in range(2)]
        po = [c_.enter_context(nc.psum_tensor(f"po{i}", [P, 512], F32)) for i in range(2)]

        e_const = sem("e_const")
        tbl_in = sem("tbl_in")
        tbl_pe = sem("tbl_pe")
        grow_rdy = sem("grow_rdy")
        crow_rdy = sem("crow_rdy")
        pe2 = sem("pe2")
        d_rdy = sem("d_rdy")
        x1_in = sem("x1_in")
        gf_rdy = sem("gf_rdy")
        g_in = [sem(f"g_in{i}") for i in range(J)]
        wg_in, wf_in, wp_in = sem("wg_in"), sem("wf_in"), sem("wp_in")
        wgh, wgl = sem("wgh"), sem("wgl")
        wph, wpl = sem("wph"), sem("wpl")
        x_pe, x_ev = sem("x_pe"), sem("x_ev")
        x_ev2 = sem("x_ev2")
        u_pe = sem("u_pe")
        th_rdy = sem("th_rdy")
        h_rdy = sem("h_rdy")
        o_pe, o_ev = sem("o_pe"), sem("o_ev")
        o_out = [sem(f"o_out{i}") for i in range(J)]
        c_in = [sem(f"c_in{i}") for i in range(SETS)]
        c_use = sem("c_use")
        y_out = sem("y_out")

        with nc.Block() as block:
            @block.sync
            def _(sp):
                def load_gf(e):
                    sp.dma_start(raw_g[:], w_gate[bass.ds(e, 1)].rearrange("a (k p) h -> p (a k) h", p=P)).then_inc(wg_in, 16)
                    sp.dma_start(raw_f[:], w_fc[bass.ds(e, 1)].rearrange("a (k p) h -> p (a k) h", p=P)).then_inc(wf_in, 16)

                def load_p(e):
                    sp.dma_start(raw_p[:], w_proj[bass.ds(e, 1)].rearrange("a (k p) d -> p (a k) d", p=P)).then_inc(wp_in, 16)

                def store(e, j):
                    sp.wait_ge(o_ev, J * e + j + 1)
                    sp.dma_start(eo_dram[bass.ds(CAP * e + P * j, P), :], o_sb[:, j, :]).then_inc(o_out[j], 16)

                for h in range(2):
                    sp.dma_start(tbl[:, h, :], tbl_dram[h * E * CAP:(h + 1) * E * CAP].rearrange("(m c) w -> m (c w)", c=P))\
                      .then_inc(tbl_in, 16)
                load_gf(0)
                load_p(0)
                def load_x1(e):
                    sp.dma_start(x1s[:, bass.ds(XT * e, XT), :],
                                 x1_dram[bass.ds(XT * e, XT)].rearrange("n p d -> p n d")).then_inc(x1_in, 16)

                def step(e, before, more_gf, more_p):
                    if more_gf:
                        sp.wait_ge(wgl, 2 * (e + 2))
                        load_gf(e + 2)
                    if before:
                        for j in range(J):
                            store(e - 1, j)
                    if more_p:
                        sp.wait_ge(wpl, e + 1)
                        load_p(e + 1)
                    load_x1(e)

                sp.wait_ge(wgl, 2)
                load_gf(1)
                step(0, False, True, True)
                with sp.Fori(1, E - 2) as e:
                    step(e, True, True, True)
                step(E - 2, True, False, True)
                step(E - 1, True, False, False)
                for j in range(J):
                    store(E - 1, j)
                with sp.Fori(0, NT // PER) as n:
                    sp.wait_ge(c_use, n + 1)
                    sp.dma_start(out_t[bass.ds(PER * n, PER)].rearrange("n p d -> p n d"),
                                 x1s[:, bass.ds(PER * n, PER), :]).then_inc(y_out, 16)
                sp.wait_ge(y_out, 16 * (NT // PER))

            @block.gpsimd
            def _(pool):
                pool.iota(rr[:], [[0, E], [P, J]], base=0, channel_multiplier=1,
                          allow_small_or_imprecise_dtypes=True).then_inc(e_const, 1)

                def gather(e):
                    for j in range(J):
                        wait_for(pool, x_pe, J * (e - 1) + j + 1)
                        pool.indirect_dma_start(rows[:, j, :], None, rows_dram,
                                                bass.IndirectOffsetOnAxis(ap=gidx[:, e, j:j + 1], axis=0),
                                                bounds_check=T - 1, oob_is_err=False).then_inc(g_in[j], 16)

                def collect(n):
                    wait_for(pool, c_use, n - SETS + 1)
                    for j in range(PER):
                        for k in range(2):
                            pool.indirect_dma_start(got[:, n % SETS, 2 * j + k, :], None, eo_dram,
                                                    bass.IndirectOffsetOnAxis(ap=cidx[:, PER * n + j, k:k + 1], axis=0),
                                                    bounds_check=E * CAP - 1, oob_is_err=False).then_inc(c_in[n % SETS], 16)

                pool.wait_ge(grow_rdy, 1)
                for e in range(E):
                    gather(e)
                pool.wait_ge(crow_rdy, 1)
                for j in range(J):
                    pool.wait_ge(o_out[j], 16 * E)
                for n in range(NT // PER):
                    collect(n)

            @block.scalar
            def _(act):
                def gf_high(e, b):
                    wait_for(act, u_pe, 4 * (e - 1))
                    act.wait_ge(wg_in, 16 * (e + 1))
                    act.activation(wg[:, b, :, 0, :], raw_g[:], ACT.Copy, scale=W_S).then_inc(wgh, 1)
                    act.wait_ge(wf_in, 16 * (e + 1))
                    act.activation(wf[:, b, :, 0, :], raw_f[:], ACT.Copy, scale=W_S).then_inc(wgh, 1)

                def p_high(e, b):
                    wait_for(act, o_pe, J * (e - 1))
                    act.wait_ge(wp_in, 16 * (e + 1))
                    act.activation(wp[:, b, :, 0, :], raw_p[:], ACT.Copy, scale=W_S).then_inc(wph, 1)

                def rows_in(e, j):
                    act.wait_ge(x_pe, J * e + j + 1)
                    act.activation(xT[:].rearrange("p k h c -> p (k h) c")[:, :, P * j:P * (j + 1)],
                                   px[j % 2][:].rearrange("p (m c) -> p m c", c=P), ACT.Copy).then_inc(x_ev, 1)

                def gate_tanh(e, h):
                    act.wait_ge(u_pe, 4 * e + 2 * h + 1)
                    wait_for(act, h_rdy, 2 * e)
                    act.activation(th[:, h, :], pg[2 * h][:], ACT.Tanh, scale=0.5 / (XN_S * W_S)).then_inc(th_rdy, 1)

                def out_rows(e, j):
                    act.wait_ge(o_pe, J * e + j + 1)
                    wait_for(act, o_out[j], 16 * e)
                    act.activation(o_sb[:, j, :], po[j % 2][:], ACT.Copy, scale=1.0 / (H_S * W_S)).then_inc(o_ev, 1)

                act.wait_ge(d_rdy, 1)
                act.activation(tmp2[:, :, 1], tmp2[:, :, 0], ACT.Exp).then_inc(pe2, 1)
                gf_high(0, 0)
                rows_in(0, 0)
                rows_in(0, 2)

                def step(e, b, down, more):
                    if more:
                        gf_high(e + 1, 1 - b)
                    gate_tanh(e, 0)
                    gate_tanh(e, 1)
                    p_high(e, b)
                    for j in range(J):
                        if more and j < 2:
                            rows_in(e + 1, 2 * j)
                        if down:
                            out_rows(e - 1, j)

                step(0, 0, False, True)
                step(1, 1, True, True)
                with act.Fori(1, E // 2 - 1) as m:
                    for b in range(2):
                        step(2 * m + b, b, True, True)
                step(E - 2, 0, True, True)
                step(E - 1, 1, True, False)
                for j in range(J):
                    out_rows(E - 1, j)
                act.wait_ge(o_ev, J * E)

            @block.vector
            def _(dve):
                def gf_low(e, b):
                    for raw, w, n in ((raw_g, wg, 1), (raw_f, wf, 2)):
                        dve.wait_ge(wgh, 2 * e + n)
                        dve.scalar_tensor_tensor(out=w[:, b, :, 1, :], in0=raw[:], scalar=W_S, in1=w[:, b, :, 0, :],
                                                 op0=ALU.mult, op1=ALU.subtract).then_inc(wgl, 1)

                def p_low(e, b):
                    dve.wait_ge(wph, e + 1)
                    dve.scalar_tensor_tensor(out=wp[:, b, :, 1, :], in0=raw_p[:], scalar=W_S, in1=wp[:, b, :, 0, :],
                                             op0=ALU.mult, op1=ALU.subtract).then_inc(wpl, 1)

                def rows_in(e, j):
                    dve.wait_ge(x_pe, J * e + j + 1)
                    dve.tensor_copy(xT[:].rearrange("p k h c -> p (k h) c")[:, :, P * j:P * (j + 1)],
                                    px[j % 2][:].rearrange("p (m c) -> p m c", c=P)).then_inc(x_ev2, 1)

                def hidden(e, h, b):
                    dve.wait_ge(th_rdy, 2 * e + h + 1)
                    dve.scalar_tensor_tensor(out=gs[:, h, :], in0=th[:, h, :], scalar=1.0, in1=pg[2 * h][:],
                                             op0=ALU.add, op1=ALU.mult)
                    dve.drain()
                    dve.wait_ge(u_pe, 4 * e + 2 * h + 2)
                    dve.scalar_tensor_tensor(out=hf[:, h, :], in0=pg[2 * h + 1][:], scalar=0.5 * H_S / (XN_S * W_S) ** 2,
                                             in1=gs[:, h, :], op0=ALU.mult, op1=ALU.mult)
                    dve.drain()
                    wait_for(dve, o_pe, J * (e - 1))
                    dve.tensor_copy(hT[:, b, h, 0, :], hf[:, h, :])
                    dve.drain()
                    dve.tensor_tensor(hT[:, b, h, 1, :], hf[:, h, :], hT[:, b, h, 0, :], ALU.subtract).then_inc(h_rdy, 1)

                dve.wait_ge(e_const, 1)
                dve.tensor_tensor(cmp[:], rr[:], tot1[:].unsqueeze(2).to_broadcast([P, E, J]), ALU.is_ge)
                dve.wait_ge(tbl_pe, 1)
                lower = pg[0][:, 0:E * J].rearrange("p (e j) -> p e j", j=J)
                dve.tensor_copy(up_t[:], pg[0][:, E * J:2 * E * J])
                dve.drain()
                dve.tensor_tensor(grow[:], up_t[:].rearrange("p (e j) -> p e j", j=J), lower, ALU.subtract)
                dve.drain()
                dve.tensor_tensor(cmp[:], cmp[:], grow[:], ALU.mult)
                dve.drain()
                dve.tensor_tensor(gidx[:], cmp[:], lower, ALU.add).then_inc(grow_rdy, 1)
                dve.tensor_tensor(tmp2[:, :, 0], M12[:, :, 1], M12[:, :, 0], ALU.subtract).then_inc(d_rdy, 1)
                gf_low(0, 0)
                rows_in(0, 1)
                rows_in(0, 3)
                dve.tensor_scalar(ee[:], R12[:], -float(CAP), float(E * CAP), ALU.mult, ALU.add)
                dve.tensor_scalar(t1m[:], tot1[:], float(CAP - 1), None, ALU.min)
                dve.drain()
                dve.tensor_tensor(sel2[:], OH2[:], t1m[:].unsqueeze(1).to_broadcast([P, NT, E]), ALU.mult)
                dve.drain()
                dve.reduce_sum(tsel[:], sel2[:], AX_X)
                dve.scalar_tensor_tensor(out=crow[:, :, 0], in0=PP[:, :, 0], scalar=float(CAP - 1), in1=ee[:, :, 0],
                                         op0=ALU.min, op1=ALU.add)
                dve.tensor_scalar(crow[:, :, 1], PP[:, :, 1], -1.0, float(CAP - 1), ALU.mult, ALU.add)
                dve.drain()
                dve.tensor_tensor(crow[:, :, 1], crow[:, :, 1], tsel[:], ALU.max)
                dve.reciprocal(pw[:, :, 0], SE[:])
                dve.wait_ge(pe2, 1)
                dve.drain()
                dve.tensor_tensor(crow[:, :, 1], crow[:, :, 1], ee[:, :, 1], ALU.add)
                dve.tensor_tensor(pw[:, :, 1], tmp2[:, :, 1], pw[:, :, 0], ALU.mult)
                dve.drain()
                dve.tensor_copy(cidx[:], crow[:]).then_inc(crow_rdy, 1)

                def step(e, b, more):
                    if more:
                        gf_low(e + 1, 1 - b)
                    hidden(e, 0, b)
                    if more:
                        rows_in(e + 1, 1)
                    hidden(e, 1, b)
                    if more:
                        rows_in(e + 1, 3)
                    p_low(e, b)

                for b in range(2):
                    step(b, b, True)
                with dve.Fori(1, E // 2 - 1) as m:
                    for b in range(2):
                        step(2 * m + b, b, True)
                step(E - 2, 0, True)
                step(E - 1, 1, False)
                dve.wait_ge(x1_in, 16 * E)

                with dve.Fori(0, NT // (PER * SETS)) as m:
                    for i in range(SETS):
                        n = SETS * m + i
                        dve.tensor_copy(cw[:, i, :], pw[:, bass.ds(PER * n, PER), :].rearrange("p n k -> p (n k)"))
                        dve.drain()
                        dve.wait_ge(c_in[i], 2 * PER * 16 * (m + 1))
                        for q in range(2):
                            for j in range(PER):
                                y = x1s[:, bass.ds(PER * n + j, 1), :].rearrange("p a d -> p (a d)")
                                last = dve.scalar_tensor_tensor(out=y, in0=got[:, i, 2 * j + q, :],
                                                                scalar=cw[:, i, 2 * j + q:2 * j + q + 1], in1=y,
                                                                op0=ALU.mult, op1=ALU.add)
                            if q == 0:
                                dve.drain()
                        last.then_inc(c_use, 1)

            @block.tensor
            def _(pe):
                def rows_T(e, j):
                    pe.wait_ge(g_in[j], 16 * (e + 1))
                    if j < 2:
                        wait_for(pe, x_ev if j % 2 == 0 else x_ev2, 2 * e)
                    else:
                        pe.wait_ge(x_ev if j % 2 == 0 else x_ev2, 2 * e + 1)
                    for k in range(KT):
                        for h in range(2):
                            m = 2 * k + h
                            last = pe.transpose(px[j % 2][:, m * P:(m + 1) * P],
                                                rows[:, j, h * D + k * P:h * D + (k + 1) * P], ident16[:])
                    last.then_inc(x_pe, 1)

                def up(e, u, b):
                    h, w = u // 2, (wg, wf)[u % 2]
                    if u == 0:
                        pe.wait_ge(x_ev, 2 * (e + 1))
                        pe.wait_ge(x_ev2, 2 * (e + 1))
                        pe.wait_ge(wgl, 2 * (e + 1))
                        wait_for(pe, h_rdy, 2 * e)
                    for k in range(KT):
                        last = three_passes(pe, pg[u][:],
                                            (w[:, b, k, 0, h * P:(h + 1) * P], w[:, b, k, 1, h * P:(h + 1) * P]),
                                            (xT[:, k, 0, :], xT[:, k, 1, :]), k == 0, k == KT - 1)
                    last.then_inc(u_pe, 1)

                def down(e, j, b):
                    if j == 0:
                        pe.wait_ge(h_rdy, 2 * (e + 1))
                        pe.wait_ge(wpl, e + 1)
                    wait_for(pe, o_ev, J * e + j - 1)
                    for k in range(HT):
                        last = three_passes(pe, po[j % 2][:],
                                            (hT[:, b, k, 0, j * P:(j + 1) * P], hT[:, b, k, 1, j * P:(j + 1) * P]),
                                            (wp[:, b, k, 0, :], wp[:, b, k, 1, :]), k == 0, k == HT - 1)
                    last.then_inc(o_pe, 1)

                def step(e, b, before, more):
                    for u in range(4):
                        up(e, u, b)
                    for j in range(J):
                        if more and j < 2:
                            rows_T(e + 1, 2 * j)
                            rows_T(e + 1, 2 * j + 1)
                        if before:
                            down(e - 1, j, 1 - b)

                pe.wait_ge(tbl_in, 32)
                for h in range(2):
                    last = pe.transpose(pg[0][:, h * E * J:(h + 1) * E * J],
                                        tbl[:, h, :].rearrange("m (c w) -> m c w", w=TW)[:, :, 0], ident[0:E * J, 0:E * J])
                last.then_inc(tbl_pe, 1)
                for j in range(J):
                    rows_T(0, j)
                pe.wait_ge(grow_rdy, 1)
                step(0, 0, False, True)
                step(1, 1, True, True)
                with pe.Fori(1, E // 2 - 1) as m:
                    for b in range(2):
                        step(2 * m + b, b, True, True)
                step(E - 2, 0, True, True)
                step(E - 1, 1, True, False)
                for j in range(J):
                    down(E - 1, j, 1)


_INS = ["x", "ctx_1024", "L0_xattn_Wk", "L0_xattn_Wv", "L0_xattn_bv", "L0_xattn_Wq", "L0_xattn_bq", "L0_xattn_Wo",
        "L0_xattn_bo", "L0_ffn_w_router", "L0_ffn_w_fc", "L0_ffn_w_gate", "L0_ffn_w_proj"]


def kernel(**inputs):
    import numpy as _np
    import concourse.bacc as _bacc
    from concourse import mybir as _mybir
    from concourse.bass_utils import run_bass_kernel_spmd as _run

    nc = _bacc.Bacc("TRN2", target_bir_lowering=False, num_devices=1)
    arrays, args = {}, []
    for name in _INS:
        a = _np.ascontiguousarray(inputs[name])
        arrays[f"in_{name}_dram"] = a
        args.append(nc.dram_tensor(f"in_{name}_dram", a.shape, _mybir.dt.from_np(a.dtype), kind="ExternalInput").ap())
    out = nc.dram_tensor("out_0_dram", inputs["x"].shape, _mybir.dt.float32, kind="ExternalOutput").ap()
    build(nc, *args, out)
    r = _run(nc, [arrays], core_ids=[0])
    return r.results[0]["out_0_dram"]
```

```python
from contextlib import ExitStack

import concourse.bass as bass
from concourse import mybir

ALU = mybir.AluOpType
ACT = mybir.ActivationFunctionType
AX_X = mybir.AxisListType.X
F32, F16, BF16, I32 = mybir.dt.float32, mybir.dt.float16, mybir.dt.bfloat16, mybir.dt.int32

P = 128
EPS = 1e-5

XN_S = 2.0 ** 10
W_S = 2.0 ** 10
CTX_S = 2.0 ** 7
Q_S = 2.0 ** 7
PR_LN = 15
H_S = 2.0 ** 4
LN2 = 0.6931471805599453


def three_passes(pe, out, stationary, moving, first, last):
    s_hi, s_lo = stationary
    m_hi, m_lo = moving
    pe.matmul(out, s_hi, m_hi, start=first, stop=False)
    pe.matmul(out, s_hi, m_lo, start=False, stop=False)
    return pe.matmul(out, s_lo, m_hi, start=False, stop=last)


def build(nc, x, ctx_in, Wk, Wv, bv, Wq, bq, Wo, bo, w_router, w_fc, w_gate, w_proj, out):
    _, T, D = x.shape
    S = ctx_in.shape[1]
    E, _, H = w_fc.shape
    KT = D // P
    NT = T // P
    G4 = 4
    NG = NT // G4
    NK = S // P
    TAIL = S - NK * P
    CAP = 2 * T // E
    SM = float(D) ** -0.5
    assert D == 512 and 0 < TAIL <= 42 and CAP == 512 and NK == 3 * NG + 1 and H == 2 * P

    x_t = x.rearrange("a (n p) d -> (a n) p d", p=P)
    ctx2 = ctx_in.rearrange("a s d -> (a s) d")
    out_t = out.rearrange("a (n p) d -> (a n) p d", p=P)

    q_dram = nc.dram_tensor("q_dram", [NT, KT, P, 2 * P], F16, kind="Internal").ap()
    x1_dram = nc.dram_tensor("x1_dram", [NT, P, D], F32, kind="Internal").ap()
    rows_dram = nc.dram_tensor("rows_dram", [T, 2 * D], F16, kind="Internal").ap()
    TW = 16
    tbl_dram = nc.dram_tensor("tbl_dram", [2 * E * CAP, TW], F32, kind="Internal").ap()
    eo_dram = nc.dram_tensor("eo_dram", [E * CAP, D], F32, kind="Internal").ap()

    with ExitStack() as whole:
        def sem(name):
            return whole.enter_context(nc.semaphore(name))

        def sb(name, shape, dt, ctx=whole):
            return ctx.enter_context(nc.sbuf_tensor(name, shape, dt))

        ident = sb("ident", [P, P], F32)
        nhalf = sb("nhalf", [P, 1], F32)
        eps_c = sb("eps_c", [P, 1], F32)
        bo_row = sb("bo_row", [P, D], F32)
        R12 = sb("R12", [P, NT, 2], F32)
        PP = sb("PP", [P, NT, 2], F32)
        M12 = sb("M12", [P, NT, 2], F32)
        SE = sb("SE", [P, NT], F32)
        OH2 = sb("OH2", [P, NT, E], BF16)
        tot1 = sb("tot1", [P, E], F32)
        s_const = sem("s_const")

        with ExitStack() as attn:
            S_PAD = -(-S // 16) * 16
            kT = sb("kT", [P, 2 * KT, S_PAD], F16, attn)
            vv = sb("vv", [P, NK, 2, D], F16, attn)
            v_tail = sb("v_tail", [3 * TAIL, D], F16, attn)
            qt = sb("qt", [P, KT, 2 * P], F16, attn)
            q_in = sem("q_in")
            setup(nc, locals())
            attend(nc, locals())
        experts(nc, locals())
    return nc


def setup(nc, v):
    sb, sem = v["sb"], v["sem"]
    x_t, ctx2, q_dram, tbl_dram, TW = (v[n] for n in ("x_t", "ctx2", "q_dram", "tbl_dram", "TW"))
    Wk, Wv, bv, Wq, bq, Wo, bo = (v[n] for n in ("Wk", "Wv", "bv", "Wq", "bq", "Wo", "bo"))
    D, S, KT, G4, NG, NK, TAIL, E, CAP = (v[n] for n in ("D", "S", "KT", "G4", "NG", "NK", "TAIL", "E", "CAP"))
    ident, nhalf, eps_c, bo_row, s_const = (v[n] for n in ("ident", "nhalf", "eps_c", "bo_row", "s_const"))
    kT, vv, v_tail = v["kT"], v["vv"], v["v_tail"]
    qt, q_in = v["qt"], v["q_in"]
    with ExitStack() as c:
        x_raw = sb("x_raw", [P, G4, D], F32, c)
        xs = sb("xs", [P, 2, D], F32, c)
        x16 = sb("x16", [P, 2, 2 * D], F16, c)
        c16 = sb("c16", [P, 2, 2 * D], F16, c)
        xnT = sb("xnT", [P, 2, 2 * KT, G4 * P], F16, c)
        q_f = sb("q_f", [P, 2, G4 * P], F32, c)
        q_st = sb("q_st", [P, 2, G4, 2, P], F16, c)
        m_w = sb("m_w", [P, KT, 2, D], F16, c)
        g_w = sb("g_w", [P, KT, 2, D], F16, c)
        w_a = sb("w_a", [P, KT, D], F32, c)
        c_raw = w_a[:, 0:3, :]
        w_b = sb("w_b", [P, KT, D], F32, c)
        w_c = sb("w_c", [P, KT, D], F32, c)
        woT = sb("woT", [P, KT, D], F32, c)
        bq_c = sb("bq_c", [P, KT], F32, c)
        bv_c = sb("bv_c", [P, KT], F32, c)
        bo_1 = sb("bo_1", [1, D], F32, c)
        ones = sb("ones", [P, P], F32, c)
        bv_b = q_f[:, 0, :].rearrange("p (k c) -> p k c", c=P)
        qb = sb("qb", [P, KT], F32, c)
        st6 = sb("st6", [P, 6], F32, c)
        mv = sb("mv", [P, 2], F32, c)
        var_e = sb("var_e", [P, 1], F32, c)
        rstd = sb("rstd", [P, 1], F32, c)
        n_zero = 2 * E * CAP // 8
        zrow = sb("zrow", [P, n_zero * TW // P], F32, c)
        tail_f = sb("tail_f", [TAIL, D], F32, c)
        tail_hi = sb("tail_hi", [TAIL, D], F16, c)
        tail_lo = sb("tail_lo", [TAIL, D], F16, c)
        bank = [c.enter_context(nc.psum_tensor(f"bank{i}", [P, 512], F32)) for i in range(8)]

        q_bank = [bank[i] for i in (4, 5, 2, 3)]
        v_bank = [bank[i] for i in (0, 1, 6)]

        s_w = [sem(f"s_w{i}") for i in range(4)]
        s_b = sem("s_b")
        s_x = [sem(f"s_x{i}") for i in range(G4)]
        s_c = [sem(f"s_c{i}") for i in range(3)]
        s_tail = sem("s_tail")
        s_zero = sem("s_zero")
        s_zr = sem("s_zr")
        mv_ready = sem("mv_ready")
        ve_ready = sem("ve_ready")
        rstd_ready = sem("rstd_ready")
        xs_ready = sem("xs_ready")
        x_hi = sem("x_hi")
        x_lo = sem("x_lo")
        xT_in = [sem(f"xT_in{i}") for i in range(G4)]
        c_hi = sem("c_hi")
        c_lo = sem("c_lo")
        cT_in = [sem(f"cT_in{i}") for i in range(3)]
        v_pe = sem("v_pe")
        v_hi = sem("v_hi")
        v_lo = sem("v_lo")
        mm_pe = sem("mm_pe")
        mm_hi = sem("mm_hi")
        mm_free = sem("mm_free")
        qb_pe = sem("qb_pe")
        qb_ready = sem("qb_ready")
        q_f_ready = sem("q_f_ready")
        q_hi = sem("q_hi")
        q_lo = sem("q_lo")
        q_out = [sem(f"q_out{i}") for i in range(2)]
        wo_pe = sem("wo_pe")
        wo_sb = sem("wo_sb")
        bvb = sem("bvb")
        bo_pe = sem("bo_pe")
        bo_done = sem("bo_done")
        tail_step = sem("tail_step")
        vt_pe = sem("vt_pe")
        kt_pe = sem("kt_pe")
        kt_hi, kt_lo = sem("kt_hi"), sem("kt_lo")
        s_vt = sem("s_vt")

        with nc.Block() as block:
            @block.sync
            def _(sp):
                def load_x(n, k):
                    sp.dma_start(x_raw[:, k, :], x_t[n, :, :]).then_inc(s_x[k], 16)

                def load_c(n, j):
                    sp.dma_start(c_raw[:, j, :], ctx2[bass.ds(n * P, P), :]).then_inc(s_c[j], 16)

                sp.dma_start(w_b[:], Wo.rearrange("(k p) d -> p k d", p=P)).then_inc(s_w[0], 16)
                sp.dma_start(w_a[:], Wv.rearrange("(k p) d -> p k d", p=P)).then_inc(s_w[1], 16)
                for k in range(G4):
                    load_x(k, k)
                sp.dma_start(w_c[:], Wk.rearrange("(k p) d -> p k d", p=P)).then_inc(s_w[2], 16)

                def transpose_x(k, b):
                    sp.dma_start_transpose(xnT[:, b, :, k * P:(k + 1) * P], x16[:, k % 2]).then_inc(xT_in[k], 16)

                def transpose_c(n, j, slot):
                    sp.dma_start_transpose(kT[:, :, bass.ds(n * P, P)], c16[:, slot]).then_inc(cT_in[j], 16)

                def store_q(g, k):
                    sp.wait_ge(q_hi, G4 * g + k + 1)
                    sp.wait_ge(q_lo, G4 * g + k + 1)
                    sp.dma_start(q_dram[bass.ds(g * G4, G4), k].rearrange("j p c -> p j c"),
                                 q_st[:, k % 2].rearrange("p j h c -> p j (h c)")).then_inc(q_out[k % 2], 16)

                for k in range(G4):
                    if k == 2:
                        sp.wait_ge(wo_pe, KT)
                        sp.dma_start(w_b[:], Wq.rearrange("(k p) d -> p k d", p=P)).then_inc(s_w[3], 16)
                    sp.wait_ge(x_lo, k + 1)
                    load_x(G4 + k, k)
                    transpose_x(k, 0)
                sp.wait_ge(mm_pe, KT)
                for j in range(3):
                    load_c(j, j)

                def step(g, b, next_x, more_x, more_c):
                    for k in range(G4):
                        if k < 3:
                            sp.wait_ge(c_lo, 3 * g + k + 1)
                            if more_c:
                                load_c(3 * (g + 1) + k, k)
                            elif k == 0:
                                load_c(NK - 1, 0)
                            transpose_c(3 * g + k, k, (b + k) % 2)
                        elif not more_c:
                            sp.wait_ge(c_lo, NK)
                            transpose_c(NK - 1, 0, 0)
                        if k == 0 and (not isinstance(g, int) or g > 0):
                            store_q(g - 1, G4 - 1)
                        if next_x:
                            sp.wait_ge(x_lo, G4 * (g + 1) + k + 1)
                            if more_x:
                                load_x(G4 * (g + 2) + k, k)
                            transpose_x(k, 1 - b)
                        if k > 0:
                            store_q(g, k - 1)

                step(0, 0, True, True, True)
                with sp.Fori(1, NG - 3, 2) as g:
                    step(g, 1, True, True, True)
                    step(g + 1, 0, True, True, True)
                step(NG - 3, 1, True, True, True)
                step(NG - 2, 0, True, False, True)
                step(NG - 1, 1, False, False, False)
                store_q(NG - 1, G4 - 1)
                for i in range(2):
                    sp.wait_ge(q_out[i], 32)
                sp.dma_start(qt[:], q_dram[0].rearrange("k p c -> p k c")).then_inc(q_in, 16)
                for i in range(2):
                    sp.wait_ge(q_out[i], 16 * NG * 2)

            @block.gpsimd
            def _(pool):
                pool.memset(ident[:], 0.0).then_inc(s_const, 1)
                pool.memset(nhalf[:], -0.5).then_inc(s_const, 1)
                pool.memset(eps_c[:], EPS).then_inc(s_const, 1)
                pool.memset(ones[:], 1.0).then_inc(s_const, 1)
                pool.memset(zrow[:], 0.0).then_inc(s_zr, 1)
                pool.wait_ge(s_const, 4)
                pool.affine_select(out=ident[:], in_=ident[:], compare_op=ALU.not_equal, fill=1.0, base=0,
                                   pattern=[[-1, P]], channel_multiplier=1).then_inc(s_const, 1)

                def deviation(n):
                    pool.wait_ge(mv_ready, n + 1)
                    pool.tensor_tensor(var_e[:], mv[:, 1:2], eps_c[:], ALU.add).then_inc(ve_ready, 1)
                    pool.wait_ge(ve_ready, n + 1)
                    pool.tensor_tensor(rstd[:], var_e[:], nhalf[:], ALU.pow).then_inc(rstd_ready, 1)

                def q_low(g, k):
                    pool.wait_ge(q_hi, G4 * g + k + 1)
                    pool.tensor_tensor(q_st[:, k % 2, :, 1, :], q_f[:, k % 2].rearrange("p (j c) -> p j c", c=P),
                                       q_st[:, k % 2, :, 0, :], ALU.subtract).then_inc(q_lo, 1)

                for n in range(G4 + 1):
                    deviation(n)
                pool.wait_ge(s_zr, 1)
                for h in range(8):
                    pool.dma_start(tbl_dram[h * n_zero:(h + 1) * n_zero].rearrange("(p r) c -> p (r c)", p=P),
                                   zrow[:]).then_inc(s_zero, 16)

                def step(g, more_x, last_x):
                    for k in range(G4):
                        if more_x and not (last_x and k == G4 - 1):
                            deviation(G4 * (g + 1) + k + 1)
                        q_low(g, k)

                with pool.Fori(0, NG - 2) as g:
                    step(g, True, False)
                step(NG - 2, True, True)
                step(NG - 1, False, False)

            @block.scalar
            def _(act):
                act.dma_start(bq_c[:], bq.rearrange("(k p) -> p k", p=P), allow_slow_non_contiguous=True).then_inc(s_b, 16)
                act.dma_start(bv_c[:], bv.rearrange("(k p) -> p k", p=P), allow_slow_non_contiguous=True).then_inc(s_b, 16)
                act.dma_start(bo_1[:], bo.rearrange("(a d) -> a d", a=1)).then_inc(s_b, 16)
                act.dma_start(tail_f[:], ctx2[NK * P:S, :]).then_inc(s_tail, 16)

                def product_high(u, out):
                    act.wait_ge(mm_pe, u + 1)
                    act.activation(out, bank[4 + u % 2][:], ACT.Copy, scale=W_S).then_inc(mm_hi, 1)

                def x_high(g, k, slot):
                    act.wait_ge(xs_ready, G4 * g + k + 1)
                    wait_for(act, xT_in[(k + 2) % G4], 16 * (g + 1 if k >= 2 else g))
                    act.activation(x16[:, slot, 0:D], xs[:, slot, :], ACT.Copy, scale=XN_S).then_inc(x_hi, 1)

                def values_high(n, j):
                    act.wait_ge(v_pe, n + 1)
                    act.activation(vv[:, bass.ds(n, 1), 0, :].rearrange("p a d -> p (a d)"), v_bank[j][:],
                                   ACT.Copy, scale=1.0 / W_S).then_inc(v_hi, 1)

                def ctx_high(g, j, slot):
                    act.wait_ge(s_c[j], 16 * (g + 1))
                    wait_for(act, cT_in[(j + 1) % 3], 16 * (g + 1 if j == 2 else g))
                    act.activation(c16[:, slot, 0:D], c_raw[:, j, :], ACT.Copy, scale=CTX_S).then_inc(c_hi, 1)

                def q_float(g, k):
                    act.wait_ge(mm_pe, 2 * KT + G4 * g + k + 1)
                    if k >= 2 or not isinstance(g, int) or g > 0:
                        act.wait_ge(q_lo, G4 * g + k - 1)
                    act.activation(q_f[:, k % 2], q_bank[k][:], ACT.Identity, bias=qb[:, k:k + 1],
                                   scale=Q_S / (XN_S * W_S)).then_inc(q_f_ready, 1)

                for u in range(KT):
                    act.wait_ge(wo_pe, u + 1)
                    act.activation(woT[:, u, :], bank[2 + u % 2][:], ACT.Copy).then_inc(wo_sb, 1)
                for k in range(2):
                    x_high(0, k, k % 2)
                for u in range(KT):
                    product_high(u, g_w[:, u, 0, :])
                for k in range(2, G4):
                    x_high(0, k, k % 2)
                x_high(1, 0, 0)
                act.wait_ge(bo_pe, 1)
                act.activation(bo_row[:], bank[6][:], ACT.Copy).then_inc(bo_done, 1)
                for u in range(KT):
                    product_high(KT + u, m_w[:, u, 0, :])
                act.wait_ge(kt_pe, 1)
                act.activation(kT[:, 0:KT, NK * P:S], bank[3][:, 0:KT * TAIL].rearrange("p (t c) -> p t c", c=TAIL),
                               ACT.Copy, scale=CTX_S).then_inc(kt_hi, 1)
                ctx_high(0, 0, 0)
                act.wait_ge(vt_pe, 1)
                act.activation(tail_hi[:], bank[7][0:TAIL, :], ACT.Copy, scale=1.0 / W_S).then_inc(tail_step, 1)
                act.wait_ge(tail_step, 2)
                for i, part in enumerate((tail_hi, tail_hi, tail_lo)):
                    act.dma_start(v_tail[TAIL * i:TAIL * (i + 1), :], part[:]).then_inc(s_vt, 16)
                act.wait_ge(qb_ready, 1)

                def step(g, b, more_x, last_x):
                    for k in range(G4):
                        if k < 2:
                            ctx_high(g, k + 1, (b + k + 1) % 2)
                        elif k == 3:
                            ctx_high(g + 1, 0, 1 - b)
                        if more_x and not (last_x and k == G4 - 1):
                            x_high(g + 1 if k < G4 - 1 else g + 2, (k + 1) % G4, (k + 1) % 2)
                        q_float(g, k)
                        if k > 0:
                            values_high(3 * g + k - 1, k - 1)

                step(0, 0, True, False)
                with act.Fori(1, NG - 3, 2) as g:
                    step(g, 1, True, False)
                    step(g + 1, 0, True, False)
                step(NG - 3, 1, True, False)
                step(NG - 2, 0, True, True)
                step(NG - 1, 1, False, False)
                values_high(NK - 1, 0)
                act.wait_ge(s_vt, 48)
                act.wait_ge(s_zero, 16 * 8)
                act.wait_ge(bo_done, 1)

            @block.vector
            def _(dve):
                def stats(n, k, s_load):
                    dve.wait_ge(s_x[k], s_load)
                    dve.bn_stats(st6[:], x_raw[:, k, :])
                    dve.drain()
                    dve.bn_aggr(mv[:], st6[:]).then_inc(mv_ready, 1)

                def normed(n, k):
                    dve.wait_ge(rstd_ready, n + 1)
                    dve.tensor_scalar(xs[:, k % 2, :], x_raw[:, k, :], mv[:, 0:1], rstd[:],
                                      ALU.subtract, ALU.mult).then_inc(xs_ready, 1)

                def x_low(n, slot):
                    dve.wait_ge(x_hi, n + 1)
                    dve.scalar_tensor_tensor(out=x16[:, slot, D:2 * D], in0=xs[:, slot, :], scalar=XN_S,
                                             in1=x16[:, slot, 0:D], op0=ALU.mult, op1=ALU.subtract).then_inc(x_lo, 1)

                def values_low(n, j):
                    dve.wait_ge(v_hi, n + 1)
                    dve.scalar_tensor_tensor(out=vv[:, bass.ds(n, 1), 1, :].rearrange("p a d -> p (a d)"),
                                             in0=v_bank[j][:], scalar=1.0 / W_S,
                                             in1=vv[:, bass.ds(n, 1), 0, :].rearrange("p a d -> p (a d)"),
                                             op0=ALU.mult, op1=ALU.subtract).then_inc(v_lo, 1)

                def ctx_low(n, j, slot):
                    dve.wait_ge(c_hi, n + 1)
                    dve.scalar_tensor_tensor(out=c16[:, slot, D:2 * D], in0=c_raw[:, j, :], scalar=CTX_S,
                                             in1=c16[:, slot, 0:D], op0=ALU.mult, op1=ALU.subtract).then_inc(c_lo, 1)

                def q_high(g, k):
                    wait_for(dve, q_out[k % 2], 16 * (2 * g + k // 2))
                    dve.wait_ge(q_f_ready, G4 * g + k + 1)
                    dve.tensor_copy(q_st[:, k % 2, :, 0, :],
                                    q_f[:, k % 2].rearrange("p (j c) -> p j c", c=P)).then_inc(q_hi, 1)

                def product_low(u, out, hi, n_hi):
                    dve.wait_ge(mm_hi, n_hi)
                    dve.scalar_tensor_tensor(out=out, in0=bank[4 + u % 2][:], scalar=W_S, in1=hi,
                                             op0=ALU.mult, op1=ALU.subtract).then_inc(mm_free, 1)

                for k in range(2):
                    stats(k, k, 16)
                    normed(k, k)
                    x_low(k, k % 2)
                dve.wait_ge(s_b, 48)
                for k in range(KT):
                    dve.tensor_scalar(bv_b[:, k, :], ones[:], bv_c[:, k:k + 1], None, ALU.mult).then_inc(bvb, 1)
                for u in range(KT):
                    product_low(u, g_w[:, u, 1, :], g_w[:, u, 0, :], u + 1)
                for k in range(2, G4):
                    stats(k, k, 16)
                    normed(k, k)
                    x_low(k, k % 2)
                stats(G4, 0, 32)
                normed(G4, 0)
                x_low(G4, 0)
                for u in range(KT):
                    product_low(u, m_w[:, u, 1, :], m_w[:, u, 0, :], KT + u + 1)
                dve.wait_ge(qb_pe, 1)
                dve.tensor_scalar(qb[:], bank[7][:, 0:KT], Q_S, None, ALU.mult).then_inc(qb_ready, 1)
                dve.wait_ge(kt_hi, 1)
                dve.scalar_tensor_tensor(out=kT[:, KT:2 * KT, NK * P:S],
                                         in0=bank[3][:, 0:KT * TAIL].rearrange("p (t c) -> p t c", c=TAIL),
                                         scalar=CTX_S, in1=kT[:, 0:KT, NK * P:S],
                                         op0=ALU.mult, op1=ALU.subtract).then_inc(kt_lo, 1)
                ctx_low(0, 0, 0)
                dve.wait_ge(tail_step, 1)
                dve.scalar_tensor_tensor(out=tail_lo[:], in0=bank[7][0:TAIL, :], scalar=1.0 / W_S, in1=tail_hi[:],
                                         op0=ALU.mult, op1=ALU.subtract).then_inc(tail_step, 1)

                def step(g, b, more_x, last_x):
                    for k in range(G4):
                        tile = more_x and not (last_x and k == G4 - 1)
                        n, slot = G4 * (g + 1) + k + 1, (k + 1) % G4
                        if tile:
                            stats(n, slot, 16 * (g + 2 if k < G4 - 1 else g + 3))
                        if k != 2:
                            c = k + 1 if k < 2 else k
                            ctx_low(3 * g + c, c % 3, (b + c) % 2)
                        if tile:
                            normed(n, slot)
                            x_low(n, slot % 2)
                        q_high(g, k)
                        if k > 0:
                            values_low(3 * g + k - 1, k - 1)

                step(0, 0, True, False)
                with dve.Fori(1, NG - 3, 2) as g:
                    step(g, 1, True, False)
                    step(g + 1, 0, True, False)
                step(NG - 3, 1, True, False)
                step(NG - 2, 0, True, True)
                step(NG - 1, 1, False, False)
                values_low(NK - 1, 0)

            @block.tensor
            def _(pe):
                def q_mm(g, k, b):
                    if k == 0:
                        for i in range(G4):
                            pe.wait_ge(xT_in[i], 16 * (g + 1))
                    wait_for(pe, q_f_ready, G4 * (g - 1) + k + 1)
                    for t in range(KT):
                        last = three_passes(pe, q_bank[k][:],
                                            (m_w[:, t, 0, k * P:(k + 1) * P], m_w[:, t, 1, k * P:(k + 1) * P]),
                                            (xnT[:, b, t, :], xnT[:, b, KT + t, :]), t == 0, t == KT - 1)
                    last.then_inc(mm_pe, 1)

                def times_g(out, n_rows, col, done):
                    for t in range(KT):
                        last = three_passes(pe, out, (kT[:, t, bass.ds(col, n_rows)], kT[:, KT + t, bass.ds(col, n_rows)]),
                                            (g_w[:, t, 0, :], g_w[:, t, 1, :]), t == 0, t == KT - 1)
                    last.then_inc(done, 1)

                def values(n, j, g):
                    pe.wait_ge(cT_in[j], 16 * (g + 1))
                    wait_for(pe, v_lo, n - 2)
                    times_g(v_bank[j][:], P, n * P, v_pe)

                def weight_product(u, a, b, first):
                    wait_for(pe, mm_free, first + u - 1)
                    for t in range(KT):
                        last = pe.matmul(bank[4 + u % 2][:], a[:, t, u * P:(u + 1) * P], b[:, t, :],
                                         start=(t == 0), stop=(t == KT - 1))
                    last.then_inc(mm_pe, 1)

                pe.wait_ge(s_const, 5)
                pe.wait_ge(s_w[0], 16)
                for u in range(KT):
                    if u >= 2:
                        pe.wait_ge(wo_sb, u - 1)
                    for t in range(KT):
                        last = pe.transpose(bank[2 + u % 2][:, t * P:(t + 1) * P], w_b[:, t, u * P:(u + 1) * P], ident[:])
                    last.then_inc(wo_pe, 1)
                pe.wait_ge(s_w[1], 16)
                pe.wait_ge(wo_sb, KT)
                for u in range(KT):
                    weight_product(u, w_a, woT, 0)
                pe.wait_ge(s_b, 48)
                pe.wait_ge(bvb, KT)
                for t in range(KT):
                    pe.matmul(bank[6][:], bv_b[:, t, :], woT[:, t, :], start=(t == 0), stop=False)
                pe.matmul(bank[6][:], ones[0:1, :], bo_1[:], start=False, stop=True).then_inc(bo_pe, 1)
                pe.wait_ge(s_tail, 16)
                for t in range(KT):
                    last = pe.transpose(bank[3][:, t * TAIL:(t + 1) * TAIL], tail_f[:, t * P:(t + 1) * P],
                                        ident[0:TAIL, 0:TAIL])
                last.then_inc(kt_pe, 1)
                pe.wait_ge(s_w[2], 16)
                pe.wait_ge(s_w[3], 16)
                for u in range(KT):
                    weight_product(u, w_b, w_c, KT)
                for u in range(KT):
                    for t in range(KT):
                        last = pe.matmul(bank[7][:, u:u + 1], w_c[:, t, u * P:(u + 1) * P], bq_c[:, t:t + 1],
                                         start=(t == 0), stop=(t == KT - 1))
                last.then_inc(qb_pe, 1)
                pe.wait_ge(mm_free, 2 * KT)
                pe.wait_ge(bo_done, 1)
                pe.wait_ge(qb_ready, 1)
                pe.wait_ge(kt_lo, 1)
                times_g(bank[7][0:TAIL, :], TAIL, NK * P, vt_pe)

                def step(g, b):
                    for k in range(G4):
                        q_mm(g, k, b)
                        if k > 0:
                            values(3 * g + k - 1, k - 1, g)

                step(0, 0)
                with pe.Fori(1, NG - 1, 2) as g:
                    step(g, 1)
                    step(g + 1, 0)
                step(NG - 1, 1)
                values(NK - 1, 0, NG)


def wait_for(engine, semaphore, n):
    if not isinstance(n, int) or n > 0:
        engine.wait_ge(semaphore, n)


def attend(nc, v):
    sb, sem = v["sb"], v["sem"]
    x_t, q_dram, x1_dram, rows_dram, w_router = (v[n] for n in ("x_t", "q_dram", "x1_dram", "rows_dram", "w_router"))
    tbl_dram, TW = v["tbl_dram"], v["TW"]
    D, S, KT, NT, NK, TAIL, E, CAP, SM = (v[n] for n in ("D", "S", "KT", "NT", "NK", "TAIL", "E", "CAP", "SM"))
    ident, nhalf, eps_c, bo_row = (v[n] for n in ("ident", "nhalf", "eps_c", "bo_row"))
    kT, vv, v_tail = v["kT"], v["vv"], v["v_tail"]
    qt, q_in = v["qt"], v["q_in"]
    R12, PP, M12, SE, OH2, tot1 = (v[n] for n in ("R12", "PP", "M12", "SE", "OH2", "tot1"))
    NCH = -(-S // 512)
    width = [min(512, S - 512 * c) for c in range(NCH)]
    SKIP = float(1 << 20)
    with ExitStack() as c_:
        def buf(name, shape, dt):
            return sb(name, shape, dt, c_)

        s_sb = buf("s_sb", [P, S], F32)
        p_sb = buf("p_sb", [P, S], F32)
        p_hl = buf("p_hl", [P, 2, NK * P], F16)
        pT = buf("pT", [P, 2, NK, P], F16)
        pT_last = kT[:, 0:2, 0:NK * P].rearrange("p h (k c) -> p h k c", c=P)
        mxc = buf("mxc", [P, NCH], F32)
        mx = buf("mx", [P, 1], F32)
        negb = buf("negb", [P, 1], F32)
        rsum = buf("rsum", [P, 1], F32)
        rs_v = buf("rs_v", [P, 1], F32)
        rinv = buf("rinv", [P, 1], F32)
        th16 = buf("th16", [P, TAIL], F16)
        tail3 = buf("tail3", [P, 3, TAIL], F32)
        tailT = buf("tailT", [3 * TAIL, P], F16)
        x_in = buf("x_in", [P, D], F32)
        xb = buf("xb", [P, D], F32)
        x1 = buf("x1", [P, D], F32)
        xs2 = buf("xs2", [P, D], F32)
        row16 = buf("row16", [P, 2 * D], F16)
        xrT = buf("xrT", [P, 2 * KT, P], F16)
        w_r16 = buf("w_r16", [P, KT, 2, E], F16)
        st6 = buf("st6b", [P, 6], F32)
        mv = buf("mvb", [P, 2], F32)
        var_e = buf("var_eb", [P, 1], F32)
        rstd = buf("rstdb", [P, 1], F32)
        w_r = buf("w_r", [P, KT, E], F32)
        rev = buf("rev", [P, E], F32)
        lg = buf("lg", [P, E], F32)
        hit = buf("hit", [P, E], F32)
        lg2 = buf("lg2", [P, E], F32)
        m12 = buf("m12", [P, 2], F32)
        r12 = buf("r12", [P, 2], F32)
        negm = buf("negm", [P, 1], F32)
        rex = buf("rex", [P, E], F32)
        oh = buf("oh", [P, 2, E], BF16)
        acc_oh = buf("acc_oh", [P, 2, E], BF16)
        before = buf("before", [P, P], BF16)
        ones_b = buf("ones_b", [P, P], BF16)
        sel = buf("sel", [P, 2, E], F32)
        sg = buf("sg", [P, 2], F32)
        off = buf("off", [P, 2], F32)
        ia = buf("ia", [P, 2], F32)
        ib = buf("ib", [P, 2], F32)
        ic = buf("ic", [P, 2], F32)
        idf = buf("idf", [P, 2], F32)
        idx = buf("idx", [P, 2], I32)
        tok_all = buf("tok_all", [P, NT, TW], F32)
        tok = buf("tok", [P, TW], F32)
        sc = [c_.enter_context(nc.psum_tensor(f"sc{i}", [P, 512], F32)) for i in range(3)]
        ps_l = c_.enter_context(nc.psum_tensor("ps_l", [P, 512], F32))
        acc = c_.enter_context(nc.psum_tensor("acc", [P, 512], F32))
        ps_t = c_.enter_context(nc.psum_tensor("ps_t", [P, 512], F32))
        ps_m = c_.enter_context(nc.psum_tensor("ps_m", [P, 512], F32))

        a_const = sem("a_const")
        a_wr = sem("a_wr")
        sc_pe = sem("sc_pe")
        sc_ev = sem("sc_ev")
        bias_rdy = sem("bias_rdy")
        exp_done = sem("exp_done")
        p_hi = sem("p_hi")
        p_lo = sem("p_lo")
        pT_in = sem("pT_in")
        rinv_rdy = sem("rinv_rdy")
        tail_rdy = sem("tail_rdy")
        tl_pe = sem("tl_pe")
        tl_rdy = sem("tl_rdy")
        pv_pe = sem("pv_pe")
        x_ld = sem("x_ld")
        xb_rdy = sem("xb_rdy")
        x1_rdy = sem("x1_rdy")
        x1_out = sem("x1_out")
        mv_rdy = sem("mv_rdy")
        ve_rdy = sem("ve_rdy")
        rs_rdy = sem("rs_rdy")
        xs_rdy = sem("xs_rdy")
        xs_hi = sem("xs_hi")
        xs_lo = sem("xs_lo")
        xr_in = sem("xr_in")
        wr_hi = sem("wr_hi")
        wr_lo = sem("wr_lo")
        lg_pe = sem("lg_pe")
        oh_rdy = sem("oh_rdy")
        rx_done = sem("rx_done")
        pos_pe = sem("pos_pe")
        idx_rdy = sem("idx_rdy")
        scat = sem("scat")
        r_out = sem("r_out")
        tot_pe = sem("tot_pe")

        with nc.Block() as block:
            @block.sync
            def _(sp):
                def load_q(t):
                    sp.dma_start(qt[:], q_dram[bass.ds(t, 1)].rearrange("a k p c -> p (a k) c")).then_inc(q_in, 16)

                def load_x(t):
                    sp.dma_start(x_in[:], x_t[bass.ds(t, 1)].rearrange("a p c -> p (a c)")).then_inc(x_ld, 16)

                def store_x1(t):
                    sp.wait_ge(x1_rdy, t + 1)
                    sp.dma_start(x1_dram[bass.ds(t, 1)].rearrange("a p c -> p (a c)"), x1[:]).then_inc(x1_out, 16)

                def store_rows(t):
                    sp.wait_ge(xs_lo, t + 1)
                    wait_for(sp, lg_pe, t)
                    if isinstance(t, int):
                        sp.dma_start_transpose(xrT[:], row16[:]).then_inc(xr_in, 16)
                    sp.dma_start(rows_dram[bass.ds(P * t, P), :], row16[:]).then_inc(r_out, 16)
                    if not isinstance(t, int):
                        sp.dma_start_transpose(xrT[:], row16[:]).then_inc(xr_in, 16)

                sp.dma_start(w_r[:], w_router.rearrange("(k p) e -> p k e", p=P)).then_inc(a_wr, 16)
                load_x(0)
                sp.wait_ge(sc_pe, NCH)
                load_q(1)

                def transpose_p(t, more):
                    sp.wait_ge(p_hi, t + 1)
                    sp.wait_ge(p_lo, t + 1)
                    if more:
                        wait_for(sp, pv_pe, t)
                    else:
                        sp.wait_ge(sc_pe, NCH * NT)
                    if more:
                        sp.wait_ge(xb_rdy, t + 1)
                        load_x(t + 1)
                    for h in range(2):
                        sp.dma_start_transpose((pT if more else pT_last)[:, h], p_hl[:, h]).then_inc(pT_in, 16)

                def step(t, post, more):
                    transpose_p(t, True)
                    if post:
                        store_x1(t - 1)
                        store_rows(t - 1)
                    if more:
                        sp.wait_ge(sc_pe, NCH * (t + 2))
                        load_q(t + 2)

                step(0, False, True)
                step(1, True, True)
                with sp.Fori(2, NT - 2) as t:
                    step(t, True, True)
                step(NT - 2, True, False)
                transpose_p(NT - 1, False)
                for t in (NT - 2, NT - 1):
                    store_x1(t)
                    store_rows(t)
                sp.wait_ge(x1_out, 16 * NT)
                sp.wait_ge(r_out, 16 * NT)

            @block.gpsimd
            def _(pool):
                pool.memset(before[:], 1.0).then_inc(a_const, 1)
                pool.memset(ones_b[:], 1.0).then_inc(a_const, 1)
                pool.memset(acc_oh[:], 0.0).then_inc(a_const, 1)
                pool.memset(sg[:, 0:1], 1.0).then_inc(a_const, 1)
                pool.memset(sg[:, 1:2], -1.0).then_inc(a_const, 1)
                pool.memset(off[:, 0:1], float(E * CAP)).then_inc(a_const, 1)
                pool.memset(off[:, 1:2], float(2 * E * CAP + CAP - 1)).then_inc(a_const, 1)
                pool.iota(rev[:], [[-1, E]], base=E, channel_multiplier=0,
                          allow_small_or_imprecise_dtypes=True).then_inc(a_const, 1)
                pool.iota(tok_all[:], [[P, NT], [0, TW]], base=0, channel_multiplier=1,
                          allow_small_or_imprecise_dtypes=True).then_inc(a_const, 1)
                pool.wait_ge(a_const, 9)
                pool.affine_select(out=before[:], in_=before[:], compare_op=ALU.is_gt, fill=0.0, base=0,
                                   pattern=[[1, P]], channel_multiplier=-1).then_inc(a_const, 1)

                def add_bias(t):
                    pool.wait_ge(x_ld, 16 * (t + 1))
                    wait_for(pool, x1_rdy, t)
                    pool.tensor_tensor(xb[:], x_in[:], bo_row[:], ALU.add).then_inc(xb_rdy, 1)

                def deviation(t):
                    pool.wait_ge(mv_rdy, t + 1)
                    pool.tensor_tensor(var_e[:], mv[:, 1:2], eps_c[:], ALU.add).then_inc(ve_rdy, 1)
                    pool.wait_ge(ve_rdy, t + 1)
                    pool.tensor_tensor(rstd[:], var_e[:], nhalf[:], ALU.pow).then_inc(rs_rdy, 1)

                def scatter(t):
                    wait_for(pool, scat, 32 * t)
                    pool.wait_ge(idx_rdy, t + 1)
                    pool.tensor_tensor(idf[:], ia[:], ic[:], ALU.add)
                    pool.tensor_copy(tok[:], tok_all[:, bass.ds(t, 1), :].rearrange("p a w -> p (a w)"))
                    pool.drain()
                    pool.tensor_copy(idx[:], idf[:])
                    pool.drain()
                    for k in range(2):
                        pool.indirect_dma_start(tbl_dram, bass.IndirectOffsetOnAxis(ap=idx[:, k:k + 1], axis=0),
                                                tok[:], None, bounds_check=2 * E * CAP - 1,
                                                oob_is_err=False).then_inc(scat, 16)

                def step(t):
                    deviation(t - 1)
                    add_bias(t)
                    scatter(t - 1)

                add_bias(0)
                step(1)
                with pool.Fori(2, NT) as t:
                    step(t)
                deviation(NT - 1)
                scatter(NT - 1)
                pool.wait_ge(scat, 32 * NT)

            @block.scalar
            def _(act):
                def exponentials(t):
                    act.wait_ge(bias_rdy, t + 1)
                    if not isinstance(t, int) or t > 0:
                        act.wait_ge(p_lo, t)
                        act.wait_ge(tail_rdy, t)
                        act.wait_ge(rinv_rdy, t)
                    act.activation(p_sb[:], s_sb[:], ACT.Exp, bias=negb[:], scale=SM / (CTX_S * Q_S),
                                   accum_out=rsum[:]).then_inc(exp_done, 1)
                    wait_for(act, pT_in, 32 * t)
                    act.wait_ge(exp_done, t + 1)
                    act.activation(p_hl[:, 0, :], p_sb[:, 0:NK * P], ACT.Copy).then_inc(p_hi, 1)

                def rows_high(t):
                    act.wait_ge(xs_rdy, t + 1)
                    wait_for(act, r_out, 16 * t)
                    wait_for(act, xr_in, 16 * t)
                    act.activation(row16[:, 0:D], xs2[:], ACT.Copy, scale=XN_S).then_inc(xs_hi, 1)

                def router_sum(t):
                    act.wait_ge(oh_rdy, t + 1)
                    act.activation(rex[:], lg[:], ACT.Exp, bias=negm[:],
                                   accum_out=SE[:, bass.ds(t, 1)]).then_inc(rx_done, 1)

                def step(t, post, more):
                    if post:
                        rows_high(t - 1)
                    if more:
                        exponentials(t + 1)
                    if post:
                        router_sum(t - 1)

                act.wait_ge(a_wr, 16)
                act.activation(w_r16[:, :, 0, :], w_r[:], ACT.Copy, scale=W_S).then_inc(wr_hi, 1)
                exponentials(0)
                step(0, False, True)
                step(1, True, True)
                with act.Fori(2, NT - 1) as t:
                    step(t, True, True)
                step(NT - 1, True, False)
                rows_high(NT - 1)
                router_sum(NT - 1)
                act.wait_ge(rx_done, NT)

            @block.vector
            def _(dve):
                def evacuate(t, c):
                    dve.wait_ge(sc_pe, NCH * t + c + 1)
                    if c == 0:
                        wait_for(dve, exp_done, t)
                    dve.tensor_scalar(s_sb[:, 512 * c:512 * c + width[c]], sc[c % 3][:, 0:width[c]], 1.0, None,
                                      ALU.mult, ALU.max, accum_out=mxc[:, c:c + 1]).then_inc(sc_ev, 1)

                def bias(t):
                    dve.drain()
                    dve.reduce_max(mx[:], mxc[:], AX_X)
                    dve.drain()
                    dve.tensor_scalar(negb[:], mx[:], -SM / (CTX_S * Q_S), PR_LN * LN2,
                                      ALU.mult, ALU.add).then_inc(bias_rdy, 1)

                def low(t):
                    dve.wait_ge(exp_done, t + 1)
                    dve.tensor_copy(th16[:], p_sb[:, NK * P:S])
                    dve.drain()
                    wait_for(dve, tl_pe, t)
                    dve.tensor_copy(tail3[:, 0, :], th16[:])
                    dve.tensor_copy(tail3[:, 2, :], th16[:])
                    dve.tensor_tensor(tail3[:, 1, :], p_sb[:, NK * P:S], th16[:], ALU.subtract).then_inc(tail_rdy, 1)
                    dve.wait_ge(p_hi, t + 1)
                    dve.tensor_tensor(p_hl[:, 1, :], p_sb[:, 0:NK * P], p_hl[:, 0, :], ALU.subtract).then_inc(p_lo, 1)

                def inverse(t):
                    dve.wait_ge(exp_done, t + 1)
                    dve.tensor_scalar(rs_v[:], rsum[:], CTX_S, None, ALU.mult)
                    dve.drain()
                    dve.reciprocal(rinv[:], rs_v[:]).then_inc(rinv_rdy, 1)

                def tail_in(t):
                    dve.wait_ge(tl_pe, t + 1)
                    dve.tensor_copy(tailT[:], ps_l[0:3 * TAIL, 0:P]).then_inc(tl_rdy, 1)

                def residual(t):
                    dve.wait_ge(pv_pe, t + 1)
                    dve.wait_ge(xb_rdy, t + 1)
                    wait_for(dve, x1_out, 16 * t)
                    dve.scalar_tensor_tensor(out=x1[:], in0=acc[:], scalar=rinv[:], in1=xb[:],
                                             op0=ALU.mult, op1=ALU.add).then_inc(x1_rdy, 1)
                    dve.drain()
                    dve.bn_stats(st6[:], x1[:])
                    dve.drain()
                    dve.bn_aggr(mv[:], st6[:]).then_inc(mv_rdy, 1)

                def normed(t):
                    dve.wait_ge(rs_rdy, t + 1)
                    dve.tensor_scalar(xs2[:], x1[:], mv[:, 0:1], rstd[:], ALU.subtract, ALU.mult).then_inc(xs_rdy, 1)

                def rows_low(t):
                    dve.wait_ge(xs_hi, t + 1)
                    dve.scalar_tensor_tensor(out=row16[:, D:2 * D], in0=xs2[:], scalar=XN_S, in1=row16[:, 0:D],
                                             op0=ALU.mult, op1=ALU.subtract).then_inc(xs_lo, 1)

                def choose(k, logits):
                    dve.reduce_max(m12[:, k:k + 1], logits[:], AX_X)
                    dve.drain()
                    dve.scalar_tensor_tensor(out=hit[:], in0=logits[:], scalar=m12[:, k:k + 1], in1=rev[:],
                                             op0=ALU.is_equal, op1=ALU.mult)
                    dve.drain()
                    dve.reduce_max(r12[:, k:k + 1], hit[:], AX_X)
                    dve.drain()
                    return dve.tensor_scalar(oh[:, k, :], rev[:], r12[:, k:k + 1], None, ALU.is_equal)

                def route(t):
                    wait_for(dve, rx_done, t)
                    dve.wait_ge(lg_pe, t + 1)
                    dve.tensor_scalar(lg2[:], ps_m[:, 0:E], 1.0 / (XN_S * W_S), None, ALU.mult)
                    dve.drain()
                    dve.scalar_tensor_tensor(out=lg[:], in0=ps_m[:, E:2 * E], scalar=1.0 / (XN_S * W_S), in1=lg2[:],
                                             op0=ALU.mult, op1=ALU.add)
                    dve.drain()
                    choose(0, lg)
                    dve.tensor_scalar(negm[:], m12[:, 0:1], -1.0, None, ALU.mult)
                    dve.drain()
                    dve.scalar_tensor_tensor(out=lg2[:], in0=oh[:, 0, :], scalar=-1e30, in1=lg[:],
                                             op0=ALU.mult, op1=ALU.add)
                    dve.drain()
                    choose(1, lg2).then_inc(oh_rdy, 1)
                    dve.tensor_copy(M12[:, bass.ds(t, 1), :].rearrange("p a k -> p (a k)"), m12[:])
                    dve.tensor_copy(R12[:, bass.ds(t, 1), :].rearrange("p a k -> p (a k)"), r12[:])

                def place(t):
                    dve.wait_ge(pos_pe, t + 1)
                    wait_for(dve, scat, 32 * t)
                    dve.tensor_tensor(sel[:], ps_m[:, 0:2 * E].rearrange("p (k e) -> p k e", k=2), oh[:], ALU.mult)
                    dve.tensor_tensor(acc_oh[:], acc_oh[:], oh[:], ALU.add)
                    dve.tensor_copy(OH2[:, bass.ds(t, 1), :].rearrange("p a e -> p (a e)"), oh[:, 1, :])
                    dve.scalar_tensor_tensor(out=ia[:], in0=r12[:], scalar=-float(CAP), in1=off[:],
                                             op0=ALU.mult, op1=ALU.add)
                    dve.drain()
                    dve.reduce_sum(ib[:], sel[:], AX_X)
                    dve.drain()
                    dve.tensor_copy(PP[:, bass.ds(t, 1), :].rearrange("p a k -> p (a k)"), ib[:])
                    dve.tensor_scalar(ic[:], ib[:], float(CAP), SKIP, ALU.is_ge, ALU.mult)
                    dve.tensor_tensor(ib[:], ib[:], sg[:], ALU.mult)
                    dve.drain()
                    dve.tensor_tensor(ia[:], ia[:], ib[:], ALU.add).then_inc(idx_rdy, 1)

                def step(t, post, more):
                    if post:
                        residual(t - 1)
                    inverse(t)
                    for c in range(NCH if more else 0):
                        evacuate(t + 1, c)
                        if c == 2:
                            if post:
                                normed(t - 1)
                                rows_low(t - 1)
                            tail_in(t)
                    if not more:
                        normed(t - 1)
                        rows_low(t - 1)
                        tail_in(t)
                    if more:
                        bias(t + 1)
                    if post:
                        route(t - 1)
                    if more:
                        low(t + 1)
                    if post:
                        place(t - 1)

                dve.wait_ge(wr_hi, 1)
                dve.scalar_tensor_tensor(out=w_r16[:, :, 1, :], in0=w_r[:], scalar=W_S, in1=w_r16[:, :, 0, :],
                                         op0=ALU.mult, op1=ALU.subtract).then_inc(wr_lo, 1)
                dve.wait_ge(a_const, 10)
                for c in range(NCH):
                    evacuate(0, c)
                bias(0)
                low(0)
                step(0, False, True)
                step(1, True, True)
                with dve.Fori(2, NT - 1) as t:
                    step(t, True, True)
                step(NT - 1, True, False)
                residual(NT - 1)
                normed(NT - 1)
                rows_low(NT - 1)
                route(NT - 1)
                place(NT - 1)
                dve.wait_ge(tot_pe, 1)
                dve.tensor_copy(tot1[:], ps_t[:, 0:E])

            @block.tensor
            def _(pe):
                def scores(t, c):
                    if c == 0:
                        pe.wait_ge(q_in, 16 * (t + 1))
                    wait_for(pe, sc_ev, NCH * t if c < 3 else NCH * t + c - 2)
                    for k in range(KT):
                        q_hi, q_lo = qt[:, k, 0:P], qt[:, k, P:2 * P]
                        lo, hi = 512 * c, 512 * c + width[c]
                        last = three_passes(pe, sc[c % 3][:, 0:width[c]], (q_hi, q_lo),
                                            (kT[:, k, lo:hi], kT[:, KT + k, lo:hi]), k == 0, k == KT - 1)
                    last.then_inc(sc_pe, 1)

                def tail_T(t):
                    pe.wait_ge(tail_rdy, t + 1)
                    wait_for(pe, tl_rdy, t)
                    pe.transpose(ps_l[0:3 * TAIL, 0:P], tail3[:].rearrange("p a k -> p (a k)"), ident[:]).then_inc(tl_pe, 1)

                def times_values(t, post, more):
                    wait_for(pe, x1_rdy, t)
                    pe.wait_ge(pT_in, 32 * (t + 1))
                    p_t = pT if more else pT_last
                    for k in range(NK):
                        three_passes(pe, acc[:], (p_t[:, 0, k, :], p_t[:, 1, k, :]), (vv[:, k, 0, :], vv[:, k, 1, :]),
                                     k == 0, False)
                        if post and not more and k == NK // 3:
                            logits(t - 1)
                        if post and k == (NK // 2 if more else NK - 4):
                            places(t - 1)
                    pe.wait_ge(tl_rdy, t + 1)
                    pe.matmul(acc[:], tailT[:], v_tail[:], start=False, stop=True).then_inc(pv_pe, 1)

                def logits(t):
                    pe.wait_ge(xr_in, 16 * (t + 1))
                    wait_for(pe, idx_rdy, t)
                    for k in range(KT):
                        pe.matmul(ps_m[:, 0:2 * E], xrT[:, k, :], w_r16[:, k].rearrange("p h e -> p (h e)"),
                                  start=(k == 0), stop=False)
                    for k in range(KT):
                        last = pe.matmul(ps_m[:, 0:E], xrT[:, KT + k, :], w_r16[:, k, 0, :],
                                         start=False, stop=(k == KT - 1))
                    last.then_inc(lg_pe, 1)

                def places(t):
                    pe.wait_ge(oh_rdy, t + 1)
                    pe.matmul(ps_m[:, 0:2 * E], before[:], oh[:].rearrange("p k e -> p (k e)"), start=True, stop=False)
                    pe.matmul(ps_m[:, 0:2 * E], ones_b[:], acc_oh[:].rearrange("p k e -> p (k e)"),
                              start=False, stop=True).then_inc(pos_pe, 1)

                def step(t, post, more):
                    for c in range(NCH if more else 0):
                        scores(t + 1, c)
                        if c == 1:
                            tail_T(t)
                    if not more:
                        tail_T(t)
                    if post and more:
                        logits(t - 1)
                    times_values(t, post, more)

                for c in range(NCH):
                    scores(0, c)
                pe.wait_ge(a_const, 10)
                pe.wait_ge(wr_lo, 1)
                step(0, False, True)
                step(1, True, True)
                with pe.Fori(2, NT - 1) as t:
                    step(t, True, True)
                step(NT - 1, True, False)
                logits(NT - 1)
                places(NT - 1)
                pe.wait_ge(idx_rdy, NT)
                pe.matmul(ps_t[:, 0:E], ones_b[:], acc_oh[:, 0, :], start=True, stop=True).then_inc(tot_pe, 1)


def experts(nc, v):
    sb, sem = v["sb"], v["sem"]
    w_fc, w_gate, w_proj, out_t = (v[n] for n in ("w_fc", "w_gate", "w_proj", "out_t"))
    x1_dram, rows_dram, eo_dram = (v[n] for n in ("x1_dram", "rows_dram", "eo_dram"))
    tbl_dram, TW, T, ident = v["tbl_dram"], v["TW"], v["T"], v["ident"]
    D, KT, NT, E, CAP, H = (v[n] for n in ("D", "KT", "NT", "E", "CAP", "H"))
    R12, PP, M12, SE, OH2, tot1 = (v[n] for n in ("R12", "PP", "M12", "SE", "OH2", "tot1"))
    J = CAP // P
    HT = H // P
    XT = NT // E
    SETS, PER = 4, 2
    with ExitStack() as c_:
        def buf(name, shape, dt):
            return sb(name, shape, dt, c_)

        x1s = buf("x1s", [P, NT, D], F32)
        crow = buf("crow", [P, NT, 2], F32)
        pw = buf("pw", [P, NT, 2], F32)
        ee = buf("ee", [P, NT, 2], F32)
        tmp2 = buf("tmp2", [P, NT, 2], F32)
        sel2 = buf("sel2", [P, NT, E], F32)
        t1m = buf("t1m", [P, E], F32)
        tsel = buf("tsel", [P, NT], F32)
        up_t = buf("up_t", [P, E * J], F32)
        rr = buf("rr", [P, E, J], F32)
        cmp = buf("cmp", [P, E, J], F32)
        grow = buf("grow", [P, E, J], F32)
        gidx = buf("gidx", [P, E, J], I32)
        rows = buf("rows", [P, 2, J * 2 * D], F16)
        xT = buf("xTe", [P, 2, J, 2, KT, P], F16)
        raw_g = buf("raw_g", [P, KT, H], F32)
        raw_f = buf("raw_f", [P, KT, H], F32)
        raw_p = buf("raw_p", [P, HT, D], F32)
        wg = buf("wg", [P, 2, KT, 2, H], F16)
        wf = buf("wf", [P, 2, KT, 2, H], F16)
        wp = buf("wp", [P, 2, HT, 2, D], F16)
        th = buf("th", [P, HT, CAP], F32)
        hf = buf("hf", [P, HT, CAP], F32)
        hT = buf("hT", [P, 2, HT, 2, CAP], F16)
        o_sb = buf("o_sb", [P, J, D], F32)
        cidx = buf("cidx", [P, NT, 2], I32)
        cw = buf("cw", [P, SETS, PER * 2], F32)
        got = buf("got", [P, SETS, PER * 2, D], F32)
        assert PER * 2 * D == P * TW
        tbl = got[0:E * J, 0:2].rearrange("m h a d -> m h (a d)")
        pg = [c_.enter_context(nc.psum_tensor(f"pg{i}", [P, 512], F32)) for i in range(4)]
        po = [c_.enter_context(nc.psum_tensor(f"po{i}", [P, 512], F32)) for i in range(4)]

        e_const = sem("e_const")
        tbl_in = sem("tbl_in")
        tbl_pe = sem("tbl_pe")
        grow_rdy = sem("grow_rdy")
        crow_rdy = sem("crow_rdy")
        pe2 = sem("pe2")
        d_rdy = sem("d_rdy")
        x1_in = sem("x1_in")
        g0_in = [sem(f"g0_in{i}") for i in range(J)]
        g_in = [sem(f"g_in{i}") for i in range(2)]
        wg_in, wf_in, wp_in = sem("wg_in"), sem("wf_in"), sem("wp_in")
        wgh, wgl = sem("wgh"), sem("wgl")
        wph, wpl = sem("wph"), sem("wpl")
        x0_in = sem("x0_in")
        x_in = [sem(f"x_in{i}") for i in range(2)]
        u_pe = sem("u_pe")
        th_rdy = sem("th_rdy")
        h_rdy = sem("h_rdy")
        o_pe, o_ev = sem("o_pe"), sem("o_ev")
        o_out = [sem(f"o_out{i}") for i in range(J)]
        c_in = [sem(f"c_in{i}") for i in range(SETS)]
        c_use = sem("c_use")
        y_out = sem("y_out")

        with nc.Block() as block:
            @block.sync
            def _(sp):
                def load_gf(e):
                    sp.dma_start(raw_g[:], w_gate[bass.ds(e, 1)].rearrange("a (k p) h -> p (a k) h", p=P)).then_inc(wg_in, 16)
                    sp.dma_start(raw_f[:], w_fc[bass.ds(e, 1)].rearrange("a (k p) h -> p (a k) h", p=P)).then_inc(wf_in, 16)

                def load_p(e):
                    sp.dma_start(raw_p[:], w_proj[bass.ds(e, 1)].rearrange("a (k p) d -> p (a k) d", p=P)).then_inc(wp_in, 16)

                def store(e, j):
                    sp.wait_ge(o_ev, J * e + j + 1)
                    sp.dma_start(eo_dram[bass.ds(CAP * e + P * j, P), :], o_sb[:, j, :]).then_inc(o_out[j], 16)

                for h in range(2):
                    sp.dma_start(tbl[:, h, :], tbl_dram[h * E * CAP:(h + 1) * E * CAP].rearrange("(m c) w -> m (c w)", c=P))\
                      .then_inc(tbl_in, 16)
                load_gf(0)
                load_p(0)

                def load_x1(first):
                    sp.dma_start(x1s[:, bass.ds(first, XT), :],
                                 x1_dram[bass.ds(first, XT)].rearrange("n p d -> p n d")).then_inc(x1_in, 16)

                def transpose_rows(b):
                    sp.dma_start_transpose(xT[:, b].rearrange("p j h k c -> p (j h k) c"), rows[:, b]).then_inc(x_in[b], 16)

                def step(m, b, before, more_gf, more_p):
                    e = 2 * m + b
                    if more_gf:
                        sp.wait_ge(wgl, 2 * (e + 2))
                        load_gf(e + 2)
                    elif more_p:
                        sp.wait_ge(u_pe, 4 * e)
                    if more_p:
                        sp.wait_ge(g_in[1 - b], 16 * J * (m + 1))
                    if more_p and isinstance(m, int):
                        transpose_rows(1 - b)
                    load_x1(XT * e)
                    if more_p and not isinstance(m, int):
                        transpose_rows(1 - b)
                    if before:
                        for j in range(J):
                            store(e - 1, j)
                    if more_p:
                        sp.wait_ge(wpl, e + 1)
                        load_p(e + 1)

                for j in range(J):
                    sp.wait_ge(g0_in[j], 16)
                    sp.dma_start_transpose(xT[:, 0, j].rearrange("p h k c -> p (h k) c"),
                                           rows[:, 0, 2 * D * j:2 * D * (j + 1)]).then_inc(x0_in, 16)
                sp.wait_ge(wgl, 2)
                load_gf(1)
                step(0, 0, False, True, True)
                step(0, 1, True, True, True)
                with sp.Fori(1, E // 2 - 1) as m:
                    for b in range(2):
                        step(m, b, True, True, True)
                step(E // 2 - 1, 0, True, False, True)
                step(E // 2 - 1, 1, True, False, False)
                for j in range(J):
                    store(E - 1, j)
                with sp.Fori(0, NT // PER) as n:
                    sp.wait_ge(c_use, n + 1)
                    sp.dma_start(out_t[bass.ds(PER * n, PER)].rearrange("n p d -> p n d"),
                                 x1s[:, bass.ds(PER * n, PER), :]).then_inc(y_out, 16)
                sp.wait_ge(y_out, 16 * (NT // PER))

            @block.gpsimd
            def _(pool):
                pool.iota(rr[:], [[0, E], [P, J]], base=0, channel_multiplier=1,
                          allow_small_or_imprecise_dtypes=True).then_inc(e_const, 1)

                def gather(e):
                    if e == 1:
                        pool.wait_ge(x0_in, 16 * J)
                    wait_for(pool, x_in[e % 2], 16 * ((e - 1) // 2))
                    for j in range(J):
                        pool.indirect_dma_start(rows[:, e % 2, 2 * D * j:2 * D * (j + 1)], None, rows_dram,
                                                bass.IndirectOffsetOnAxis(ap=gidx[:, e, j:j + 1], axis=0),
                                                bounds_check=T - 1, oob_is_err=False).then_inc(g0_in[j] if e == 0 else g_in[e % 2], 16)

                def collect(n):
                    wait_for(pool, c_use, n - SETS + 1)
                    for j in range(PER):
                        for k in range(2):
                            pool.indirect_dma_start(got[:, n % SETS, 2 * j + k, :], None, eo_dram,
                                                    bass.IndirectOffsetOnAxis(ap=cidx[:, PER * n + j, k:k + 1], axis=0),
                                                    bounds_check=E * CAP - 1, oob_is_err=False).then_inc(c_in[n % SETS], 16)

                pool.wait_ge(grow_rdy, 1)
                for e in range(E):
                    gather(e)
                pool.wait_ge(crow_rdy, 1)
                for j in range(J):
                    pool.wait_ge(o_out[j], 16 * E)
                for n in range(NT // PER):
                    collect(n)

            @block.scalar
            def _(act):
                def gf_high(e, b):
                    wait_for(act, u_pe, 4 * (e - 1))
                    act.wait_ge(wg_in, 16 * (e + 1))
                    act.activation(wg[:, b, :, 0, :], raw_g[:], ACT.Copy, scale=W_S).then_inc(wgh, 1)
                    act.wait_ge(wf_in, 16 * (e + 1))
                    act.activation(wf[:, b, :, 0, :], raw_f[:], ACT.Copy, scale=W_S).then_inc(wgh, 1)

                def p_high(e, b):
                    wait_for(act, o_pe, J * (e - 1))
                    act.wait_ge(wp_in, 16 * (e + 1))
                    act.activation(wp[:, b, :, 0, :], raw_p[:], ACT.Copy, scale=W_S).then_inc(wph, 1)

                def gate_tanh(e, h):
                    act.wait_ge(u_pe, 4 * e + 2 * h + 1)
                    wait_for(act, h_rdy, 2 * e)
                    act.activation(th[:, h, :], pg[2 * h][:], ACT.Tanh, scale=0.5 / (XN_S * W_S)).then_inc(th_rdy, 1)

                def out_rows(e, j):
                    act.wait_ge(o_pe, J * e + j + 1)
                    wait_for(act, o_out[j], 16 * e)
                    act.activation(o_sb[:, j, :], po[j][:], ACT.Copy, scale=1.0 / (H_S * W_S)).then_inc(o_ev, 1)

                act.wait_ge(d_rdy, 1)
                act.activation(tmp2[:, :, 1], tmp2[:, :, 0], ACT.Exp).then_inc(pe2, 1)
                gf_high(0, 0)

                def step(e, b, down, more):
                    if more:
                        gf_high(e + 1, 1 - b)
                    gate_tanh(e, 0)
                    gate_tanh(e, 1)
                    p_high(e, b)
                    if down:
                        for j in range(J):
                            out_rows(e - 1, j)

                step(0, 0, False, True)
                step(1, 1, True, True)
                with act.Fori(1, E // 2 - 1) as m:
                    for b in range(2):
                        step(2 * m + b, b, True, True)
                step(E - 2, 0, True, True)
                step(E - 1, 1, True, False)
                for j in range(J):
                    out_rows(E - 1, j)
                act.wait_ge(o_ev, J * E)

            @block.vector
            def _(dve):
                def gf_low(e, b):
                    for raw, w, n in ((raw_g, wg, 1), (raw_f, wf, 2)):
                        dve.wait_ge(wgh, 2 * e + n)
                        dve.scalar_tensor_tensor(out=w[:, b, :, 1, :], in0=raw[:], scalar=W_S, in1=w[:, b, :, 0, :],
                                                 op0=ALU.mult, op1=ALU.subtract).then_inc(wgl, 1)

                def p_low(e, b):
                    dve.wait_ge(wph, e + 1)
                    dve.scalar_tensor_tensor(out=wp[:, b, :, 1, :], in0=raw_p[:], scalar=W_S, in1=wp[:, b, :, 0, :],
                                             op0=ALU.mult, op1=ALU.subtract).then_inc(wpl, 1)

                def hidden(e, h, b):
                    dve.wait_ge(th_rdy, 2 * e + h + 1)
                    dve.scalar_tensor_tensor(out=hf[:, h, :], in0=th[:, h, :], scalar=1.0, in1=pg[2 * h][:],
                                             op0=ALU.add, op1=ALU.mult)
                    dve.drain()
                    dve.wait_ge(u_pe, 4 * e + 2 * h + 2)
                    dve.scalar_tensor_tensor(out=hf[:, h, :], in0=pg[2 * h + 1][:], scalar=0.5 * H_S / (XN_S * W_S) ** 2,
                                             in1=hf[:, h, :], op0=ALU.mult, op1=ALU.mult)
                    dve.drain()
                    wait_for(dve, o_pe, J * (e - 1))
                    dve.tensor_copy(hT[:, b, h, 0, :], hf[:, h, :])
                    dve.drain()
                    dve.tensor_tensor(hT[:, b, h, 1, :], hf[:, h, :], hT[:, b, h, 0, :], ALU.subtract).then_inc(h_rdy, 1)

                dve.wait_ge(e_const, 1)
                dve.tensor_tensor(cmp[:], rr[:], tot1[:].unsqueeze(2).to_broadcast([P, E, J]), ALU.is_ge)
                dve.wait_ge(tbl_pe, 1)
                lower = pg[0][:, 0:E * J].rearrange("p (e j) -> p e j", j=J)
                dve.tensor_copy(up_t[:], pg[0][:, E * J:2 * E * J])
                dve.drain()
                dve.tensor_tensor(grow[:], up_t[:].rearrange("p (e j) -> p e j", j=J), lower, ALU.subtract)
                dve.drain()
                dve.tensor_tensor(cmp[:], cmp[:], grow[:], ALU.mult)
                dve.drain()
                dve.tensor_tensor(gidx[:], cmp[:], lower, ALU.add).then_inc(grow_rdy, 1)
                dve.tensor_tensor(tmp2[:, :, 0], M12[:, :, 1], M12[:, :, 0], ALU.subtract).then_inc(d_rdy, 1)
                gf_low(0, 0)
                dve.tensor_scalar(ee[:], R12[:], -float(CAP), float(E * CAP), ALU.mult, ALU.add)
                dve.tensor_scalar(t1m[:], tot1[:], float(CAP - 1), None, ALU.min)
                dve.drain()
                dve.tensor_tensor(sel2[:], OH2[:], t1m[:].unsqueeze(1).to_broadcast([P, NT, E]), ALU.mult)
                dve.drain()
                dve.reduce_sum(tsel[:], sel2[:], AX_X)
                dve.scalar_tensor_tensor(out=crow[:, :, 0], in0=PP[:, :, 0], scalar=float(CAP - 1), in1=ee[:, :, 0],
                                         op0=ALU.min, op1=ALU.add)
                dve.tensor_scalar(crow[:, :, 1], PP[:, :, 1], -1.0, float(CAP - 1), ALU.mult, ALU.add)
                dve.drain()
                dve.tensor_tensor(crow[:, :, 1], crow[:, :, 1], tsel[:], ALU.max)
                dve.reciprocal(pw[:, :, 0], SE[:])
                dve.wait_ge(pe2, 1)
                dve.drain()
                dve.tensor_tensor(crow[:, :, 1], crow[:, :, 1], ee[:, :, 1], ALU.add)
                dve.tensor_tensor(pw[:, :, 1], tmp2[:, :, 1], pw[:, :, 0], ALU.mult)
                dve.drain()
                dve.tensor_copy(cidx[:], crow[:]).then_inc(crow_rdy, 1)

                def step(e, b, more):
                    if more:
                        gf_low(e + 1, 1 - b)
                    hidden(e, 0, b)
                    hidden(e, 1, b)
                    p_low(e, b)

                for b in range(2):
                    step(b, b, True)
                with dve.Fori(1, E // 2 - 1) as m:
                    for b in range(2):
                        step(2 * m + b, b, True)
                step(E - 2, 0, True)
                step(E - 1, 1, False)
                dve.wait_ge(x1_in, 16 * E)

                with dve.Fori(0, NT // (PER * SETS)) as m:
                    for i in range(SETS):
                        n = SETS * m + i
                        dve.tensor_copy(cw[:, i, :], pw[:, bass.ds(PER * n, PER), :].rearrange("p n k -> p (n k)"))
                        dve.drain()
                        dve.wait_ge(c_in[i], 2 * PER * 16 * (m + 1))
                        for q in range(2):
                            for j in range(PER):
                                y = x1s[:, bass.ds(PER * n + j, 1), :].rearrange("p a d -> p (a d)")
                                last = dve.scalar_tensor_tensor(out=y, in0=got[:, i, 2 * j + q, :],
                                                                scalar=cw[:, i, 2 * j + q:2 * j + q + 1], in1=y,
                                                                op0=ALU.mult, op1=ALU.add)
                            if q == 0:
                                dve.drain()
                        last.then_inc(c_use, 1)

            @block.tensor
            def _(pe):
                def up(m, b, u):
                    e, h, w = 2 * m + b, u // 2, (wg, wf)[u % 2]
                    if u == 0:
                        if isinstance(m, int) and m == 0 and b == 0:
                            pe.wait_ge(x0_in, 16 * J)
                        wait_for(pe, x_in[b], 16 * (m + b))
                        pe.wait_ge(wgl, 2 * (e + 1))
                        wait_for(pe, h_rdy, 2 * e)
                    for k in range(KT):
                        last = three_passes(pe, pg[u][:].rearrange("p (j c) -> p j c", c=P),
                                            (w[:, b, k, 0, h * P:(h + 1) * P], w[:, b, k, 1, h * P:(h + 1) * P]),
                                            (xT[:, b, :, 0, k, :], xT[:, b, :, 1, k, :]), k == 0, k == KT - 1)
                    last.then_inc(u_pe, 1)

                def down(e, j, b):
                    if j == 0:
                        pe.wait_ge(h_rdy, 2 * (e + 1))
                        pe.wait_ge(wpl, e + 1)
                    wait_for(pe, o_ev, J * (e - 1) + j + 1)
                    for k in range(HT):
                        last = three_passes(pe, po[j][:],
                                            (hT[:, b, k, 0, j * P:(j + 1) * P], hT[:, b, k, 1, j * P:(j + 1) * P]),
                                            (wp[:, b, k, 0, :], wp[:, b, k, 1, :]), k == 0, k == HT - 1)
                    last.then_inc(o_pe, 1)

                def step(m, b, before):
                    for u in range(4):
                        up(m, b, u)
                    if before:
                        for j in range(J):
                            down(2 * m + b - 1, j, 1 - b)

                pe.wait_ge(tbl_in, 32)
                for h in range(2):
                    last = pe.transpose(pg[0][:, h * E * J:(h + 1) * E * J],
                                        tbl[:, h, :].rearrange("m (c w) -> m c w", w=TW)[:, :, 0], ident[0:E * J, 0:E * J])
                last.then_inc(tbl_pe, 1)
                pe.wait_ge(grow_rdy, 1)
                step(0, 0, False)
                step(0, 1, True)
                with pe.Fori(1, E // 2) as m:
                    for b in range(2):
                        step(m, b, True)
                for j in range(J):
                    down(E - 1, j, 1)


_INS = ["x", "ctx_1024", "L0_xattn_Wk", "L0_xattn_Wv", "L0_xattn_bv", "L0_xattn_Wq", "L0_xattn_bq", "L0_xattn_Wo",
        "L0_xattn_bo", "L0_ffn_w_router", "L0_ffn_w_fc", "L0_ffn_w_gate", "L0_ffn_w_proj"]


def kernel(**inputs):
    import numpy as _np
    import concourse.bacc as _bacc
    from concourse import mybir as _mybir
    from concourse.bass_utils import run_bass_kernel_spmd as _run

    nc = _bacc.Bacc("TRN2", target_bir_lowering=False, num_devices=1)
    arrays, args = {}, []
    for name in _INS:
        a = _np.ascontiguousarray(inputs[name])
        arrays[f"in_{name}_dram"] = a
        args.append(nc.dram_tensor(f"in_{name}_dram", a.shape, _mybir.dt.from_np(a.dtype), kind="ExternalInput").ap())
    out = nc.dram_tensor("out_0_dram", inputs["x"].shape, _mybir.dt.float32, kind="ExternalOutput").ap()
    build(nc, *args, out)
    r = _run(nc, [arrays], core_ids=[0])
    return r.results[0]["out_0_dram"]
```
